# Optimizing a Trainium2 kernel written in Bass

```python
import numpy as np
import jax
import jax.numpy as jnp

def _softmax(x, axis=-1):
    return jax.nn.softmax(x, axis=axis)

def _gelu(x):
    return jax.nn.gelu(x, approximate=True)

def _silu(x):
    return jax.nn.silu(x)

def _sigmoid(x):
    return jax.nn.sigmoid(x)

def _layernorm(x, axis=-1, eps=1e-05):
    m = jnp.mean(x, axis=axis, keepdims=True)
    v = jnp.var(x, axis=axis, keepdims=True)
    return (x - m) / jnp.sqrt(v + eps)

def _scatter_add(tgt, idx, src, axis=0):
    return tgt.at[idx].add(src)

def _segment_sum(src, seg, n):
    return jax.ops.segment_sum(src, seg, n)
kernel_name = 'mk_decoder_postln_d1_seqx_r4_5c2a32'

def setup_inputs(seed: int=0):
    np.random.seed(seed)
    _w = jnp.asarray

    def _rec_inputs():
        import jax
        import jax.numpy as jnp
        _rk = jax.random.key(seed)
        x = -0.0003929 + 0.9999 * jax.random.normal(jax.random.fold_in(_rk, 1), (16, 112, 256), jnp.float32)
        _lenS = 112 - jax.random.randint(jax.random.fold_in(_rk, 7), (16,), 0, max(1, 112 // 4) + 1, jnp.int32)
        _lenS2 = 375 - jax.random.randint(jax.random.fold_in(_rk, 8), (16,), 0, max(1, 375 // 4) + 1, jnp.int32)
        _ctx_2048P = jax.random.normal(jax.random.fold_in(_rk, 11), (16, 16, 512), jnp.float32)
        _ctx_2048c = jax.random.dirichlet(jax.random.fold_in(_rk, 511), 0.3 * jnp.ones((16,), jnp.float32), (16, 375))
        _ctx_2048t = jnp.einsum('bsk,bkd->bsd', _ctx_2048c, _ctx_2048P)
        _ctx_2048t = _ctx_2048t * jax.lax.rsqrt(jnp.mean(jnp.square(_ctx_2048t)) + 1e-12) * 0.953939
        ctx_2048 = 4.13588e-05 + 0.999923 * (_ctx_2048t + 0.3 * jax.random.normal(jax.random.fold_in(_rk, 611), (16, 375, 512), jnp.float32))
        _validS = jnp.arange(112)[None, :] < _lenS[:, None]
        _validS2 = jnp.arange(375)[None, :] < _lenS2[:, None]
        _causal = jnp.tril(jnp.ones((112, 112), dtype=bool))
        mask_BxS2_if0 = jnp.where(jnp.ones((16, 375), dtype=bool), 4, 0).astype(jnp.int32)
        return (x, ctx_2048, mask_BxS2_if0)
    x, ctx_2048, mask_BxS2_if0 = _rec_inputs()

    def _L0_attn_setup():
        import jax, jax.numpy as jnp
        import numpy as np
        from jax import lax
        H = 512
        N = 8
        B, L, D_MODEL = (4, 1024, 256)
        D_CONV = 4

        def _s4d_kernel(log_dt, log_A_real, A_imag, C_re, C_im, L):
            dt = jnp.exp(log_dt)
            A = -jnp.exp(log_A_real) + 1j * A_imag
            C = C_re + 1j * C_im
            dtA = dt[:, None] * A
            Ct = C * (jnp.exp(dtA) - 1.0) / A
            t = jnp.arange(L, dtype=jnp.float32)
            vand = jnp.exp(dtA[:, :, None] * t)
            return 2.0 * jnp.einsum('hn,hnl->hl', Ct, vand).real
        key = jax.random.key(seed)
        ks = jax.random.split(key, 10)
        hidden_states = jax.random.normal(ks[0], (B, L, D_MODEL), dtype=jnp.float32)
        W_in = jax.random.normal(ks[1], (2 * H, D_MODEL), dtype=jnp.float32) / np.sqrt(D_MODEL)
        conv_w = jax.random.normal(ks[2], (H, D_CONV), dtype=jnp.float32) / np.sqrt(D_CONV)
        conv_b = jax.random.normal(ks[3], (H,), dtype=jnp.float32) * 0.1
        u = jax.random.uniform(ks[4], (H,), dtype=jnp.float32)
        log_dt = jnp.log(0.001) + u * (jnp.log(0.1) - jnp.log(0.001))
        log_A_real = jnp.log(0.5 * jnp.ones((H, N), dtype=jnp.float32))
        A_imag = jnp.pi * jnp.broadcast_to(jnp.arange(N, dtype=jnp.float32), (H, N)).copy()
        C_re = jax.random.normal(ks[5], (H, N), dtype=jnp.float32)
        C_im = jax.random.normal(ks[6], (H, N), dtype=jnp.float32)
        D = jnp.ones((H,), dtype=jnp.float32)
        W_out = jax.random.normal(ks[7], (D_MODEL, H), dtype=jnp.float32) / np.sqrt(H)
        return dict(hidden_states=hidden_states, W_in=W_in, conv_w=conv_w, conv_b=conv_b, log_dt=log_dt, log_A_real=log_A_real, A_imag=A_imag, C_re=C_re, C_im=C_im, D=D, W_out=W_out)
    _L0_attn_all = _L0_attn_setup()
    _L0_attn_in = {k: v for k, v in _L0_attn_all.items() if k in ('W_in', 'conv_w', 'conv_b', 'log_dt', 'log_A_real', 'A_imag', 'C_re', 'C_im', 'D', 'W_out')}
    del _L0_attn_all

    def _L0_xattn_setup():
        import jax, jax.numpy as jnp
        import numpy as np
        B, L, P = (4, 1024, 256)
        D_MODEL = 256
        D_GLOBAL = 512
        HEADDIM = 32
        EPSILON = 0.001
        RMS_EPS = 1e-05

        def rmsnorm(x, g, eps=RMS_EPS):
            var = jnp.mean(jnp.square(x), axis=-1, keepdims=True)
            return x * jax.lax.rsqrt(var + eps) * g

        def _hnet_depool(h, h_patch_full, patch_lens):
            h_patch = h_patch_full[..., :D_MODEL]
            bsz, plen = (h_patch.shape[0], h_patch.shape[1])
            seqlen = h.shape[1]
            logp = jnp.full((bsz, plen), -EPSILON, dtype=jnp.float32)
            bidx = jnp.cumsum(patch_lens, axis=1) - 1
            boundary_mask = jnp.zeros((bsz, seqlen), dtype=jnp.int32)
            boundary_mask = boundary_mask.at[jnp.arange(bsz)[:, None], bidx].set(1)
            dt = (-jnp.log(-jnp.expm1(logp))).astype(h_patch.dtype)
            x = h_patch / dt[..., None]
            n_heads = D_MODEL // HEADDIM
            A = -jnp.ones((n_heads,), dtype=jnp.float32)
            bcoef = jnp.exp(logp).astype(h_patch.dtype)
            x4 = x.reshape(bsz, plen, n_heads, HEADDIM)
            a = jnp.exp(dt[:, :, None] * A[None, None, :])
            u = (dt * bcoef)[:, :, None, None] * x4
            a_b = jnp.broadcast_to(a[..., None], u.shape)

            def comb(lft, rgt):
                aL, uL = lft
                aR, uR = rgt
                return (aL * aR, uL * aR + uR)
            _, s = jax.lax.associative_scan(comb, (a_b, u), axis=1)
            depool = s.reshape(bsz, plen, D_MODEL)
            plug = jnp.clip(jnp.cumsum(boundary_mask, axis=1) - 1, 0, plen - 1)
            depool_out = depool[jnp.arange(bsz)[:, None], plug]
            return depool_out + h
        key = jax.random.key(seed)
        k1, k2, k3, k4 = jax.random.split(key, 4)
        embeds = jax.random.normal(k1, (B, L, D_MODEL), dtype=jnp.float32)
        patch_embeds = jax.random.normal(k2, (B, P, D_GLOBAL), dtype=jnp.float32)
        patch_lens = jnp.full((B, P), L // P, dtype=jnp.int64)
        W_in = jax.random.normal(k3, (D_MODEL, D_MODEL), dtype=jnp.float32) * 0.02
        b_in = jnp.zeros((D_MODEL,), dtype=jnp.float32)
        g_res = jnp.ones((D_MODEL,), dtype=jnp.float32)
        g_init = jnp.ones((D_GLOBAL,), dtype=jnp.float32)
        return {'embeds': embeds, 'patch_embeds': patch_embeds, 'patch_lens': patch_lens, 'W_in': W_in, 'b_in': b_in, 'g_res': g_res, 'g_init': g_init}
    _L0_xattn_all = _L0_xattn_setup()
    _L0_xattn_in = {k: v for k, v in _L0_xattn_all.items() if k in ('W_in', 'b_in', 'g_res', 'g_init')}
    del _L0_xattn_all

    def _L0_ffn_setup():
        import jax, jax.numpy as jnp
        import numpy as np
        D_MODEL, D_FF, N_EXP = (256, 1024, 8)
        key = jax.random.key(seed)
        ks = jax.random.split(key, 8)
        s = lambda fan_in: 1.0 / np.sqrt(fan_in)
        x = jax.random.normal(ks[0], (4, 512, D_MODEL), dtype=jnp.float32)
        Wr = jax.random.uniform(ks[1], (N_EXP, D_MODEL), jnp.float32, -s(D_MODEL), s(D_MODEL))
        br = jax.random.uniform(ks[2], (N_EXP,), jnp.float32, -s(D_MODEL), s(D_MODEL))
        W1 = jax.random.uniform(ks[3], (N_EXP, D_FF, D_MODEL), jnp.float32, -s(D_MODEL), s(D_MODEL))
        b1 = jax.random.uniform(ks[4], (N_EXP, D_FF), jnp.float32, -s(D_MODEL), s(D_MODEL))
        W2 = jax.random.uniform(ks[5], (N_EXP, D_MODEL, D_FF), jnp.float32, -s(D_FF), s(D_FF))
        b2 = jax.random.uniform(ks[6], (N_EXP, D_MODEL), jnp.float32, -s(D_FF), s(D_FF))
        return {'x': x, 'Wr': Wr, 'br': br, 'W1': W1, 'b1': b1, 'W2': W2, 'b2': b2}
    _L0_ffn_all = _L0_ffn_setup()
    _L0_ffn_in = {k: v for k, v in _L0_ffn_all.items() if k in ('Wr', 'br', 'W1', 'b1', 'W2', 'b2')}
    del _L0_ffn_all
    return {'x': x, 'ctx_2048': ctx_2048, 'mask_BxS2_if0': mask_BxS2_if0, 'L0_attn_W_in': _L0_attn_in['W_in'], 'L0_attn_conv_w': _L0_attn_in['conv_w'], 'L0_attn_conv_b': _L0_attn_in['conv_b'], 'L0_attn_log_dt': _L0_attn_in['log_dt'], 'L0_attn_log_A_real': _L0_attn_in['log_A_real'], 'L0_attn_A_imag': _L0_attn_in['A_imag'], 'L0_attn_C_re': _L0_attn_in['C_re'], 'L0_attn_C_im': _L0_attn_in['C_im'], 'L0_attn_D': _L0_attn_in['D'], 'L0_attn_W_out': _L0_attn_in['W_out'], 'L0_xattn_W_in': _L0_xattn_in['W_in'], 'L0_xattn_b_in': _L0_xattn_in['b_in'], 'L0_xattn_g_res': _L0_xattn_in['g_res'], 'L0_xattn_g_init': _L0_xattn_in['g_init'], 'L0_ffn_Wr': _L0_ffn_in['Wr'], 'L0_ffn_br': _L0_ffn_in['br'], 'L0_ffn_W1': _L0_ffn_in['W1'], 'L0_ffn_b1': _L0_ffn_in['b1'], 'L0_ffn_W2': _L0_ffn_in['W2'], 'L0_ffn_b2': _L0_ffn_in['b2']}

def reference(x, ctx_2048, mask_BxS2_if0, L0_attn_W_in, L0_attn_conv_w, L0_attn_conv_b, L0_attn_log_dt, L0_attn_log_A_real, L0_attn_A_imag, L0_attn_C_re, L0_attn_C_im, L0_attn_D, L0_attn_W_out, L0_xattn_W_in, L0_xattn_b_in, L0_xattn_g_res, L0_xattn_g_init, L0_ffn_Wr, L0_ffn_br, L0_ffn_W1, L0_ffn_b1, L0_ffn_W2, L0_ffn_b2):
    import jax
    import jax.numpy as jnp

    def _L0_attn_ref(hidden_states, W_in, conv_w, conv_b, log_dt, log_A_real, A_imag, C_re, C_im, D, W_out):
        import jax, jax.numpy as jnp
        import numpy as np
        from jax import lax
        H = 512
        N = 8
        B, L, D_MODEL = (4, 1024, 256)
        D_CONV = 4

        def _s4d_kernel(log_dt, log_A_real, A_imag, C_re, C_im, L):
            dt = jnp.exp(log_dt)
            A = -jnp.exp(log_A_real) + 1j * A_imag
            C = C_re + 1j * C_im
            dtA = dt[:, None] * A
            Ct = C * (jnp.exp(dtA) - 1.0) / A
            t = jnp.arange(L, dtype=jnp.float32)
            vand = jnp.exp(dtA[:, :, None] * t)
            return 2.0 * jnp.einsum('hn,hnl->hl', Ct, vand).real
        B, L, _ = hidden_states.shape
        xz = jnp.einsum('bld,ed->bel', hidden_states, W_in)
        x, z = jnp.split(xz, 2, axis=1)
        w = conv_w.shape[-1]
        xp = jnp.pad(x, ((0, 0), (0, 0), (w - 1, 0)))
        x = lax.conv_general_dilated(xp, conv_w[:, None, :], (1,), 'VALID', dimension_numbers=('NCH', 'OIH', 'NCH'), feature_group_count=x.shape[1])
        x = jax.nn.silu(x + conv_b[None, :, None])
        k = _s4d_kernel(log_dt, log_A_real, A_imag, C_re, C_im, L)
        n = 2 * L
        y = jnp.fft.irfft(jnp.fft.rfft(x, n=n) * jnp.fft.rfft(k, n=n), n=n)[..., :L]
        y = y + x * D[None, :, None]
        y = y * jax.nn.silu(z)
        return jnp.einsum('bhl,dh->bld', y, W_out)

    def _L0_xattn_ref(embeds, patch_embeds, patch_lens, W_in, b_in, g_res, g_init):
        import jax, jax.numpy as jnp
        import numpy as np
        B, L, P = (4, 1024, 256)
        D_MODEL = 256
        D_GLOBAL = 512
        HEADDIM = 32
        EPSILON = 0.001
        RMS_EPS = 1e-05

        def rmsnorm(x, g, eps=RMS_EPS):
            var = jnp.mean(jnp.square(x), axis=-1, keepdims=True)
            return x * jax.lax.rsqrt(var + eps) * g

        def _hnet_depool(h, h_patch_full, patch_lens):
            h_patch = h_patch_full[..., :D_MODEL]
            bsz, plen = (h_patch.shape[0], h_patch.shape[1])
            seqlen = h.shape[1]
            logp = jnp.full((bsz, plen), -EPSILON, dtype=jnp.float32)
            bidx = jnp.cumsum(patch_lens, axis=1) - 1
            boundary_mask = jnp.zeros((bsz, seqlen), dtype=jnp.int32)
            boundary_mask = boundary_mask.at[jnp.arange(bsz)[:, None], bidx].set(1)
            dt = (-jnp.log(-jnp.expm1(logp))).astype(h_patch.dtype)
            x = h_patch / dt[..., None]
            n_heads = D_MODEL // HEADDIM
            A = -jnp.ones((n_heads,), dtype=jnp.float32)
            bcoef = jnp.exp(logp).astype(h_patch.dtype)
            x4 = x.reshape(bsz, plen, n_heads, HEADDIM)
            a = jnp.exp(dt[:, :, None] * A[None, None, :])
            u = (dt * bcoef)[:, :, None, None] * x4
            a_b = jnp.broadcast_to(a[..., None], u.shape)

            def comb(lft, rgt):
                aL, uL = lft
                aR, uR = rgt
                return (aL * aR, uL * aR + uR)
            _, s = jax.lax.associative_scan(comb, (a_b, u), axis=1)
            depool = s.reshape(bsz, plen, D_MODEL)
            plug = jnp.clip(jnp.cumsum(boundary_mask, axis=1) - 1, 0, plen - 1)
            depool_out = depool[jnp.arange(bsz)[:, None], plug]
            return depool_out + h
        h = rmsnorm(embeds, g_res)
        h = jnp.einsum('bld,ed->ble', h, W_in) + b_in
        h_patch = rmsnorm(patch_embeds, g_init)
        return _hnet_depool(h, h_patch, patch_lens)

    def _L0_ffn_ref(x, Wr, br, W1, b1, W2, b2):
        import jax, jax.numpy as jnp
        import numpy as np
        D_MODEL, D_FF, N_EXP = (256, 1024, 8)
        B, S, D = x.shape
        xf = x.reshape(-1, D)
        logits = xf @ Wr.T + br
        expert_idx = jnp.argmax(logits, axis=-1)
        h = jax.nn.relu(jnp.einsum('td,efd->etf', xf, W1) + b1[:, None, :])
        y = jnp.einsum('etf,edf->etd', h, W2) + b2[:, None, :]
        out = y[expert_idx, jnp.arange(xf.shape[0])]
        return out.reshape(B, S, D)
    x = _layernorm(x + _L0_attn_ref(x, L0_attn_W_in, L0_attn_conv_w, L0_attn_conv_b, L0_attn_log_dt, L0_attn_log_A_real, L0_attn_A_imag, L0_attn_C_re, L0_attn_C_im, L0_attn_D, L0_attn_W_out), axis=-1)
    x = _layernorm(x + _L0_xattn_ref(x, ctx_2048, mask_BxS2_if0, L0_xattn_W_in, L0_xattn_b_in, L0_xattn_g_res, L0_xattn_g_init), axis=-1)
    x = _layernorm(x + _L0_ffn_ref(x, L0_ffn_Wr, L0_ffn_br, L0_ffn_W1, L0_ffn_b1, L0_ffn_W2, L0_ffn_b2), axis=-1)
    return x

_drawn_inputs = setup_inputs


def setup_inputs(seed=0):
    import zlib

    import numpy as np

    out = dict(_drawn_inputs(seed))
    spreads = {'L0_attn_log_A_real': (-0.6931471824645996, 0.2),
     'L0_attn_D': (1.0, 0.2),
     'L0_xattn_b_in': (0.0, 0.1),
     'L0_xattn_g_res': (1.0, 0.2),
     'L0_xattn_g_init': (1.0, 0.2)}
    factors = {'L0_ffn_b1': 4.024, 'L0_ffn_b2': 3.166}
    for name, (base, spread) in spreads.items():
        noise = np.random.default_rng([zlib.crc32(name.encode()), seed]).standard_normal(out[name].shape)
        drawn = base * np.exp(spread * noise) if base else spread * noise
        out[name] = jnp.asarray(drawn.astype(out[name].dtype))
    for name, factor in factors.items():
        out[name] = (out[name] * factor).astype(out[name].dtype)
    return out
```

```python
from contextlib import ExitStack
import math

import numpy as np
import concourse.bass as bass
from concourse import mybir

F32 = mybir.dt.float32
BF16 = mybir.dt.bfloat16
I32 = mybir.dt.int32
ALU = mybir.AluOpType
ACT = mybir.ActivationFunctionType
AX_X = mybir.AxisListType.X

NB, L, D = 16, 112, 256
H, MODES, TAPS = 512, 8, 4
C, PATCHES = 512, 375
NE, FF = 8, 1024
T = NB * L
P = 128
HT = H // P
DT = D // P
FT = FF // P
NC = 4
CB = NB // NC
CW = CB * L
NFFT = 2 * L
PT, PP = 3, 125
LO, LA = 16, L // 16
TILES = (T - NE) // P + NE
SLOTS = TILES * P
ROW = D + 4
TPE = -(-T // P)

EPS = 1e-5
LOGP = -0.001
DECAY = -math.log(-math.expm1(LOGP))
BCOEF = math.exp(LOGP)
MAGIC = 1.5 * 2.0 ** 23
TWO_PI_HI = 6.28125
TWO_PI_LO = 2 * math.pi - TWO_PI_HI
PI_BELOW = 3.1415925
PAST = 1.0e4


def constant_columns():
    t = np.arange(L)
    parts = {}

    def put(name, a):
        full = np.zeros((P, a.shape[1]), np.float32)
        full[:a.shape[0]] = a
        parts[name] = full

    put("ident", np.eye(P))
    angle = 2 * np.pi * np.outer(t, t) / NFFT
    cos, sin = np.cos(angle), np.sin(angle)
    nyquist = (-1.0) ** t
    zero0 = (t > 0).astype(float)
    put("f_re", cos)
    f_im = -sin
    f_im[:, 0] = nyquist
    put("f_im", f_im)
    put("f_im0", -sin * zero0)
    f_d = cos.copy()
    f_d[:, 0] = nyquist
    put("f_d", f_d)
    g_re = 2 * cos / NFFT
    g_re[0] = 1.0 / NFFT
    put("g_re", g_re)
    g_im = -2 * sin / NFFT
    g_im[0] = nyquist / NFFT
    put("g_im", g_im)
    put("earlier", (t[:, None] < t[None, :]).astype(float))
    put("iota_t", np.tile(t, (P, 1)))
    put("part", np.arange(P)[:, None])
    put("expert_m8", np.tile(np.arange(NE) - NE, (P, NB)))
    not_first = np.ones((NE, NB))
    not_first[:, 0] = 0
    put("seq_reset", np.tile(not_first.ravel(), (P, 1)))
    put("tile_from", np.tile(P * np.arange(TPE), (P, NE)))
    put("tile_no", np.tile(np.arange(TILES).repeat(NE), (P, 1)))
    lags = list(LO * np.arange(LA)) + list(range(LO)) + [0.5]
    put("lags", np.tile(np.array(lags), (P, 1)))
    put("m_half", np.full((P, 1), -0.5))
    put("zero", np.zeros((P, 1)))
    put("eps", np.full((P, 1), EPS))
    at, n = {}, 0
    for name, a in parts.items():
        at[name] = (n, n + a.shape[1])
        n += a.shape[1]
    return at, np.concatenate(list(parts.values()), axis=1)


def need(engine, semaphore, value):
    if not (isinstance(value, int) and value <= 0):
        engine.wait_ge(semaphore, value)


def decoder_layer(nc, ins, out):
    at, _ = constant_columns()
    n_const = max(b for _, b in at.values())
    NLAG = LA + LO + 1

    with ExitStack() as ctx:
        def sb(name, shape, dt=F32):
            return ctx.enter_context(nc.sbuf_tensor(name, shape, dt))

        def sem(name):
            return ctx.enter_context(nc.semaphore(name))

        slot_rows = nc.dram_tensor("slot_rows", (SLOTS, ROW), F32, kind="Internal").ap()
        ps = ctx.enter_context(nc.psum_tensor("ps", [P, 8, 512], F32))

        class Region:

            def __init__(self, tensor, words):
                self.tensor, self.words, self.used = tensor, words, 0

            def cut(self, words, rows=P):
                self.used += words
                assert self.used <= self.words, (self.used, self.words)
                return self.tensor[0:rows, self.used - words:self.used]

        consts = sb("consts", [P, n_const])

        def const(name, rows=P):
            a, b = at[name]
            return consts[0:rows, a:b]

        ident = const("ident")
        ones16 = sb("ones16", [P, P], BF16)
        tri16 = sb("tri16", [L, L], BF16)
        iota16 = sb("iota16", [P, L], BF16)
        w_x = sb("w_x", [P, DT, D])
        g_res = sb("g_res", [P, DT])
        w_r = sb("w_r", [P, DT, NE])
        b_r = sb("b_r", [L, NE])
        g_init = sb("g_init", [L, D])
        b1 = sb("b1", [P, NE * FT])
        logits = sb("logits", [L, NB * NE])
        x2_all = sb("x2_all", [L, NB, ROW])

        w1_flat = sb("w1", [P, NE * DT * FF])
        w1 = w1_flat[:, :].rearrange("p (e k f) -> p e k f", e=NE, k=DT)
        r = Region(w1_flat, NE * DT * FF)
        nm = HT * NLAG * MODES
        theta = r.cut(2 * nm)
        turns = r.cut(2 * nm)
        mag = r.cut(nm)
        n_prod = LA * LO * 2 * MODES
        k_prods = [w1_flat[:, 0:n_prod], w1_flat[:, n_prod:2 * n_prod], r.cut(n_prod)]
        assert 2 * n_prod <= 5 * nm
        k_tmp = r.cut(HT * LA * MODES).rearrange("p (h a m) -> p h a m", h=HT, a=LA)
        modes_a = r.cut(HT * LA * 2 * MODES).rearrange("p (h a m) -> p h a m", h=HT, a=LA)
        modes_c = r.cut(HT * LO * 2 * MODES).rearrange("p (h c m) -> p h c m", h=HT, c=LO)
        cplx = r.cut(HT * LA * MODES * 2).rearrange("p (s h a m) -> p s h a m", s=2, h=HT, a=LA)
        kern = r.cut(HT * L).rearrange("p (h l) -> p h l", h=HT)
        kern_t = r.cut(H, L)
        log_dt, dt, d_skip = r.cut(HT), r.cut(HT), r.cut(HT)
        ssm = r.cut(4 * HT * MODES).rearrange("p (s m) -> p s m", s=4)
        km = r.cut(24 * HT * MODES).rearrange("p (s m) -> p s m", s=24)
        conv_w = r.cut(HT * TAPS).rearrange("p (h w) -> p h w", h=HT)
        conv_b = r.cut(HT)
        conv_acc = r.cut(2 * CW).rearrange("p (r n) -> p r n", r=2)
        conv_x = r.cut(2 * CW).rearrange("p (r n) -> p r n", r=2)
        lens = r.cut(PATCHES, NB).bitcast(I32)
        ends = r.cut(4 * PATCHES, NB).rearrange("b (s n) -> b s n", s=4)
        ends_t = r.cut(PT * NB // 2, PP).bitcast(BF16)
        pad_row = r.cut(ROW)
        assert r.used >= 3 * DT * FF
        fall = w1_flat[0:L, r.used:r.used + T]
        hits = r.cut(PT * T // 2, PP).bitcast(BF16).rearrange("p (k n) -> p k n", k=PT)
        dt_count, recip_count, mag_count, modes_count = [], [], [], []

        w2_flat = sb("w2", [P, NE * FT * D])
        w2 = w2_flat[:, :].rearrange("p (e m d) -> p e m d", e=NE, m=FT)
        r = Region(w2_flat, NE * FT * D)
        x_time = r.cut(NB * H, L).rearrange("p (b h) -> p b h", b=NB)
        hid_t = r.cut(DT * T).rearrange("p (k t) -> p k t", k=DT)
        w_in = r.cut(DT * 2 * H).rearrange("p (k h) -> p k h", k=DT)
        w_out = r.cut(HT * D).rearrange("p (k d) -> p k d", k=HT)
        spec = r.cut(3 * H, L).rearrange("p (s h) -> p s h", s=3)

        shared = sb("shared", [P, 2048])
        plug = shared[0:L, 0:T]
        decay = shared[0:L + 1, 0:T]
        b2 = shared[:, :].rearrange("p (e d) -> p e d", e=NE)

        N_B = 10176
        stage_b = sb("stage_b", [P, N_B])
        r = Region(stage_b, N_B)

        def two(words, rows=P):
            return r.cut(2 * words, rows).rearrange("p (r n) -> p r n", r=2)

        prod = r.cut(4 * H, L).rearrange("p (s h) -> p s h", s=4)
        y_spec = r.cut(2 * H, L).rearrange("p (s h) -> p s h", s=2)
        z_act, gated = two(HT * L), two(HT * L)
        x_res, x1, x2_sum, x2, ctx_sb = two(D, L), two(D, L), two(D, L), two(D, L), two(C, L)
        x1_pre = r.cut(D, L)
        x1_t, x2_t = two(DT * L), two(DT * L)
        u = two(D, L + 1)
        decay_b = two(L, L + 1)
        ctx_sq = r.cut(C // 2, L).bitcast(BF16)
        small_b = r.cut(80, L)
        bn = [small_b[:, 0:6], small_b[:, 6:12]]
        mv = [[small_b[:, 12 + 4 * n + 2 * q:14 + 4 * n + 2 * q] for q in range(2)] for n in range(2)]
        nr = [[small_b[:, 20 + 8 * n + 4 * q:24 + 8 * n + 4 * q] for q in range(2)] for n in range(2)]
        cs = [small_b[:, 36 + 4 * q:40 + 4 * q] for q in range(2)]
        rr = [small_b[:, 44 + 4 * q:48 + 4 * q] for q in range(2)]
        r = Region(stage_b, N_B)
        h_sb = r.cut(FF)
        h_t = two(FF)
        rows_t = two(D)
        y_sum, y_row = two(D), two(D)
        rows = r.cut(4 * ROW).rearrange("p (r n) -> p r n", r=4)
        rt = r.cut(9 * NB * NE).rearrange("p (s n) -> p s n", s=9)
        one_hot = r.cut(NB * NE // 2, L).bitcast(BF16)
        tile_n = r.cut(NE * TPE)
        per_e = r.cut(4 * NE).rearrange("p (s e) -> p s e", s=4)
        tile_hits = r.cut(TILES * NE)
        tile_e = r.cut(2 * TILES).rearrange("p (s n) -> p s n", s=2)
        tile_expert = r.cut(TILES).bitcast(I32)
        slot_f = r.cut(NB, L)
        slot = r.cut(NB, L).bitcast(I32)
        f_bn, f_mv, f_nr = r.cut(6), two(2), two(2)
        f_index = two(1).bitcast(I32)

        loaded = {k: sem("loaded_" + k) for k in (
            "consts", "ssm", "w_in_x", "w_in_z", "conv", "w_out", "lens", "small", "b2", "w1", "w2", "pad")}
        hid_loaded = [sem(f"hid_loaded{c}") for c in range(NC)]
        iota_set = sem("iota_set")
        ones_set, tri_set = sem("ones_set"), sem("tri_set")
        b_step, ends_ps, ends_sb, hits_set, count_ps = (
            sem(s) for s in ("b_step", "ends_ps", "ends_sb", "hits_set", "count_ps"))
        run_set, plug_set, plug_scan, plug_ready, fall_step, decay_set, decay_kept = (
            sem(s) for s in ("run_set", "plug_set", "plug_scan", "plug_ready", "fall_step", "decay_set",
                             "decay_kept"))
        k_exp, k_pool, k_phase, k_recip, k_sin, k_prod_set, k_own, k_sum = (
            sem(s) for s in ("k_exp", "k_pool", "k_phase", "k_recip", "k_sin", "k_prod_set", "k_own", "k_sum"))
        kern_ps, kern_sb, spec_ps, spec_set = (sem(s) for s in ("kern_ps", "kern_sb", "spec_ps", "spec_set"))
        in_ps, acc_set, tap_set, conv_done, act_x, xt_ps, xt_set = (
            sem(s) for s in ("in_ps", "acc_set", "tap_set", "conv_done", "act_x", "xt_ps", "xt_set"))
        dft_ps, prod_set, y_set, z_ps, z_set, idft_ps, gate_set, out_ps = (
            sem(s) for s in ("dft_ps", "prod_set", "y_set", "z_ps", "z_set", "idft_ps", "gate_set", "out_ps"))
        x_loaded = [sem(f"x_loaded{q}") for q in range(2)]
        c_loaded = [sem(f"c_loaded{q}") for q in range(2)]
        pre_set, bn1_set, mv1_set, nr1_step, r1_set, x1_set = (
            sem(s) for s in ("pre_set", "bn1_set", "mv1_set", "nr1_step", "r1_set", "x1_set"))
        sq_set, cs_step, cs_set, u_set = (sem(s) for s in ("sq_set", "cs_step", "cs_set", "u_set"))
        x1t_ps, x1t_set, cross_ps, sum1_set, sum2_set = (
            sem(s) for s in ("x1t_ps", "x1t_set", "cross_ps", "sum1_set", "sum2_set"))
        bn2_set, mv2_set, nr2_step, r2_set, x2_set, x2_kept = (
            sem(s) for s in ("bn2_set", "mv2_set", "nr2_step", "r2_set", "x2_set", "x2_kept"))
        x2t_ps, x2t_set, logit_ps, logit_set = (
            sem(s) for s in ("x2t_ps", "x2t_set", "logit_ps", "logit_set"))
        r_step, one_hot_set, rank_ps, slot_set, experts_set, number_set, scattered = (
            sem(s) for s in ("r_step", "one_hot_set", "rank_ps", "slot_set", "experts_set", "number_set",
                             "scattered"))
        rows_loaded = [sem(f"rows_loaded{q}") for q in range(4)]
        rows_out = [sem(f"rows_out{q}") for q in range(4)]
        rt_ps, rt_set, h_ps, h_set, ht_ps, ht_set, f_ps = (
            sem(s) for s in ("rt_ps", "rt_set", "h_ps", "h_set", "ht_ps", "ht_set", "f_ps"))
        fb_set, fs_set, fbn_set, fmv_set, fn_step, fr_set, y_done = (
            sem(s) for s in ("fb_set", "fs_set", "fbn_set", "fmv_set", "fn_step", "fr_set", "y_done"))
        index_set = sem("index_set")

        PRO, EPI = 6, 4
        F_PRO, F_UNROLL = 4, 4

        def b_steps(engine, step):
            for s in range(PRO):
                step(s // 2, s % 2)
            with engine.Fori(PRO // 2, NB // 2) as pair:
                for q in range(2):
                    step(pair, q)
            for s in range(NB, NB + EPI):
                step(s // 2, s % 2)

        def seq(pair, q, lag):
            par, half = (q - lag) % 2, pair + (q - lag) // 2
            b = 2 * half + par
            if isinstance(b, int) and not 0 <= b < NB:
                return None, par, half
            return b, par, half

        def f_steps(engine, step, last):
            groups = (TILES - 1 - F_PRO) // F_UNROLL
            for s in range(F_PRO):
                step(s // F_UNROLL, s % F_UNROLL)
            with engine.Fori(1, 1 + groups) as group:
                for q in range(F_UNROLL):
                    step(group, q)
            for s in range(F_UNROLL * (1 + groups), last + 1):
                step(s // F_UNROLL, s % F_UNROLL)

        def tile_of(group, q, lag):
            place, g = (q - lag) % F_UNROLL, group + (q - lag) // F_UNROLL
            i = F_UNROLL * g + place
            if isinstance(i, int) and not 0 <= i < TILES:
                return None, place, g
            return i, place, g

        def apart(engine, *waits):
            waits = [(s, v if isinstance(v, int) else engine.snap(v)) for s, v in waits]
            if not all(isinstance(v, int) for _, v in waits):
                engine.wait_ge(loaded["consts"], 16)
            for s, v in waits:
                need(engine, s, v)

        K_PHASE = 7
        POOL_K = 2

        def k_products(engine, h, dst):
            for a in range(LA):
                last = engine.tensor_tensor(
                    dst[:, a * LO * 2 * MODES:(a + 1) * LO * 2 * MODES].rearrange("p (c m) -> p c m", c=LO),
                    modes_c[:, h], modes_a[:, h, a].unsqueeze(1).to_broadcast([P, LO, 2 * MODES]), ALU.mult)
            return last

        block = ctx.enter_context(nc.Block())

        @block.sync
        def _(sp):
            sp.dma_start(lens, ins["lens"]).then_inc(loaded["lens"], 16)
            sp.dma_start(consts[:, :], ins["consts"]).then_inc(loaded["consts"], 16)
            for dst, name in ((log_dt, "log_dt"), (d_skip, "d_skip"), (ssm, "ssm")):
                sp.dma_start(dst, ins[name]).then_inc(loaded["ssm"], 16)
            sp.dma_start(w_in[:, :, 0:H], ins["w_in"][:, :, 0:H]).then_inc(loaded["w_in_x"], 16)
            sp.dma_start(conv_w, ins["conv_w"]).then_inc(loaded["conv"], 16)
            sp.dma_start(conv_b, ins["conv_b"]).then_inc(loaded["conv"], 16)
            for c in range(NC):
                sp.dma_start(hid_t[:, :, c * CW:(c + 1) * CW], ins["x_t"][:, :, c * CW:(c + 1) * CW])\
                  .then_inc(hid_loaded[c], 16)
            sp.dma_start(w_in[:, :, H:2 * H], ins["w_in"][:, :, H:2 * H]).then_inc(loaded["w_in_z"], 16)
            sp.dma_start(w_out, ins["w_out"]).then_inc(loaded["w_out"], 16)
            for dst, name in ((w_x[:, :, :], "w_x"), (g_res[:, :], "g_res"), (w_r[:, :, :], "w_r"),
                              (b1[:, :], "b1"),
                              (u[L:L + 1, 0, :], "b_x"), (u[L:L + 1, 1, :], "b_x"),
                              (decay[L:L + 1, :], "one_row")):
                sp.dma_start(dst, ins[name]).then_inc(loaded["small"], 16)
            sp.dma_start(b_r[:, :], ins["b_r"].to_broadcast([L, NE])).then_inc(loaded["small"], 16)
            sp.dma_start(g_init[:, :], ins["g_init"].to_broadcast([L, D])).then_inc(loaded["small"], 16)
            sp.wait_ge(number_set, 2)
            sp.dma_start(slot_rows.rearrange("(i p) c -> p i c", p=P),
                         pad_row.unsqueeze(1).to_broadcast([P, TILES, ROW])).then_inc(loaded["pad"], 16)

            def step(pair, q):
                b, par, half = seq(pair, q, 0)
                if b is None:
                    return
                need(sp, u_set, b - 1)
                sp.dma_start(ctx_sb[:, par, :], ins["ctx"][b, :, :]).then_inc(c_loaded[par], 16)
                need(sp, pre_set, b - 1)
                sp.dma_start(x_res[:, par, :], ins["x"][b, :, :]).then_inc(x_loaded[par], 16)
                if isinstance(b, int) and b == 0:
                    sp.wait_ge(spec_set, 3)
                    sp.wait_ge(xt_ps, HT * NC)
                    sp.wait_ge(loaded["pad"], 16)
                if not isinstance(b, int):
                    sp.wait_ge(decay_set, 1)
                sp.dma_start(w1[:, half, par, :], ins["w1"][:, half, par, :]).then_inc(loaded["w1"], 16)

            b_steps(sp, step)
            sp.wait_ge(out_ps, NB)
            sp.wait_ge(gate_set, NB)
            for e in range(NE):
                sp.dma_start(w2[:, e, :, :], ins["w2"][:, e, :, :]).then_inc(loaded["w2"], 16)
            sp.wait_ge(cross_ps, NB)
            sp.dma_start(shared[:, :], ins["b2"].to_broadcast([P, NE * D])).then_inc(loaded["b2"], 16)

            sp.wait_ge(scattered, 16 * NB)

            def f_step(group, q):
                i, place, g = tile_of(group, q, 0)
                if i is None:
                    return
                need(sp, index_set, i - 3)
                sp.dma_start(rows[:, place, :], slot_rows[bass.ds(i * P, P), :]).then_inc(rows_loaded[place], 16)

            f_steps(sp, f_step, TILES - 1)
            for place in range(4):
                sp.wait_ge(rows_out[place], 16 * len(range(place, TILES, 4)))

        @block.gpsimd
        def _(pool):
            g = nc.gpsimd
            pool.wait_ge(loaded["consts"], 16)
            g.memset(ones16[:, :], 1.0).then_inc(ones_set, 1)
            g.tensor_copy(iota16[:, :], const("iota_t")).then_inc(iota_set, 1)
            g.tensor_copy(tri16[:, :], const("earlier", L)).then_inc(tri_set, 1)
            g.memset(pad_row, 0.0).then_inc(number_set, 1)
            pool.wait_ge(number_set, 1)
            g.iota(pad_row[:, D:D + 1].bitcast(I32), [[0, 1]], base=T, channel_multiplier=1).then_inc(number_set, 1)
            g.memset(x2_all[:, :, D:ROW], 0.0).then_inc(number_set, 1)
            pool.wait_ge(number_set, 3)
            g.iota(x2_all[:, :, D:D + 1].bitcast(I32), [[L, NB], [0, 1]], base=0, channel_multiplier=1)\
             .then_inc(number_set, 1)

            run = stage_b[0:L, 0:T]
            g.memset(run, 1.0).then_inc(run_set, 1)
            pool.wait_ge(run_set, 1)
            g.memset(run.rearrange("p (b t) -> p b t", b=NB)[:, :, 0:1], 0.0).then_inc(run_set, 1)

            done = 0

            def link(ins_):
                nonlocal done
                done += 1
                ins_.then_inc(k_pool, 1)
                pool.wait_ge(k_pool, done)

            def mul(o, a, b):
                link(g.tensor_tensor(o, a, b, ALU.mult))

            def add(o, a, b):
                link(g.tensor_tensor(o, a, b, ALU.add))

            def sub(o, a, b):
                link(g.tensor_tensor(o, a, b, ALU.subtract))

            def scale(o, a, m, c=0.0):
                link(g.tensor_scalar(o, a, m, c, ALU.mult, ALU.add))

            a_re, a_im, c_re, c_im = (ssm[:, n, :] for n in range(4))
            K = [km[:, n, :] for n in range(24)]
            a_abs, dta, dtb, th, em1, den, sq1, sq2, q_inv, sn, cs_, e_re, e_im, n_re, n_im, ct_re, ct_im, \
                tmp, tmp2 = K[0:19]
            pool.wait_ge(k_exp, 2)
            dt_b = dt.unsqueeze(2).to_broadcast([P, HT, MODES])
            as_hm = lambda v: v.rearrange("p (h m) -> p h m", h=HT)
            mul(as_hm(dta), as_hm(a_abs), dt_b)
            scale(dta, dta, -1.0)
            mul(as_hm(dtb), as_hm(a_im), dt_b)
            dt_count.append(done)
            th4 = theta.rearrange("p (s h l m) -> p s h l m", s=2, h=HT, l=NLAG)
            mg4 = mag.rearrange("p (h l m) -> p h l m", h=HT, l=NLAG)
            mul(mg4, const("lags").unsqueeze(1).unsqueeze(3).to_broadcast([P, HT, NLAG, MODES]),
                as_hm(dta).unsqueeze(2).to_broadcast([P, HT, NLAG, MODES]))
            mag_count.append(done)
            mul(sq1, a_abs, a_abs)
            mul(sq2, a_im, a_im)
            add(sq1, sq1, sq2)
            pool.wait_ge(k_exp, 3)
            scale(den, th, -1.0, 1.0)
            recip_count.append(done)
            pool.wait_ge(k_recip, 2)
            mul(em1, th, den)
            scale(em1, em1, 2.0)
            pool.wait_ge(k_exp, 4)
            pool.wait_ge(k_sin, 1)
            s_half = th4[:, 0, :, NLAG - 1, :]
            c_half = th4[:, 1, :, NLAG - 1, :]
            mul(as_hm(sn), s_half, c_half)
            scale(sn, sn, 2.0)
            mul(as_hm(tmp), s_half, s_half)
            scale(tmp, tmp, 2.0)
            scale(cs_, tmp, -1.0, 1.0)
            mul(e_re, em1, cs_)
            sub(e_re, e_re, tmp)
            scale(tmp, em1, 1.0, 1.0)
            mul(e_im, tmp, sn)
            mul(n_re, c_re, e_re)
            mul(tmp, c_im, e_im)
            sub(n_re, n_re, tmp)
            mul(n_im, c_re, e_im)
            mul(tmp, c_im, e_re)
            add(n_im, n_im, tmp)
            mul(tmp, n_im, a_im)
            mul(tmp2, n_re, a_abs)
            sub(tmp, tmp, tmp2)
            mul(ct_re, tmp, sq1)
            mul(tmp, n_re, a_im)
            mul(tmp2, n_im, a_abs)
            add(tmp, tmp, tmp2)
            mul(ct_im, tmp, sq1)
            scale(ct_re, ct_re, 2.0)
            scale(ct_im, ct_im, -2.0)
            for s, dst in ((1, 0), (0, MODES)):
                mul(modes_c[:, :, :, dst:dst + MODES], th4[:, s, :, LA:LA + LO, :], mg4[:, :, LA:LA + LO, :])
                mul(cplx[:, 1 - s], th4[:, s, :, 0:LA, :], mg4[:, :, 0:LA, :])
            cr = as_hm(ct_re).unsqueeze(2).to_broadcast([P, HT, LA, MODES])
            ci = as_hm(ct_im).unsqueeze(2).to_broadcast([P, HT, LA, MODES])
            a_r, a_i = modes_a[:, :, :, 0:MODES], modes_a[:, :, :, MODES:2 * MODES]
            mul(a_r, cplx[:, 0], cr)
            mul(k_tmp, cplx[:, 1], ci)
            sub(a_r, a_r, k_tmp)
            mul(a_i, cplx[:, 0], ci)
            mul(k_tmp, cplx[:, 1], cr)
            add(a_i, a_i, k_tmp)
            scale(a_i, a_i, -1.0)
            modes_count.append(done)
            for h in range(POOL_K):
                k_products(g, h, k_prods[h]).then_inc(k_prod_set, 1)

            m_half = const("m_half", L)

            def rsqrt(o, a, tmp_, chain, count):
                g.tensor_tensor(tmp_, a, const("eps", a.shape[0]), ALU.add).then_inc(chain, 1)
                pool.wait_ge(chain, count + 1)
                return g.tensor_tensor(o, tmp_, m_half[0:o.shape[0]], ALU.pow)

            def step(pair, q):
                b, par, half = seq(pair, q, 1)
                if b is not None:
                    pool.wait_ge(sq_set, b + 1)
                    need(pool, u_set, b - 1)
                    g.tensor_tensor(cs[par][:, 1:2], cs[par][:, 0:1], const("eps", L), ALU.add).then_inc(cs_step, 1)
                    pool.wait_ge(cs_step, b + 1)
                    g.tensor_tensor(rr[par][:, 0:1], cs[par][:, 1:2], m_half, ALU.pow).then_inc(cs_set, 1)
                b, par, half = seq(pair, q, 0)
                if b is not None:
                    pool.wait_ge(prod_set, b + 1)
                    need(pool, idft_ps, b)
                    g.tensor_tensor(y_spec[:, 0, :], prod[:, 0, :], prod[:, 1, :], ALU.subtract)
                    g.tensor_tensor(y_spec[:, 1, :], prod[:, 2, :], prod[:, 3, :], ALU.add).then_inc(y_set, 1)
                b, par, half = seq(pair, q, 2)
                if b is not None:
                    pool.wait_ge(mv1_set, b + 1)
                    need(pool, x1_set, b - 1)
                    need(pool, sum1_set, b - 1)
                    n_ = nr[0][par]
                    rsqrt(n_[:, 1:2], mv[0][par][:, 1:2], n_[:, 0:1], nr1_step, 5 * b).then_inc(nr1_step, 1)
                    pool.wait_ge(nr1_step, 5 * b + 2)
                    g.tensor_tensor(n_[:, 2:3], mv[0][par][:, 1:2], n_[:, 1:2], ALU.mult).then_inc(nr1_step, 1)
                    pool.wait_ge(nr1_step, 5 * b + 3)
                    g.tensor_tensor(n_[:, 2:3], n_[:, 2:3], n_[:, 1:2], ALU.mult).then_inc(nr1_step, 1)
                    pool.wait_ge(nr1_step, 5 * b + 4)
                    rsqrt(n_[:, 3:4], n_[:, 2:3], n_[:, 0:1], nr1_step, 5 * b + 4).then_inc(r1_set, 1)
                b, par, half = seq(pair, q, 3)
                if b is not None:
                    pool.wait_ge(mv2_set, b + 1)
                    need(pool, x2_set, b - 1)
                    rsqrt(nr[1][par][:, 1:2], mv[1][par][:, 1:2], nr[1][par][:, 0:1], nr2_step, b)\
                        .then_inc(r2_set, 1)

            b_steps(pool, step)

            pool.wait_ge(slot_set, 1)
            pool.wait_ge(number_set, 4)
            pool.wait_ge(loaded["pad"], 16)
            for b in range(NB):
                g.indirect_dma_start(slot_rows, bass.IndirectOffsetOnAxis(ap=slot[:, b:b + 1], axis=0),
                                     x2_all[:, b, :], None).then_inc(scattered, 16)

            m_half_f = const("m_half")
            last_token = pool.to_reg(T - 1)

            def f_step(group, q):
                i, place, gr = tile_of(group, q, 1)
                par = place % 2
                if i is not None:
                    pool.wait_ge(fmv_set, i + 1)
                    need(pool, y_done, i - 1)
                    g.tensor_tensor(f_nr[:, par, 0:1], f_mv[:, par, 1:2], const("eps"), ALU.add).then_inc(fn_step, 1)
                    pool.wait_ge(fn_step, i + 1)
                    g.tensor_tensor(f_nr[:, par, 1:2], f_nr[:, par, 0:1], m_half_f, ALU.pow).then_inc(fr_set, 1)
                    pool.wait_ge(y_done, i + 1)
                    g.tensor_tensor(f_index[:, par, :], rows[:, place, D:D + 1].bitcast(I32),
                                    const("zero").bitcast(I32), ALU.add).then_inc(index_set, 1)
                    apart(pool, (index_set, i + 1))
                    g.indirect_dma_start(out, bass.IndirectOffsetOnAxis(
                        ap=f_index[:, par, :], axis=0), y_row[:, par, :], None,
                        bounds_check=last_token, oob_is_err=False).then_inc(rows_out[place], 16)

            f_steps(pool, f_step, TILES)

        @block.scalar
        def _(act):
            a = nc.scalar
            act.wait_ge(loaded["ssm"], 48)
            a.activation(dt, log_dt, ACT.Exp).then_inc(k_exp, 1)
            a.activation(km[:, 0, :], ssm[:, 0, :], ACT.Exp).then_inc(k_exp, 1)
            act.wait_ge(k_pool, 2)
            a.activation(km[:, 3, :], km[:, 1, :], ACT.Tanh, scale=0.5).then_inc(k_exp, 1)

            def a_step(c, h):
                unit = HT * c + h
                par = h % 2
                act.wait_ge(in_ps, unit + 1)
                need(act, act_x, unit - 1)
                a.activation(conv_acc[:, par, :], ps[:, h, 0:CW], ACT.Copy, scale=conv_w[:, h, TAPS - 1:TAPS])\
                 .then_inc(acc_set, 1)

            def a_silu(unit, h):
                par = h % 2
                act.wait_ge(conv_done, unit + 1)
                need(act, xt_ps, unit - 1)
                a.activation(conv_x[:, par, :], conv_acc[:, par, :], ACT.Silu, bias=conv_b[:, h:h + 1])\
                 .then_inc(act_x, 1)

            def a_move(c, h):
                unit = HT * c + h
                act.wait_ge(xt_ps, unit + 1)
                a.activation(x_time[:, bass.ds(CB * c, CB), h * P:(h + 1) * P],
                             ps[0:L, 4 + h % 2, :].rearrange("p (b h) -> p b h", b=CB), ACT.Copy)\
                 .then_inc(xt_set, 1)

            def a_unit(c, h):
                a_step(c, h)
                before = (c, h - 1) if h else (c - 1, HT - 1)
                if not (isinstance(c, int) and before[0] < 0):
                    a_silu(HT * c + h - 1, (h - 1) % HT)
                before2 = (c, h - 2) if h >= 2 else (c - 1, h + HT - 2)
                if not (isinstance(c, int) and before2[0] < 0):
                    a_move(*before2)

            act.wait_ge(loaded["conv"], 32)
            for h in range(HT):
                a_unit(0, h)
            act.wait_ge(k_pool, mag_count[0])
            a.activation(mag, mag, ACT.Exp).then_inc(k_exp, 1)
            act.wait_ge(k_phase, K_PHASE)
            a.activation(theta, theta, ACT.Sin).then_inc(k_sin, 1)
            with act.Fori(1, NC) as c:
                for h in range(HT):
                    a_unit(c, h)
            a_silu(HT * NC - 1, HT - 1)
            a_move(NC - 1, HT - 2)
            a_move(NC - 1, HT - 1)
            act.wait_ge(kern_ps, 1)
            a.activation(kern_t, ps[0:L, 4, :], ACT.Copy).then_inc(kern_sb, 1)
            for s in range(3):
                act.wait_ge(spec_ps, s + 1)
                a.activation(spec[:, s, :], ps[0:L, 5 + s, :], ACT.Copy).then_inc(spec_set, 1)

            def step(pair, q):
                b, par, half = seq(pair, q, 1)
                if b is not None:
                    act.wait_ge(c_loaded[par], 16 * (half + 1))
                    need(act, cs_set, b - 1)
                    need(act, sq_set, b)
                    a.activation(ctx_sq, ctx_sb[:, par, :], ACT.Square, scale=C ** -0.5, accum_out=cs[par][:, 0:1])\
                     .then_inc(sq_set, 1)
                b, par, half = seq(pair, q, 2)
                if b is not None:
                    act.wait_ge(decay_set, 1)
                    need(act, cross_ps, b - 1)
                    a.activation(decay_b[:, par, :], decay[:, bass.ds(b * L, L)], ACT.Copy).then_inc(decay_kept, 1)
                b, par, half = seq(pair, q, 4)
                if b is not None:
                    act.wait_ge(x2_set, b + 1)
                    a.activation(x2_all[:, b, 0:D], x2[:, par, :], ACT.Copy).then_inc(x2_kept, 1)
                b, par, half = seq(pair, q, 0)
                if b is not None:
                    act.wait_ge(z_ps, b + 1)
                    need(act, gate_set, b - 1)
                    a.activation(z_act[:, par, :], ps[:, 2, 0:HT * L], ACT.Silu).then_inc(z_set, 1)
                b, par, half = seq(pair, q, 3)
                if b is not None:
                    act.wait_ge(x1t_ps, b + 1)
                    need(act, cross_ps, b - 1)
                    a.activation(x1_t[:, par, :], ps[:, 5, 0:DT * L], ACT.Copy).then_inc(x1t_set, 1)
                b, par, half = seq(pair, q, 4)
                if b is not None:
                    act.wait_ge(x2t_ps, b + 1)
                    need(act, logit_ps, b - 1)
                    a.activation(x2_t[:, par, :], ps[:, 7, 0:DT * L], ACT.Copy).then_inc(x2t_set, 1)
                if isinstance(pair, int) and (pair, q) == (0, 0):
                    act.wait_ge(plug_ready, 2)
                    a.activation(fall, fall, ACT.Exp, scale=-DECAY).then_inc(fall_step, 1)

            b_steps(act, step)

            def f_step(group, q):
                i, place, gr = tile_of(group, q, -1)
                if i is not None:
                    move_rows(i, place)
                i, place, gr = tile_of(group, q, 0)
                par = place % 2
                if i is not None:
                    e = act.value_load(tile_expert[0:1, bass.ds(i, 1)], min_val=0, max_val=NE - 1)
                    act.wait_ge(ht_ps, i + 1)
                    need(act, f_ps, i - 1)
                    for m in range(FT):
                        last = a.activation(h_t[:, par, m * P:(m + 1) * P],
                                            ps[:, 2 + m // 4, (m % 4) * P:(m % 4 + 1) * P], ACT.Relu,
                                            bias=b1[:, bass.ds(e * FT + m, 1)])
                    last.then_inc(ht_set, 1)

            def move_rows(i, place):
                par = place % 2
                act.wait_ge(rt_ps, i + 1)
                need(act, h_ps, i - 1)
                a.activation(rows_t[:, par, :], ps[:, 6, 0:D], ACT.Copy).then_inc(rt_set, 1)

            act.wait_ge(experts_set, 1)
            move_rows(0, 0)
            f_steps(act, f_step, TILES - 1)

        @block.vector
        def _(dve):
            v = nc.vector
            dve.wait_ge(loaded["lens"], 16)
            v.tensor_copy(ends[:, 0, :], lens).then_inc(b_step, 1)
            v.memset(ends[:, 1, :], 1.0).then_inc(b_step, 1)
            dve.wait_ge(b_step, 2)
            v.tensor_tensor_scan(ends[:, 2, :], ends[:, 1, :], ends[:, 0, :], 0.0, ALU.mult, ALU.add)\
             .then_inc(b_step, 1)
            dve.wait_ge(b_step, 3)
            v.tensor_scalar(ends[:, 2, :], ends[:, 2, :], 1.0, None, ALU.subtract).then_inc(b_step, 1)
            dve.wait_ge(b_step, 4)
            v.tensor_scalar(ends[:, 3, :], ends[:, 2, :], 0.0, float(L), ALU.is_lt, ALU.mult).then_inc(b_step, 1)
            dve.wait_ge(b_step, 5)
            v.tensor_tensor(ends[:, 2, :], ends[:, 2, :], ends[:, 3, :], ALU.add).then_inc(b_step, 1)
            dve.wait_ge(ends_ps, 1)
            v.tensor_copy(ends_t, ps[0:PP, 6, 0:PT * NB]).then_inc(ends_sb, 1)
            dve.wait_ge(loaded["consts"], 16)
            dve.wait_ge(k_pool, dt_count[0])
            done = 0

            def phase(ins_):
                nonlocal done
                done += 1
                ins_.then_inc(k_phase, 1)
                dve.wait_ge(k_phase, done)

            phase(v.tensor_tensor(
                theta[:, 0:nm].rearrange("p (h l m) -> p h l m", h=HT, l=NLAG),
                const("lags").unsqueeze(1).unsqueeze(3).to_broadcast([P, HT, NLAG, MODES]),
                km[:, 2, :].rearrange("p (h m) -> p h m", h=HT).unsqueeze(2).to_broadcast([P, HT, NLAG, MODES]),
                ALU.mult))
            phase(v.tensor_scalar(theta[:, nm:2 * nm], theta[:, 0:nm], math.pi / 2, None, ALU.add))
            phase(v.tensor_scalar(turns, theta, 1 / (2 * math.pi), MAGIC, ALU.mult, ALU.add))
            phase(v.tensor_scalar(turns, turns, MAGIC, None, ALU.subtract))
            phase(v.scalar_tensor_tensor(theta, turns, -TWO_PI_HI, theta, ALU.mult, ALU.add))
            phase(v.scalar_tensor_tensor(theta, turns, -TWO_PI_LO, theta, ALU.mult, ALU.add))
            v.tensor_scalar(theta, theta, PI_BELOW, -PI_BELOW, ALU.min, ALU.max).then_inc(k_phase, 1)
            assert done + 1 == K_PHASE
            dve.wait_ge(ends_sb, 1)
            dve.wait_ge(iota_set, 1)
            iota_b = iota16[0:PP, :].unsqueeze(1).to_broadcast([PP, NB, L])
            for k in range(PT):
                last = v.tensor_tensor(
                    hits[:, k, :].rearrange("p (b t) -> p b t", b=NB), iota_b,
                    ends_t[:, k * NB:(k + 1) * NB].unsqueeze(2).to_broadcast([PP, NB, L]), ALU.is_equal)
            last.then_inc(hits_set, 1)

            def a_step(c, h):
                unit = HT * c + h
                par = h % 2
                dve.wait_ge(acc_set, unit + 1)
                acc = conv_acc[:, par, :].rearrange("p (b t) -> p b t", b=CB)
                raw = ps[:, h, 0:CW].rearrange("p (b t) -> p b t", b=CB)
                for back in range(1, TAPS):
                    tap = TAPS - 1 - back
                    ins_ = v.scalar_tensor_tensor(acc[:, :, back:L], raw[:, :, 0:L - back],
                                                  conv_w[:, h, tap:tap + 1], acc[:, :, back:L],
                                                  ALU.mult, ALU.add)
                    if back < TAPS - 1:
                        ins_.then_inc(tap_set, 1)
                        dve.wait_ge(tap_set, (TAPS - 2) * unit + back)
                    else:
                        ins_.then_inc(conv_done, 1)

            dve.wait_ge(loaded["conv"], 32)
            dve.wait_ge(k_pool, recip_count[0])
            v.reciprocal(km[:, 5, :], km[:, 5, :]).then_inc(k_recip, 1)
            v.reciprocal(km[:, 6, :], km[:, 6, :]).then_inc(k_recip, 1)
            for h in range(HT):
                a_step(0, h)
            with dve.Fori(1, NC) as c:
                for h in range(HT):
                    a_step(c, h)
            for c in range(NC):
                dve.wait_ge(count_ps, c + 1)
                v.tensor_scalar(plug[:, c * CW:(c + 1) * CW], ps[0:L, 4 + c, 0:CW], 1.0, None, ALU.min)\
                 .then_inc(plug_set, 1)
            own = 0
            for n, h in enumerate((0, 2, 1, 3)):
                if h < POOL_K:
                    dve.wait_ge(k_prod_set, h + 1)
                    products = k_prods[h]
                else:
                    products = k_prods[2]
                    if own:
                        dve.wait_ge(k_sum, n - 1)
                    own += 1
                    dve.wait_ge(k_pool, modes_count[0])
                    k_products(v, h, products).then_inc(k_own, 1)
                    dve.wait_ge(k_own, own)
                v.tensor_reduce(kern[:, h, :], products.rearrange("p (l m) -> p l m", m=2 * MODES), AX_X, ALU.add)\
                 .then_inc(k_sum, 1)
            dve.wait_ge(k_sum, HT)
            v.tensor_tensor(kern[:, :, 0:1], kern[:, :, 0:1], d_skip.unsqueeze(2), ALU.add).then_inc(k_sum, 1)

            dve.wait_ge(plug_set, NC)
            dve.wait_ge(run_set, 2)
            v.tensor_tensor_scan(plug, stage_b[0:L, 0:T], plug, 0.0, ALU.mult, ALU.add).then_inc(plug_scan, 1)
            dve.wait_ge(plug_scan, 1)
            v.tensor_scalar(plug, plug, -1.0, 0.0, ALU.add, ALU.max).then_inc(plug_ready, 1)
            dve.wait_ge(plug_ready, 1)
            v.tensor_scalar(fall, plug, const("part", L), 0.0, ALU.subtract, ALU.max).then_inc(plug_ready, 1)

            dve.wait_ge(loaded["small"], 16 * 9)
            for k in range(DT):
                v.tensor_scalar(w_x[:, k, :], w_x[:, k, :], g_res[:, k:k + 1], None, ALU.mult).then_inc(b_step, 1)
            v.tensor_scalar(g_init[:, :], g_init[:, :], BCOEF, None, ALU.mult).then_inc(b_step, 1)

            def normalize(o, src, m, rs):
                return v.tensor_scalar(o, src, m, rs, ALU.subtract, ALU.mult)

            def step(pair, q):
                b, par, half = seq(pair, q, 3)
                if b is not None:
                    dve.wait_ge(r1_set, b + 1)
                    need(dve, x1t_ps, b - 1)
                    need(dve, sum1_set, b - 1)
                    normalize(x1[:, par, :], x1_pre, mv[0][par][:, 0:1], nr[0][par][:, 1:2]).then_inc(x1_set, 1)
                b, par, half = seq(pair, q, 0)
                if b is not None:
                    dve.wait_ge(dft_ps, b + 1)
                    dve.wait_ge(spec_set, 3)
                    need(dve, y_set, b)
                    for n, (x_part, k_part) in enumerate(((0, 0), (1, 1), (0, 1), (1, 2))):
                        last = v.tensor_tensor(prod[:, n, :], ps[0:L, x_part, :], spec[:, k_part, :], ALU.mult)
                    last.then_inc(prod_set, 1)
                b, par, half = seq(pair, q, 4)
                if b is not None:
                    dve.wait_ge(r2_set, b + 1)
                    need(dve, x2t_ps, b - 1)
                    need(dve, x2_kept, b - 1)
                    normalize(x2[:, par, :], x2_sum[:, par, :], mv[1][par][:, 0:1], nr[1][par][:, 1:2])\
                        .then_inc(x2_set, 1)
                b, par, half = seq(pair, q, 2)
                if b is not None:
                    dve.wait_ge(cs_set, b + 1)
                    dve.wait_ge(b_step, 6 + DT + 1)
                    need(dve, cross_ps, b - 1)
                    v.scalar_tensor_tensor(u[0:L, par, :], ctx_sb[:, par, 0:D], rr[par][:, 0:1], g_init[:, :],
                                           ALU.mult, ALU.mult).then_inc(u_set, 1)
                b, par, half = seq(pair, q, 1)
                if b is not None:
                    dve.wait_ge(idft_ps, b + 1)
                    dve.wait_ge(z_set, b + 1)
                    need(dve, out_ps, b - 1)
                    v.tensor_tensor(gated[:, par, :], ps[:, 3, 0:HT * L], z_act[:, par, :], ALU.mult)\
                     .then_inc(gate_set, 1)
                b, par, half = seq(pair, q, 2)
                if b is not None:
                    dve.wait_ge(out_ps, b + 1)
                    dve.wait_ge(x_loaded[par], 16 * (half + 1))
                    need(dve, x1_set, b)
                    v.tensor_tensor(x1_pre, ps[0:L, 4, 0:D], x_res[:, par, :], ALU.add).then_inc(pre_set, 1)
                    dve.wait_ge(pre_set, b + 1)
                    v.bn_stats(bn[0], x1_pre).then_inc(bn1_set, 1)
                    apart(dve, (bn1_set, b + 1), (r1_set, b - 1))
                    v.bn_aggr(mv[0][par], bn[0]).then_inc(mv1_set, 1)
                b, par, half = seq(pair, q, 3)
                if b is not None:
                    dve.wait_ge(cross_ps, b + 1)
                    dve.wait_ge(x1_set, b + 1)
                    need(dve, x2_set, b - 1)
                    s2 = x2_sum[:, par, :]
                    v.scalar_tensor_tensor(s2, ps[0:L, 6, 0:D], nr[0][par][:, 3:4], x1[:, par, :],
                                           ALU.mult, ALU.add).then_inc(sum1_set, 1)
                    dve.wait_ge(sum1_set, b + 1)
                    v.tensor_tensor(s2, s2, ps[0:L, 6, D:2 * D], ALU.add).then_inc(sum2_set, 1)
                    dve.wait_ge(sum2_set, b + 1)
                    v.bn_stats(bn[1], s2).then_inc(bn2_set, 1)
                    apart(dve, (bn2_set, b + 1), (r2_set, b - 1))
                    v.bn_aggr(mv[1][par], bn[1]).then_inc(mv2_set, 1)
                b, par, half = seq(pair, q, 4)
                if b is not None:
                    dve.wait_ge(logit_ps, b + 1)
                    v.tensor_tensor(logits[:, bass.ds(b * NE, NE)], ps[0:L, 7, 256:256 + NE], b_r[:, :],
                                    ALU.add).then_inc(logit_set, 1)
                if isinstance(pair, int) and (pair, q) == (0, 1):
                    dve.wait_ge(fall_step, 1)
                    v.scalar_tensor_tensor(plug, plug, const("part", L), fall, ALU.is_ge, ALU.mult)\
                     .then_inc(decay_set, 1)

            b_steps(dve, step)

            done = 0

            def link(ins_):
                nonlocal done
                done += 1
                ins_.then_inc(r_step, 1)
                dve.wait_ge(r_step, done)

            dve.wait_ge(logit_set, NB)
            dve.wait_ge(x2t_set, NB)
            dve.wait_ge(x2_kept, NB)
            be = lambda x, n=L: x[0:n].rearrange("p (b e) -> p b e", b=NB)
            lg = logits[:, :].rearrange("p (b e) -> p b e", b=NB)
            best, key, first = rt[0:L, 0, 0:NB], rt[0:L, 1, :], rt[0:L, 2, 0:NB]
            m8 = const("expert_m8", L)
            link(v.tensor_reduce(best, lg, AX_X, ALU.max))
            link(v.tensor_tensor(be(key), lg, best.unsqueeze(2).to_broadcast([L, NB, NE]), ALU.is_equal))
            link(v.tensor_tensor(key, key, m8, ALU.mult))
            link(v.tensor_reduce(first, be(key), AX_X, ALU.min))
            link(v.tensor_tensor(be(rt[0:L, 3, :]), be(m8), first.unsqueeze(2).to_broadcast([L, NB, NE]),
                                 ALU.is_equal))
            chosen = rt[0:L, 3, :]
            v.tensor_copy(one_hot, chosen).then_inc(one_hot_set, 1)
            dve.wait_ge(rank_ps, 1)
            tot, run_, excl = rt[:, 4, :], rt[:, 5, :], rt[:, 6, :]
            link(v.tensor_copy(tot.rearrange("p (e b) -> p b e", b=NB),
                               ps[:, 1, 0:NB * NE].rearrange("p (b e) -> p b e", b=NB)))
            link(v.tensor_tensor_scan(run_, const("seq_reset"), tot, 0.0, ALU.mult, ALU.add))
            link(v.tensor_tensor(excl, run_, tot, ALU.subtract))
            count = run_.rearrange("p (e b) -> p e b", b=NB)[:, :, NB - 1:NB]
            tn = tile_n.rearrange("p (e j) -> p e j", e=NE)
            link(v.tensor_tensor(tn, count.to_broadcast([P, NE, TPE]),
                                 const("tile_from").rearrange("p (e j) -> p e j", e=NE), ALU.is_gt))
            link(v.tensor_reduce(per_e[:, 0, :], tn, AX_X, ALU.add))
            link(v.memset(per_e[:, 1, :], 1.0))
            link(v.tensor_tensor_scan(per_e[:, 2, :], per_e[:, 1, :], per_e[:, 0, :], 0.0, ALU.mult, ALU.add))
            link(v.tensor_tensor(per_e[:, 3, :], per_e[:, 2, :], per_e[:, 0, :], ALU.subtract))
            link(v.scalar_tensor_tensor(
                rt[0:L, 7, :].rearrange("p (b e) -> p e b", b=NB),
                per_e[0:L, 3, :].unsqueeze(2).to_broadcast([L, NE, NB]), float(P),
                excl[0:L].rearrange("p (e b) -> p e b", b=NB), ALU.mult, ALU.add))
            link(v.tensor_tensor(rt[0:L, 7, :], rt[0:L, 7, :], ps[0:L, 0, 0:NB * NE], ALU.add))
            link(v.tensor_tensor(rt[0:L, 7, :], rt[0:L, 7, :], chosen, ALU.mult))
            link(v.tensor_reduce(slot_f, be(rt[:, 7, :]), AX_X, ALU.add))
            v.tensor_copy(slot, slot_f).then_inc(slot_set, 1)
            link(v.tensor_tensor(tile_hits.rearrange("p (i e) -> p i e", e=NE),
                                 const("tile_no").rearrange("p (i e) -> p i e", e=NE),
                                 per_e[:, 2, :].unsqueeze(1).to_broadcast([P, TILES, NE]), ALU.is_ge))
            link(v.tensor_reduce(tile_e[:, 0, :], tile_hits.rearrange("p (i e) -> p i e", e=NE), AX_X, ALU.add))
            link(v.tensor_scalar(tile_e[:, 1, :], tile_e[:, 0, :], float(NE - 1), None, ALU.min))
            v.tensor_copy(tile_expert, tile_e[:, 1, :]).then_inc(experts_set, 1)
            dve.wait_ge(experts_set, 1)
            dve.wait_ge(loaded["b2"], 16)

            def f_step(group, q):
                i, place, gr = tile_of(group, q, 2)
                par = place % 2
                if i is not None:
                    dve.wait_ge(fr_set, i + 1)
                    before, b_place, b_gr = tile_of(group, q, 4)
                    need(dve, rows_out[b_place], 16 * (b_gr + 1) if before is not None else 0)
                    normalize(y_row[:, par, :], y_sum[:, par, :], f_mv[:, par, 0:1], f_nr[:, par, 1:2])\
                        .then_inc(y_done, 1)
                i, place, gr = tile_of(group, q, 0)
                if i is not None:
                    dve.wait_ge(h_ps, i + 1)
                    need(dve, ht_ps, i)
                    v.tensor_copy(h_sb.rearrange("p (n f) -> p n f", n=2), ps[:, 0:2, :]).then_inc(h_set, 1)
                i, place, gr = tile_of(group, q, 1)
                par = place % 2
                if i is not None:
                    e = dve.value_load(tile_expert[0:1, bass.ds(i, 1)], min_val=0, max_val=NE - 1)
                    dve.wait_ge(f_ps, i + 1)
                    need(dve, y_done, i - 1)
                    v.tensor_tensor(y_sum[:, par, :], ps[:, 4 + par, 0:D], b2[:, e, :], ALU.add).then_inc(fb_set, 1)
                    dve.wait_ge(fb_set, i + 1)
                    dve.wait_ge(rows_loaded[place], 16 * (gr + 1))
                    v.tensor_tensor(y_sum[:, par, :], y_sum[:, par, :], rows[:, place, 0:D], ALU.add)\
                     .then_inc(fs_set, 1)
                    dve.wait_ge(fs_set, i + 1)
                    v.bn_stats(f_bn, y_sum[:, par, :]).then_inc(fbn_set, 1)
                    apart(dve, (fbn_set, i + 1), (fr_set, i - 1))
                    v.bn_aggr(f_mv[:, par, :], f_bn).then_inc(fmv_set, 1)

            f_steps(dve, f_step, TILES + 1)

        @block.tensor
        def _(pe):
            m = nc.tensor
            pe.wait_ge(loaded["consts"], 16)
            pe.wait_ge(b_step, 6)
            for k in range(PT):
                last = m.transpose(ps[0:PP, 6, k * NB:(k + 1) * NB], ends[:, 2, k * PP:(k + 1) * PP],
                                   ident[0:NB, 0:NB])
            last.then_inc(ends_ps, 1)

            def a_in(c, h):
                unit = HT * c + h
                need(pe, conv_done, unit - HT + 1)
                for k in range(DT):
                    last_ = m.matmul(ps[:, h, 0:CW], w_in[:, k, h * P:(h + 1) * P],
                                     hid_t[:, k, bass.ds(c * CW, CW)], start=(k == 0), stop=(k == DT - 1))
                last_.then_inc(in_ps, 1)

            def a_turn(unit, h):
                pe.wait_ge(act_x, unit + 1)
                need(pe, xt_set, unit - 1)
                for b in range(CB):
                    last_ = m.transpose(ps[0:L, 4 + h % 2, b * P:(b + 1) * P],
                                        conv_x[:, h % 2, b * L:(b + 1) * L], ident)
                last_.then_inc(xt_ps, 1)

            def a_unit(c, h):
                a_in(c, h)
                if not (isinstance(c, int) and c == 0 and h < 2):
                    a_turn(HT * c + h - 2, (h - 2) % HT)

            pe.wait_ge(loaded["w_in_x"], 16)
            pe.wait_ge(hid_loaded[0], 16)
            for h in range(HT):
                a_unit(0, h)
            for c in range(1, NC):
                pe.wait_ge(hid_loaded[c], 16)
            with pe.Fori(1, NC) as c:
                for h in range(HT):
                    a_unit(c, h)
            a_turn(HT * NC - 2, HT - 2)
            a_turn(HT * NC - 1, HT - 1)
            pe.wait_ge(xt_set, HT * NC)
            pe.wait_ge(hits_set, 1)
            pe.wait_ge(ones_set, 1)
            for c in range(NC):
                for k in range(PT):
                    last = m.matmul(ps[0:L, 4 + c, 0:CW], ones16[0:PP, 0:L], hits[:, k, c * CW:(c + 1) * CW],
                                    start=(k == 0), stop=(k == PT - 1))
                last.then_inc(count_ps, 1)
            pe.wait_ge(k_sum, HT + 1)
            pe.wait_ge(plug_set, NC)
            for h in range(HT):
                last = m.transpose(ps[0:L, 4, h * P:(h + 1) * P], kern[:, h, :], ident)
            last.then_inc(kern_ps, 1)
            pe.wait_ge(kern_sb, 1)
            for s, name in enumerate(("f_re", "f_im0", "f_d")):
                m.matmul(ps[0:L, 5 + s, :], const(name, L), kern_t, start=True, stop=True).then_inc(spec_ps, 1)
            pe.wait_ge(xt_set, HT * NC)
            pe.wait_ge(loaded["w_in_z"], 16)
            pe.wait_ge(loaded["w_out"], 16)
            pe.wait_ge(loaded["small"], 16 * 9)
            pe.wait_ge(spec_set, 3)

            def step(pair, q):
                b, par, half = seq(pair, q, 0)
                if b is not None:
                    need(pe, prod_set, b)
                    m.matmul(ps[0:L, 0, :], const("f_re", L), x_time[:, b, :], start=True, stop=True)
                    m.matmul(ps[0:L, 1, :], const("f_im", L), x_time[:, b, :], start=True, stop=True)\
                     .then_inc(dft_ps, 1)
                b, par, half = seq(pair, q, 0)
                if b is not None:
                    need(pe, z_set, b)
                    for h in range(HT):
                        for k in range(DT):
                            last_ = m.matmul(ps[:, 2, h * L:(h + 1) * L], w_in[:, k, H + h * P:H + (h + 1) * P],
                                             hid_t[:, k, bass.ds(b * L, L)], start=(k == 0), stop=(k == DT - 1))
                    last_.then_inc(z_ps, 1)
                b, par, half = seq(pair, q, 1)
                if b is not None:
                    pe.wait_ge(y_set, b + 1)
                    need(pe, gate_set, b)
                    for h in range(HT):
                        for s, name in enumerate(("g_re", "g_im")):
                            last_ = m.matmul(ps[:, 3, h * L:(h + 1) * L], y_spec[:, s, h * P:(h + 1) * P],
                                             const(name, L), start=(s == 0), stop=(s == 1))
                    last_.then_inc(idft_ps, 1)
                b, par, half = seq(pair, q, 3)
                if b is not None:
                    pe.wait_ge(x1_set, b + 1)
                    need(pe, x1t_set, b)
                    for k in range(DT):
                        last_ = m.transpose(ps[:, 5, k * L:(k + 1) * L], x1[:, par, k * P:(k + 1) * P],
                                            ident[0:L, 0:L])
                    last_.then_inc(x1t_ps, 1)
                b, par, half = seq(pair, q, 2)
                if b is not None:
                    pe.wait_ge(gate_set, b + 1)
                    need(pe, pre_set, b)
                    for h in range(HT):
                        last_ = m.matmul(ps[0:L, 4, 0:D], gated[:, par, h * L:(h + 1) * L], w_out[:, h, :],
                                         start=(h == 0), stop=(h == HT - 1))
                    last_.then_inc(out_ps, 1)
                b, par, half = seq(pair, q, 3)
                if b is not None:
                    pe.wait_ge(x1t_set, b + 1)
                    pe.wait_ge(b_step, 6 + DT + 1)
                    need(pe, sum2_set, b)
                    for k in range(DT):
                        m.matmul(ps[0:L, 6, 0:D], x1_t[:, par, k * L:(k + 1) * L], w_x[:, k, :],
                                 start=(k == 0), stop=(k == DT - 1))
                    pe.wait_ge(u_set, b + 1)
                    pe.wait_ge(decay_kept, b + 1)
                    m.matmul(ps[0:L, 6, D:2 * D], decay_b[:, par, :], u[:, par, :], start=True, stop=True)\
                     .then_inc(cross_ps, 1)
                b, par, half = seq(pair, q, 4)
                if b is not None:
                    pe.wait_ge(x2_set, b + 1)
                    need(pe, x2t_set, b)
                    need(pe, logit_set, b)
                    for k in range(DT):
                        last_ = m.transpose(ps[:, 7, k * L:(k + 1) * L], x2[:, par, k * P:(k + 1) * P],
                                            ident[0:L, 0:L])
                    last_.then_inc(x2t_ps, 1)
                b, par, half = seq(pair, q, 4)
                if b is not None:
                    pe.wait_ge(x2t_set, b + 1)
                    for k in range(DT):
                        last_ = m.matmul(ps[0:L, 7, 256:256 + NE], x2_t[:, par, k * L:(k + 1) * L], w_r[:, k, :],
                                         start=(k == 0), stop=(k == DT - 1))
                    last_.then_inc(logit_ps, 1)

            b_steps(pe, step)

            pe.wait_ge(one_hot_set, 1)
            pe.wait_ge(tri_set, 1)
            m.matmul(ps[0:L, 0, 0:NB * NE], tri16[:, :], one_hot, start=True, stop=True)
            m.matmul(ps[:, 1, 0:NB * NE], ones16[0:L, :], one_hot, start=True, stop=True).then_inc(rank_ps, 1)

            def turn_rows(i, place, gr):
                pe.wait_ge(rows_loaded[place], 16 * (gr + 1))
                need(pe, rt_set, i)
                for k in range(DT):
                    last_ = m.transpose(ps[:, 6, k * P:(k + 1) * P], rows[:, place, k * P:(k + 1) * P], ident)
                last_.then_inc(rt_ps, 1)

            def f_step(group, q):
                i, place, gr = tile_of(group, q, 0)
                if i is not None:
                    par = place % 2
                    e = pe.value_load(tile_expert[0:1, bass.ds(i, 1)], min_val=0, max_val=NE - 1)
                    pe.wait_ge(rt_set, i + 1)
                    need(pe, h_set, i)
                    for n in range(2):
                        for k in range(DT):
                            last_ = m.matmul(ps[:, n, :], rows_t[:, par, k * P:(k + 1) * P],
                                             w1[:, e, k, n * 512:(n + 1) * 512], start=(k == 0), stop=(k == DT - 1))
                    last_.then_inc(h_ps, 1)
                i, place, gr = tile_of(group, q, -1)
                if i is not None:
                    turn_rows(i, place, gr)
                i, place, gr = tile_of(group, q, 1)
                if i is not None:
                    par = place % 2
                    e = pe.value_load(tile_expert[0:1, bass.ds(i, 1)], min_val=0, max_val=NE - 1)
                    pe.wait_ge(ht_set, i + 1)
                    need(pe, fb_set, i - 1)
                    for f in range(FT):
                        last_ = m.matmul(ps[:, 4 + par, 0:D], h_t[:, par, f * P:(f + 1) * P], w2[:, e, f, :],
                                         start=(f == 0), stop=(f == FT - 1))
                    last_.then_inc(f_ps, 1)
                i, place, gr = tile_of(group, q, 0)
                if i is not None:
                    pe.wait_ge(h_set, i + 1)
                    need(pe, ht_set, i)
                    for f in range(FT):
                        last_ = m.transpose(ps[:, 2 + f // 4, (f % 4) * P:(f % 4 + 1) * P],
                                            h_sb[:, f * P:(f + 1) * P], ident)
                    last_.then_inc(ht_ps, 1)

            pe.wait_ge(experts_set, 1)
            turn_rows(0, 0, 0)
            pe.wait_ge(loaded["w1"], 16 * NB)
            pe.wait_ge(loaded["w2"], 16 * NE)
            f_steps(pe, f_step, TILES)


def kernel(**inputs):
    import numpy as _np
    import concourse.bacc as _bacc
    from concourse import mybir as _mybir
    from concourse.bass_utils import run_bass_kernel_spmd as _run

    a = {k.removeprefix("L0_"): _np.asarray(v) for k, v in inputs.items()}

    def rows(x, tiles):
        return x.reshape(tiles, P, *x.shape[1:]).swapaxes(0, 1)

    _, table = constant_columns()
    laid = {
        "consts": table,
        "lens": a["mask_BxS2_if0"],
        "x": a["x"],
        "x_t": rows(a["x"].reshape(T, D).T, DT),
        "ctx": a["ctx_2048"][:, :L, :],
        "w_in": rows(a["attn_W_in"].T, DT),
        "conv_w": rows(a["attn_conv_w"], HT),
        "conv_b": rows(a["attn_conv_b"], HT),
        "log_dt": rows(a["attn_log_dt"], HT),
        "d_skip": rows(a["attn_D"], HT),
        "ssm": _np.stack([rows(a["attn_" + n], HT).reshape(P, HT * MODES)
                          for n in ("log_A_real", "A_imag", "C_re", "C_im")], axis=1),
        "w_out": rows(a["attn_W_out"].T, HT),
        "w_x": rows(a["xattn_W_in"].T, DT),
        "b_x": a["xattn_b_in"].reshape(1, D),
        "one_row": _np.ones((1, T), _np.float32),
        "g_res": rows(a["xattn_g_res"], DT),
        "g_init": a["xattn_g_init"][:D].reshape(1, D),
        "w_r": rows(a["ffn_Wr"].T, DT),
        "b_r": a["ffn_br"].reshape(1, NE),
        "w1": a["ffn_W1"].transpose(0, 2, 1).reshape(NE, DT, P, FF).transpose(2, 0, 1, 3),
        "b1": a["ffn_b1"].reshape(NE, FT, P).transpose(2, 0, 1).reshape(P, NE * FT),
        "w2": a["ffn_W2"].transpose(0, 2, 1).reshape(NE, FT, P, D).transpose(2, 0, 1, 3),
        "b2": a["ffn_b2"].reshape(1, NE * D),
    }
    nc = _bacc.Bacc("TRN2", target_bir_lowering=False, num_devices=1)
    arrays, ins = {}, {}
    for name, x in laid.items():
        x = _np.ascontiguousarray(x)
        arrays[f"in_{name}"] = x
        ins[name] = nc.dram_tensor(f"in_{name}", x.shape, _mybir.dt.from_np(x.dtype), kind="ExternalInput").ap()
    out = nc.dram_tensor("out_0", (T, D), F32, kind="ExternalOutput").ap()
    decoder_layer(nc, ins, out)
    r = _run(nc, [arrays], core_ids=[0])
    return r.results[0]["out_0"].reshape(NB, L, D)
```

```python
from contextlib import ExitStack
import math

import numpy as np
import concourse.bass as bass
from concourse import mybir

F32 = mybir.dt.float32
BF16 = mybir.dt.bfloat16
I32 = mybir.dt.int32
ALU = mybir.AluOpType
ACT = mybir.ActivationFunctionType
AX_X = mybir.AxisListType.X

NB, L, D = 16, 112, 256
H, MODES, TAPS = 512, 8, 4
C, PATCHES = 512, 375
NE, FF = 8, 1024
T = NB * L
P = 128
HT = H // P
DT = D // P
FT = FF // P
NC = 4
CB = NB // NC
CW = CB * L
NFFT = 2 * L
PT, PP = 3, 125
LO, LA = 16, L // 16
TILES = (T - NE) // P + NE
TPE = -(-T // P)

EPS = 1e-5
LOGP = -0.001
DECAY = -math.log(-math.expm1(LOGP))
BCOEF = math.exp(LOGP)
MAGIC = 1.5 * 2.0 ** 23
TWO_PI_HI = 6.28125
TWO_PI_LO = 2 * math.pi - TWO_PI_HI
PI_BELOW = 3.1415925
PAST = 1.0e4


def constant_columns():
    t = np.arange(L)
    parts = {}

    def put(name, a):
        full = np.zeros((P, a.shape[1]), np.float32)
        full[:a.shape[0]] = a
        parts[name] = full

    put("ident", np.eye(P))
    angle = 2 * np.pi * np.outer(t, t) / NFFT
    cos, sin = np.cos(angle), np.sin(angle)
    nyquist = (-1.0) ** t
    zero0 = (t > 0).astype(float)
    put("f_re", cos)
    f_im = -sin
    f_im[:, 0] = nyquist
    put("f_im", f_im)
    put("f_im0", -sin * zero0)
    f_d = cos.copy()
    f_d[:, 0] = nyquist
    put("f_d", f_d)
    g_re = 2 * cos / NFFT
    g_re[0] = 1.0 / NFFT
    put("g_re", g_re)
    g_im = -2 * sin / NFFT
    g_im[0] = nyquist / NFFT
    put("g_im", g_im)
    put("earlier", (t[:, None] < t[None, :]).astype(float))
    put("iota", np.tile(np.arange(P), (P, 1)))
    put("seq_m16", np.tile(np.arange(NB) - NB, (P, 1)))
    put("part", np.arange(P)[:, None])
    put("expert_m8", np.tile(np.arange(NE) - NE, (P, NB)))
    not_first = np.ones((NE, NB))
    not_first[:, 0] = 0
    put("seq_reset", np.tile(not_first.ravel(), (P, 1)))
    put("tile_from", np.tile(P * np.arange(TPE), (P, NE)))
    put("tile_no", np.tile(np.arange(TILES).repeat(NE), (P, 1)))
    lags = list(LO * np.arange(LA)) + list(range(LO)) + [0.5]
    put("lags", np.tile(np.array(lags), (P, 1)))
    put("m_half", np.full((P, 1), -0.5))
    put("zero", np.zeros((P, 1)))
    put("eps", np.full((P, 1), EPS))
    at, n = {}, 0
    for name, a in parts.items():
        at[name] = (n, n + a.shape[1])
        n += a.shape[1]
    return at, np.concatenate(list(parts.values()), axis=1)


def need(engine, semaphore, value):
    if not (isinstance(value, int) and value <= 0):
        engine.wait_ge(semaphore, value)


def decoder_layer(nc, ins, out):
    at, _ = constant_columns()
    n_const = max(b for _, b in at.values())
    NLAG = LA + LO + 1

    with ExitStack() as ctx:
        def sb(name, shape, dt=F32):
            return ctx.enter_context(nc.sbuf_tensor(name, shape, dt))

        def sem(name):
            return ctx.enter_context(nc.semaphore(name))

        x2_rows = nc.dram_tensor("x2_rows", (T + 1, D), F32, kind="Internal").ap()
        ps = ctx.enter_context(nc.psum_tensor("ps", [P, 8, 512], F32))

        class Region:

            def __init__(self, tensor, words):
                self.tensor, self.words, self.used = tensor, words, 0

            def cut(self, words, rows=P):
                self.used += words
                assert self.used <= self.words, (self.used, self.words)
                return self.tensor[0:rows, self.used - words:self.used]

        consts = sb("consts", [P, n_const])

        def const(name, rows=P):
            a, b = at[name]
            return consts[0:rows, a:b]

        ident = const("ident")
        ones16 = sb("ones16", [P, P], BF16)
        tri16 = sb("tri16", [L, L], BF16)
        w_x = sb("w_x", [P, DT, D])
        g_res = sb("g_res", [P, DT])
        w_r = sb("w_r", [P, DT, NE])
        b_r = sb("b_r", [L, NE])
        g_init = sb("g_init", [L, D])
        b1 = sb("b1", [P, NE * FT])
        logits = sb("logits", [L, NB * NE])

        w1_flat = sb("w1", [P, NE * DT * FF])
        w1 = w1_flat[:, :].rearrange("p (e k f) -> p e k f", e=NE, k=DT)
        r = Region(w1_flat, NE * DT * FF)
        nm = HT * NLAG * MODES
        theta = r.cut(2 * nm)
        turns = r.cut(2 * nm)
        mag = r.cut(nm)
        n_prod = LA * LO * 2 * MODES
        k_prods = [w1_flat[:, 0:n_prod], w1_flat[:, n_prod:2 * n_prod], r.cut(n_prod)]
        assert 2 * n_prod <= 5 * nm
        k_tmp = r.cut(HT * LA * MODES).rearrange("p (h a m) -> p h a m", h=HT, a=LA)
        modes_a = r.cut(HT * LA * 2 * MODES).rearrange("p (h a m) -> p h a m", h=HT, a=LA)
        modes_c = r.cut(HT * LO * 2 * MODES).rearrange("p (h c m) -> p h c m", h=HT, c=LO)
        cplx = r.cut(HT * LA * MODES * 2).rearrange("p (s h a m) -> p s h a m", s=2, h=HT, a=LA)
        kern = r.cut(HT * L).rearrange("p (h l) -> p h l", h=HT)
        kern_t = r.cut(H, L)
        log_dt, dt, d_skip = r.cut(HT), r.cut(HT), r.cut(HT)
        ssm = r.cut(4 * HT * MODES).rearrange("p (s m) -> p s m", s=4)
        km = r.cut(24 * HT * MODES).rearrange("p (s m) -> p s m", s=24)
        conv_w = r.cut(HT * TAPS).rearrange("p (h w) -> p h w", h=HT)
        conv_b = r.cut(HT)
        conv_acc = r.cut(2 * CW).rearrange("p (r n) -> p r n", r=2)
        conv_x = r.cut(2 * CW).rearrange("p (r n) -> p r n", r=2)
        lens = r.cut(PATCHES, NB).bitcast(I32)
        ends = r.cut(4 * PATCHES, NB).rearrange("b (s n) -> b s n", s=4)
        ends_t = r.cut(PT * NB, PP)
        far = k_prods[2][0:PP, 0:T]
        pad_row = r.cut(D, 1)
        assert r.used >= 3 * DT * FF
        k_prods.append(r.cut(n_prod))
        fall = k_prods[3][0:L, 0:T]
        dt_count, recip_count, mag_count, modes_count = [], [], [], []

        w2_flat = sb("w2", [P, NE * FT * D])
        w2 = w2_flat[:, :].rearrange("p (e m d) -> p e m d", e=NE, m=FT)
        r = Region(w2_flat, NE * FT * D)
        x_time = r.cut(NB * H, L).rearrange("p (b h) -> p b h", b=NB)
        hid_t = r.cut(DT * T).rearrange("p (k t) -> p k t", k=DT)
        w_in = r.cut(DT * 2 * H).rearrange("p (k h) -> p k h", k=DT)
        w_out = r.cut(HT * D).rearrange("p (k d) -> p k d", k=HT)
        spec = r.cut(3 * H, L).rearrange("p (s h) -> p s h", s=3)

        shared = sb("shared", [P, 2048])
        plug = shared[0:L, 0:T]
        decay = shared[0:L + 1, 0:T]
        b2 = shared[:, :].rearrange("p (e d) -> p e d", e=NE)

        N_B = 10176
        stage_b = sb("stage_b", [P, N_B])
        r = Region(stage_b, N_B)

        def two(words, rows=P):
            return r.cut(2 * words, rows).rearrange("p (r n) -> p r n", r=2)

        prod = r.cut(4 * H, L).rearrange("p (s h) -> p s h", s=4)
        y_spec = r.cut(2 * H, L).rearrange("p (s h) -> p s h", s=2)
        z_act, gated = two(HT * L), two(HT * L)
        x_res, x1, x2_sum, x2, ctx_sb = two(D, L), two(D, L), two(D, L), two(D, L), two(C, L)
        x1_pre = r.cut(D, L)
        x1_t, x2_t = two(DT * L), two(DT * L)
        u = two(D, L + 1)
        decay_b = two(L, L + 1)
        ctx_sq = r.cut(C // 2, L).bitcast(BF16)
        small_b = r.cut(80, L)
        bn = [small_b[:, 0:6], small_b[:, 6:12]]
        mv = [[small_b[:, 12 + 4 * n + 2 * q:14 + 4 * n + 2 * q] for q in range(2)] for n in range(2)]
        nr = [[small_b[:, 20 + 8 * n + 4 * q:24 + 8 * n + 4 * q] for q in range(2)] for n in range(2)]
        cs = [small_b[:, 36 + 4 * q:40 + 4 * q] for q in range(2)]
        rr = [small_b[:, 44 + 4 * q:48 + 4 * q] for q in range(2)]
        r = Region(stage_b, N_B)
        run = r.cut(T, L)
        hits = r.cut(PT * T // 2, PP).bitcast(BF16).rearrange("p (k n) -> p k n", k=PT)
        assert r.used <= 6 * H + 4 * HT * L
        r = Region(stage_b, N_B)
        h_sb = r.cut(FF)
        h_t = two(FF)
        rows_t = two(D)
        y_sum, y_row = two(D), two(D)
        rows = r.cut(4 * D).rearrange("p (r n) -> p r n", r=4)
        rt = r.cut(9 * NB * NE).rearrange("p (s n) -> p s n", s=9)
        one_hot = r.cut(NB * NE // 2, L).bitcast(BF16)
        tile_n = r.cut(NE * TPE)
        per_e = r.cut(4 * NE).rearrange("p (s e) -> p s e", s=4)
        tile_hits = r.cut(TILES * NE)
        tile_e = r.cut(2 * (TILES + 1)).rearrange("p (s n) -> p s n", s=2)
        tile_expert = r.cut(TILES + 1).bitcast(I32)
        slot_f = r.cut(NB, L)
        slot_part, slot_tile = r.cut(NB, L), r.cut(NB, L)
        in_place = r.cut(NB * P // 2, L).bitcast(BF16).rearrange("p (b n) -> p b n", b=NB)
        in_tile = r.cut(NB * TILES, L).rearrange("p (b i) -> p b i", b=NB)
        token_parts = r.cut(NB * TILES, L).bitcast(BF16).rearrange("p (b s i) -> p b s i", b=NB, s=2)
        token_of = r.cut(TILES).bitcast(I32)
        token_f = r.cut(TILES)
        f_bn, f_mv, f_nr = r.cut(6), two(2), two(2)
        f_index = two(1).bitcast(I32)
        g_index = r.cut(4).bitcast(I32).rearrange("p (r n) -> p r n", r=4)

        loaded = {k: sem("loaded_" + k) for k in (
            "consts", "ssm", "w_in_x", "w_in_z", "conv", "w_out", "lens", "small", "b2", "w1", "w2", "pad")}
        hid_loaded = [sem(f"hid_loaded{c}") for c in range(NC)]
        far_set = sem("far_set")
        ones_set, tri_set = sem("ones_set"), sem("tri_set")
        b_step, ends_ps, ends_sb, hits_set, count_ps = (
            sem(s) for s in ("b_step", "ends_ps", "ends_sb", "hits_set", "count_ps"))
        run_set, plug_set, plug_scan, plug_ready, fall_step, decay_set, decay_kept = (
            sem(s) for s in ("run_set", "plug_set", "plug_scan", "plug_ready", "fall_step", "decay_set",
                             "decay_kept"))
        k_exp, k_pool, k_phase, k_recip, k_sin, k_prod_set, k_own, k_sum = (
            sem(s) for s in ("k_exp", "k_pool", "k_phase", "k_recip", "k_sin", "k_prod_set", "k_own", "k_sum"))
        kern_ps, kern_sb, spec_ps, spec_set = (sem(s) for s in ("kern_ps", "kern_sb", "spec_ps", "spec_set"))
        in_ps, acc_set, tap_set, conv_done, act_x, xt_ps, xt_set = (
            sem(s) for s in ("in_ps", "acc_set", "tap_set", "conv_done", "act_x", "xt_ps", "xt_set"))
        dft_ps, prod_set, y_set, z_ps, z_set, idft_ps, gate_set, out_ps = (
            sem(s) for s in ("dft_ps", "prod_set", "y_set", "z_ps", "z_set", "idft_ps", "gate_set", "out_ps"))
        x_loaded = [sem(f"x_loaded{q}") for q in range(2)]
        c_loaded = [sem(f"c_loaded{q}") for q in range(2)]
        pre_set, bn1_set, mv1_set, nr1_step, r1_set, x1_set = (
            sem(s) for s in ("pre_set", "bn1_set", "mv1_set", "nr1_step", "r1_set", "x1_set"))
        sq_set, cs_step, cs_set, u_set = (sem(s) for s in ("sq_set", "cs_step", "cs_set", "u_set"))
        x1t_ps, x1t_set, cross_ps, sum1_set, sum2_set = (
            sem(s) for s in ("x1t_ps", "x1t_set", "cross_ps", "sum1_set", "sum2_set"))
        bn2_set, mv2_set, nr2_step, r2_set, x2_set = (
            sem(s) for s in ("bn2_set", "mv2_set", "nr2_step", "r2_set", "x2_set"))
        x2_stored = [sem(f"x2_stored{q}") for q in range(2)]
        x2t_ps, x2t_set, logit_ps, logit_set = (
            sem(s) for s in ("x2t_ps", "x2t_set", "logit_ps", "logit_set"))
        r_step, one_hot_set, rank_ps, experts_set, pad_set = (
            sem(s) for s in ("r_step", "one_hot_set", "rank_ps", "experts_set", "pad_set"))
        place_set, in_tile_set, parts_set, token_ps, token_step, token_set = (
            sem(s) for s in ("place_set", "in_tile_set", "parts_set", "token_ps", "token_step", "token_set"))
        rows_loaded = [sem(f"rows_loaded{q}") for q in range(4)]
        rows_out = [sem(f"rows_out{q}") for q in range(4)]
        rt_ps, rt_set, h_ps, h_set, ht_ps, ht_set, f_ps = (
            sem(s) for s in ("rt_ps", "rt_set", "h_ps", "h_set", "ht_ps", "ht_set", "f_ps"))
        fb_set, fs_set, fbn_set, fmv_set, fn_step, fr_set, y_done = (
            sem(s) for s in ("fb_set", "fs_set", "fbn_set", "fmv_set", "fn_step", "fr_set", "y_done"))
        index_set, g_index_set = sem("index_set"), sem("g_index_set")

        PRO, EPI = 6, 4
        F_PRO, F_UNROLL = 4, 4
        F_AHEAD = 3

        def b_steps(engine, step):
            for s in range(PRO):
                step(s // 2, s % 2)
            with engine.Fori(PRO // 2, NB // 2) as pair:
                for q in range(2):
                    step(pair, q)
            for s in range(NB, NB + EPI):
                step(s // 2, s % 2)

        def seq(pair, q, lag):
            par, half = (q - lag) % 2, pair + (q - lag) // 2
            b = 2 * half + par
            if isinstance(b, int) and not 0 <= b < NB:
                return None, par, half
            return b, par, half

        def f_steps(engine, step, finish=None):
            groups = (TPE + 2 - F_PRO) // F_UNROLL
            for s in range(F_PRO):
                step(s // F_UNROLL, s % F_UNROLL)
            with engine.Fori(1, 1 + groups) as group:
                for q in range(F_UNROLL):
                    step(group, q)
            used = engine.value_load(tile_expert[0:1, TILES:TILES + 1], min_val=TPE, max_val=TILES)

            def last_steps(s):
                def end(tiles):
                    for n in range(s, tiles + 2):
                        step(n // F_UNROLL, n % F_UNROLL, tiles)
                    if finish:
                        finish(tiles)

                if s == TILES:
                    end(TILES)
                    return
                with engine.If(used > s):
                    step(s // F_UNROLL, s % F_UNROLL)
                    last_steps(s + 1)
                with engine.Else():
                    end(s)

            last_steps(F_UNROLL * (1 + groups))

        def tile_of(group, q, lag, tiles):
            place, g = (q - lag) % F_UNROLL, group + (q - lag) // F_UNROLL
            i = F_UNROLL * g + place
            if isinstance(i, int) and not 0 <= i < tiles:
                return None, place, g
            return i, place, g

        def apart(engine, *waits):
            waits = [(s, v if isinstance(v, int) else engine.snap(v)) for s, v in waits]
            if not all(isinstance(v, int) for _, v in waits):
                engine.wait_ge(loaded["consts"], 16)
            for s, v in waits:
                need(engine, s, v)

        K_PHASE = 7
        POOL_K = 3

        def k_products(engine, h, dst):
            for a in range(LA):
                last = engine.tensor_tensor(
                    dst[:, a * LO * 2 * MODES:(a + 1) * LO * 2 * MODES].rearrange("p (c m) -> p c m", c=LO),
                    modes_c[:, h], modes_a[:, h, a].unsqueeze(1).to_broadcast([P, LO, 2 * MODES]), ALU.mult)
            return last

        block = ctx.enter_context(nc.Block())

        @block.sync
        def _(sp):
            sp.dma_start(lens, ins["lens"]).then_inc(loaded["lens"], 16)
            sp.dma_start(consts[:, :], ins["consts"]).then_inc(loaded["consts"], 16)
            for dst, name in ((log_dt, "log_dt"), (d_skip, "d_skip"), (ssm, "ssm")):
                sp.dma_start(dst, ins[name]).then_inc(loaded["ssm"], 16)
            sp.dma_start(w_in[:, :, 0:H], ins["w_in"][:, :, 0:H]).then_inc(loaded["w_in_x"], 16)
            sp.dma_start(conv_w, ins["conv_w"]).then_inc(loaded["conv"], 16)
            sp.dma_start(conv_b, ins["conv_b"]).then_inc(loaded["conv"], 16)
            for c in range(NC):
                sp.dma_start(hid_t[:, :, c * CW:(c + 1) * CW], ins["x_t"][:, :, c * CW:(c + 1) * CW])\
                  .then_inc(hid_loaded[c], 16)
            sp.dma_start(w_in[:, :, H:2 * H], ins["w_in"][:, :, H:2 * H]).then_inc(loaded["w_in_z"], 16)
            sp.dma_start(w_out, ins["w_out"]).then_inc(loaded["w_out"], 16)
            for dst, name in ((w_x[:, :, :], "w_x"), (g_res[:, :], "g_res"), (w_r[:, :, :], "w_r"),
                              (b1[:, :], "b1"),
                              (u[L:L + 1, 0, :], "b_x"), (u[L:L + 1, 1, :], "b_x"),
                              (decay[L:L + 1, :], "one_row")):
                sp.dma_start(dst, ins[name]).then_inc(loaded["small"], 16)
            sp.dma_start(b_r[:, :], ins["b_r"].to_broadcast([L, NE])).then_inc(loaded["small"], 16)
            sp.dma_start(g_init[:, :], ins["g_init"].to_broadcast([L, D])).then_inc(loaded["small"], 16)
            sp.wait_ge(pad_set, 1)
            sp.dma_start(x2_rows[T:T + 1, :], pad_row).then_inc(loaded["pad"], 16)
            w2_pieces = ins["w2"].rearrange("p e m d -> p (e m d)")

            def step(pair, q):
                b, par, half = seq(pair, q, 4)
                if b is not None:
                    sp.wait_ge(x2_set, b + 1)
                    sp.dma_start(x2_rows[bass.ds(b * L, L), :], x2[:, par, :]).then_inc(x2_stored[par], 16)
                b, par, half = seq(pair, q, 1)
                if b is not None:
                    sp.wait_ge(dft_ps, b + 1)
                    sp.dma_start(w2_flat[:, bass.ds(b * H, H)], w2_pieces[:, bass.ds(b * H, H)])\
                      .then_inc(loaded["w2"], 16)
                b, par, half = seq(pair, q, 0)
                if b is None:
                    return
                need(sp, u_set, b - 1)
                sp.dma_start(ctx_sb[:, par, :], ins["ctx"][b, :, :]).then_inc(c_loaded[par], 16)
                need(sp, pre_set, b - 1)
                sp.dma_start(x_res[:, par, :], ins["x"][b, :, :]).then_inc(x_loaded[par], 16)
                if isinstance(b, int) and b == 0:
                    sp.wait_ge(spec_set, 3)
                    sp.wait_ge(xt_ps, HT * NC)
                    sp.wait_ge(loaded["pad"], 16)
                if not isinstance(b, int):
                    sp.wait_ge(decay_set, 1)
                sp.dma_start(w1[:, half, par, :], ins["w1"][:, half, par, :]).then_inc(loaded["w1"], 16)

            b_steps(sp, step)
            sp.wait_ge(out_ps, NB)
            sp.wait_ge(gate_set, NB)
            for e in range(NE // 2, NE):
                sp.dma_start(w2[:, e, :, :], ins["w2"][:, e, :, :]).then_inc(loaded["w2"], 16)
            sp.wait_ge(cross_ps, NB)
            sp.dma_start(shared[:, :], ins["b2"].to_broadcast([P, NE * D])).then_inc(loaded["b2"], 16)


        @block.gpsimd
        def _(pool):
            g = nc.gpsimd
            pool.wait_ge(loaded["consts"], 16)
            g.memset(ones16[:, :], 1.0).then_inc(ones_set, 1)
            g.tensor_copy(tri16[:, :], const("earlier", L)).then_inc(tri_set, 1)
            g.memset(pad_row, 0.0).then_inc(pad_set, 1)
            g.memset(run, 1.0).then_inc(run_set, 1)
            pool.wait_ge(run_set, 1)
            g.memset(run.rearrange("p (b t) -> p b t", b=NB)[:, :, 0:1], 0.0).then_inc(run_set, 1)

            done = 0

            def link(ins_):
                nonlocal done
                done += 1
                ins_.then_inc(k_pool, 1)
                pool.wait_ge(k_pool, done)

            def mul(o, a, b):
                link(g.tensor_tensor(o, a, b, ALU.mult))

            def add(o, a, b):
                link(g.tensor_tensor(o, a, b, ALU.add))

            def sub(o, a, b):
                link(g.tensor_tensor(o, a, b, ALU.subtract))

            def scale(o, a, m, c=0.0):
                link(g.tensor_scalar(o, a, m, c, ALU.mult, ALU.add))

            a_re, a_im, c_re, c_im = (ssm[:, n, :] for n in range(4))
            K = [km[:, n, :] for n in range(24)]
            a_abs, dta, dtb, th, em1, den, sq1, sq2, q_inv, sn, cs_, e_re, e_im, n_re, n_im, ct_re, ct_im, \
                tmp, tmp2 = K[0:19]
            pool.wait_ge(k_exp, 2)
            dt_b = dt.unsqueeze(2).to_broadcast([P, HT, MODES])
            as_hm = lambda v: v.rearrange("p (h m) -> p h m", h=HT)
            mul(as_hm(dta), as_hm(a_abs), dt_b)
            scale(dta, dta, -1.0)
            mul(as_hm(dtb), as_hm(a_im), dt_b)
            dt_count.append(done)
            th4 = theta.rearrange("p (s h l m) -> p s h l m", s=2, h=HT, l=NLAG)
            mg4 = mag.rearrange("p (h l m) -> p h l m", h=HT, l=NLAG)
            mul(mg4, const("lags").unsqueeze(1).unsqueeze(3).to_broadcast([P, HT, NLAG, MODES]),
                as_hm(dta).unsqueeze(2).to_broadcast([P, HT, NLAG, MODES]))
            mag_count.append(done)
            mul(sq1, a_abs, a_abs)
            mul(sq2, a_im, a_im)
            add(sq1, sq1, sq2)
            pool.wait_ge(k_exp, 3)
            scale(den, th, -1.0, 1.0)
            recip_count.append(done)
            pool.wait_ge(ends_sb, 1)
            hits_at = 0
            for k in range(PT):
                last = g.tensor_tensor(
                    far.rearrange("p (b t) -> p b t", b=NB),
                    const("iota", PP)[:, 0:L].unsqueeze(1).to_broadcast([PP, NB, L]),
                    ends_t[:, k * NB:(k + 1) * NB].unsqueeze(2).to_broadcast([PP, NB, L]), ALU.subtract)
                last.then_inc(far_set, 1)
                hits_at += 1
                pool.wait_ge(far_set, hits_at)
                g.tensor_scalar(hits[:, k, :], far, 0.0, None, ALU.is_equal).then_inc(hits_set, 1)
                pool.wait_ge(hits_set, hits_at)
            pool.wait_ge(k_recip, 2)
            mul(em1, th, den)
            scale(em1, em1, 2.0)
            pool.wait_ge(k_exp, 4)
            pool.wait_ge(k_sin, 1)
            s_half = th4[:, 0, :, NLAG - 1, :]
            c_half = th4[:, 1, :, NLAG - 1, :]
            mul(as_hm(sn), s_half, c_half)
            scale(sn, sn, 2.0)
            mul(as_hm(tmp), s_half, s_half)
            scale(tmp, tmp, 2.0)
            scale(cs_, tmp, -1.0, 1.0)
            mul(e_re, em1, cs_)
            sub(e_re, e_re, tmp)
            scale(tmp, em1, 1.0, 1.0)
            mul(e_im, tmp, sn)
            mul(n_re, c_re, e_re)
            mul(tmp, c_im, e_im)
            sub(n_re, n_re, tmp)
            mul(n_im, c_re, e_im)
            mul(tmp, c_im, e_re)
            add(n_im, n_im, tmp)
            mul(tmp, n_im, a_im)
            mul(tmp2, n_re, a_abs)
            sub(tmp, tmp, tmp2)
            mul(ct_re, tmp, sq1)
            mul(tmp, n_re, a_im)
            mul(tmp2, n_im, a_abs)
            add(tmp, tmp, tmp2)
            mul(ct_im, tmp, sq1)
            scale(ct_re, ct_re, 2.0)
            scale(ct_im, ct_im, -2.0)
            for s, dst in ((1, 0), (0, MODES)):
                mul(modes_c[:, :, :, dst:dst + MODES], th4[:, s, :, LA:LA + LO, :], mg4[:, :, LA:LA + LO, :])
                mul(cplx[:, 1 - s], th4[:, s, :, 0:LA, :], mg4[:, :, 0:LA, :])
            cr = as_hm(ct_re).unsqueeze(2).to_broadcast([P, HT, LA, MODES])
            ci = as_hm(ct_im).unsqueeze(2).to_broadcast([P, HT, LA, MODES])
            a_r, a_i = modes_a[:, :, :, 0:MODES], modes_a[:, :, :, MODES:2 * MODES]
            mul(a_r, cplx[:, 0], cr)
            mul(k_tmp, cplx[:, 1], ci)
            sub(a_r, a_r, k_tmp)
            mul(a_i, cplx[:, 0], ci)
            mul(k_tmp, cplx[:, 1], cr)
            add(a_i, a_i, k_tmp)
            scale(a_i, a_i, -1.0)
            modes_count.append(done)
            for h in range(POOL_K):
                k_products(g, h, k_prods[h]).then_inc(k_prod_set, 1)

            m_half = const("m_half", L)

            def rsqrt(o, a, tmp_, chain, count):
                g.tensor_tensor(tmp_, a, const("eps", a.shape[0]), ALU.add).then_inc(chain, 1)
                pool.wait_ge(chain, count + 1)
                return g.tensor_tensor(o, tmp_, m_half[0:o.shape[0]], ALU.pow)

            def step(pair, q):
                b, par, half = seq(pair, q, 1)
                if b is not None:
                    pool.wait_ge(sq_set, b + 1)
                    need(pool, u_set, b - 1)
                    g.tensor_tensor(cs[par][:, 1:2], cs[par][:, 0:1], const("eps", L), ALU.add).then_inc(cs_step, 1)
                    pool.wait_ge(cs_step, b + 1)
                    g.tensor_tensor(rr[par][:, 0:1], cs[par][:, 1:2], m_half, ALU.pow).then_inc(cs_set, 1)
                b, par, half = seq(pair, q, 0)
                if b is not None:
                    pool.wait_ge(prod_set, b + 1)
                    need(pool, idft_ps, b)
                    g.tensor_tensor(y_spec[:, 0, :], prod[:, 0, :], prod[:, 1, :], ALU.subtract)
                    g.tensor_tensor(y_spec[:, 1, :], prod[:, 2, :], prod[:, 3, :], ALU.add).then_inc(y_set, 1)
                b, par, half = seq(pair, q, 2)
                if b is not None:
                    pool.wait_ge(mv1_set, b + 1)
                    need(pool, x1_set, b - 1)
                    need(pool, sum1_set, b - 1)
                    n_ = nr[0][par]
                    rsqrt(n_[:, 1:2], mv[0][par][:, 1:2], n_[:, 0:1], nr1_step, 5 * b).then_inc(nr1_step, 1)
                    pool.wait_ge(nr1_step, 5 * b + 2)
                    g.tensor_tensor(n_[:, 2:3], mv[0][par][:, 1:2], n_[:, 1:2], ALU.mult).then_inc(nr1_step, 1)
                    pool.wait_ge(nr1_step, 5 * b + 3)
                    g.tensor_tensor(n_[:, 2:3], n_[:, 2:3], n_[:, 1:2], ALU.mult).then_inc(nr1_step, 1)
                    pool.wait_ge(nr1_step, 5 * b + 4)
                    rsqrt(n_[:, 3:4], n_[:, 2:3], n_[:, 0:1], nr1_step, 5 * b + 4).then_inc(r1_set, 1)
                b, par, half = seq(pair, q, 3)
                if b is not None:
                    pool.wait_ge(mv2_set, b + 1)
                    need(pool, x2_set, b - 1)
                    rsqrt(nr[1][par][:, 1:2], mv[1][par][:, 1:2], nr[1][par][:, 0:1], nr2_step, b)\
                        .then_inc(r2_set, 1)

            b_steps(pool, step)

            pool.wait_ge(in_tile_set, 1)
            g.tensor_tensor(token_parts[:, :, 0, :], in_tile,
                            const("seq_m16", L).unsqueeze(2).to_broadcast([L, NB, TILES]), ALU.mult)
            g.tensor_scalar(token_parts[:, :, 1, :], in_tile, const("part", L), None, ALU.mult)\
             .then_inc(parts_set, 1)

            m_half_f = const("m_half")
            last_token = pool.to_reg(T - 1)

            def take_index(i, place):
                g.tensor_copy(g_index[:, place, :], token_of[:, bass.ds(i, 1)]).then_inc(g_index_set, 1)

            def gather(place):
                g.indirect_dma_start(rows[:, place, :], None, x2_rows, bass.IndirectOffsetOnAxis(
                    ap=g_index[:, place, :], axis=0)).then_inc(rows_loaded[place], 16)

            pool.wait_ge(token_set, 1)
            pool.wait_ge(loaded["pad"], 16)
            for i in range(F_AHEAD):
                take_index(i, i)
                pool.wait_ge(g_index_set, i + 1)
                gather(i)

            def f_step(group, q, tiles=TILES):
                ahead, a_place, a_gr = tile_of(group, q, -F_AHEAD, tiles)
                if ahead is not None:
                    apart(pool, (fs_set, ahead - 3))
                    take_index(ahead, a_place)
                i, place, gr = tile_of(group, q, 1, tiles)
                par = place % 2
                if i is not None:
                    pool.wait_ge(fmv_set, i + 1)
                    need(pool, y_done, i - 1)
                if ahead is not None:
                    pool.wait_ge(g_index_set, ahead + 1)
                if i is not None:
                    g.tensor_tensor(f_nr[:, par, 0:1], f_mv[:, par, 1:2], const("eps"), ALU.add).then_inc(fn_step, 1)
                if ahead is not None:
                    gather(a_place)
                if i is not None:
                    pool.wait_ge(fn_step, i + 1)
                    g.tensor_tensor(f_nr[:, par, 1:2], f_nr[:, par, 0:1], m_half_f, ALU.pow).then_inc(fr_set, 1)
                    apart(pool, (y_done, i + 1))
                    g.tensor_copy(f_index[:, par, :], token_of[:, bass.ds(i, 1)]).then_inc(index_set, 1)
                    apart(pool, (index_set, i + 1))
                    g.indirect_dma_start(out, bass.IndirectOffsetOnAxis(
                        ap=f_index[:, par, :], axis=0), y_row[:, par, :], None,
                        bounds_check=last_token, oob_is_err=False).then_inc(rows_out[place], 16)
            def finish(tiles):
                for i in range(tiles + 1, min(tiles + F_AHEAD, TILES)):
                    pool.wait_ge(rows_loaded[i % 4], 16 * (i // 4 + 1))
                for place in range(4):
                    pool.wait_ge(rows_out[place], 16 * len(range(place, tiles, 4)))

            f_steps(pool, f_step, finish)

        @block.scalar
        def _(act):
            a = nc.scalar
            act.wait_ge(loaded["ssm"], 48)
            a.activation(dt, log_dt, ACT.Exp).then_inc(k_exp, 1)
            a.activation(km[:, 0, :], ssm[:, 0, :], ACT.Exp).then_inc(k_exp, 1)
            act.wait_ge(k_pool, 2)
            a.activation(km[:, 3, :], km[:, 1, :], ACT.Tanh, scale=0.5).then_inc(k_exp, 1)

            def a_step(c, h):
                unit = HT * c + h
                par = h % 2
                act.wait_ge(in_ps, unit + 1)
                need(act, act_x, unit - 1)
                a.activation(conv_acc[:, par, :], ps[:, h, 0:CW], ACT.Copy, scale=conv_w[:, h, TAPS - 1:TAPS])\
                 .then_inc(acc_set, 1)

            def a_silu(unit, h):
                par = h % 2
                act.wait_ge(conv_done, unit + 1)
                need(act, xt_ps, unit - 1)
                a.activation(conv_x[:, par, :], conv_acc[:, par, :], ACT.Silu, bias=conv_b[:, h:h + 1])\
                 .then_inc(act_x, 1)

            def a_move(c, h):
                unit = HT * c + h
                act.wait_ge(xt_ps, unit + 1)
                a.activation(x_time[:, bass.ds(CB * c, CB), h * P:(h + 1) * P],
                             ps[0:L, 4 + h % 2, :].rearrange("p (b h) -> p b h", b=CB), ACT.Copy)\
                 .then_inc(xt_set, 1)

            def a_unit(c, h):
                before = (c, h - 1) if h else (c - 1, HT - 1)
                if not (isinstance(c, int) and before[0] < 0):
                    a_silu(HT * c + h - 1, (h - 1) % HT)
                if not (isinstance(c, int) and (c, h) == (NC - 1, HT - 1)):
                    a_step(*((c, h + 1) if h < HT - 1 else (c + 1, 0)))
                before2 = (c, h - 2) if h >= 2 else (c - 1, h + HT - 2)
                if not (isinstance(c, int) and before2[0] < 0):
                    a_move(*before2)

            act.wait_ge(loaded["conv"], 32)
            a_step(0, 0)
            for h in range(HT):
                a_unit(0, h)
                if h == 1:
                    act.wait_ge(k_pool, mag_count[0])
                    a.activation(mag, mag, ACT.Exp).then_inc(k_exp, 1)
                    act.wait_ge(k_phase, K_PHASE)
                    a.activation(theta, theta, ACT.Sin).then_inc(k_sin, 1)
            with act.Fori(1, NC - 1) as c:
                for h in range(HT):
                    a_unit(c, h)
            for h in range(HT):
                a_unit(NC - 1, h)
            a_silu(HT * NC - 1, HT - 1)
            a_move(NC - 1, HT - 2)
            a_move(NC - 1, HT - 1)
            act.wait_ge(kern_ps, 1)
            a.activation(kern_t, ps[0:L, 4, :], ACT.Copy).then_inc(kern_sb, 1)
            for s in range(3):
                act.wait_ge(spec_ps, s + 1)
                a.activation(spec[:, s, :], ps[0:L, 5 + s, :], ACT.Copy).then_inc(spec_set, 1)

            def step(pair, q):
                b, par, half = seq(pair, q, 1)
                if b is not None:
                    act.wait_ge(c_loaded[par], 16 * (half + 1))
                    need(act, cs_set, b - 1)
                    need(act, sq_set, b)
                    a.activation(ctx_sq, ctx_sb[:, par, :], ACT.Square, scale=C ** -0.5, accum_out=cs[par][:, 0:1])\
                     .then_inc(sq_set, 1)
                b, par, half = seq(pair, q, 2)
                if b is not None:
                    act.wait_ge(decay_set, 1)
                    need(act, cross_ps, b - 1)
                    a.activation(decay_b[:, par, :], decay[:, bass.ds(b * L, L)], ACT.Copy).then_inc(decay_kept, 1)
                b, par, half = seq(pair, q, 0)
                if b is not None:
                    act.wait_ge(z_ps, b + 1)
                    need(act, gate_set, b - 1)
                    a.activation(z_act[:, par, :], ps[:, 2, 0:HT * L], ACT.Silu).then_inc(z_set, 1)
                b, par, half = seq(pair, q, 3)
                if b is not None:
                    act.wait_ge(x1t_ps, b + 1)
                    need(act, cross_ps, b - 1)
                    a.activation(x1_t[:, par, :], ps[:, 5, 0:DT * L], ACT.Copy).then_inc(x1t_set, 1)
                b, par, half = seq(pair, q, 4)
                if b is not None:
                    act.wait_ge(x2t_ps, b + 1)
                    need(act, logit_ps, b - 1)
                    a.activation(x2_t[:, par, :], ps[:, 7, 0:DT * L], ACT.Copy).then_inc(x2t_set, 1)
                if isinstance(pair, int) and (pair, q) == (0, 0):
                    act.wait_ge(plug_ready, 2)
                    a.activation(fall, fall, ACT.Exp, scale=-DECAY).then_inc(fall_step, 1)

            b_steps(act, step)

            def f_step(group, q, tiles=TILES):
                i, place, gr = tile_of(group, q, -1, tiles)
                if i is not None:
                    move_rows(i, place)
                i, place, gr = tile_of(group, q, 0, tiles)
                par = place % 2
                if i is not None:
                    e = act.value_load(tile_expert[0:1, bass.ds(i, 1)], min_val=0, max_val=NE - 1)
                    act.wait_ge(ht_ps, i + 1)
                    need(act, f_ps, i - 1)
                    for m in range(FT):
                        last = a.activation(h_t[:, par, m * P:(m + 1) * P],
                                            ps[:, 2 + m // 4, (m % 4) * P:(m % 4 + 1) * P], ACT.Relu,
                                            bias=b1[:, bass.ds(e * FT + m, 1)])
                    last.then_inc(ht_set, 1)

            def move_rows(i, place):
                par = place % 2
                act.wait_ge(rt_ps, i + 1)
                need(act, h_ps, i - 1)
                a.activation(rows_t[:, par, :], ps[:, 6, 0:D], ACT.Copy).then_inc(rt_set, 1)

            act.wait_ge(experts_set, 1)
            move_rows(0, 0)
            f_steps(act, f_step)

        @block.vector
        def _(dve):
            v = nc.vector
            dve.wait_ge(loaded["lens"], 16)
            v.tensor_copy(ends[:, 0, :], lens).then_inc(b_step, 1)
            v.memset(ends[:, 1, :], 1.0).then_inc(b_step, 1)
            dve.wait_ge(b_step, 2)
            v.tensor_tensor_scan(ends[:, 2, :], ends[:, 1, :], ends[:, 0, :], 0.0, ALU.mult, ALU.add)\
             .then_inc(b_step, 1)
            dve.wait_ge(b_step, 3)
            v.tensor_scalar(ends[:, 2, :], ends[:, 2, :], 1.0, None, ALU.subtract).then_inc(b_step, 1)
            dve.wait_ge(b_step, 4)
            v.tensor_scalar(ends[:, 3, :], ends[:, 2, :], 0.0, float(L), ALU.is_lt, ALU.mult).then_inc(b_step, 1)
            dve.wait_ge(b_step, 5)
            v.tensor_tensor(ends[:, 2, :], ends[:, 2, :], ends[:, 3, :], ALU.add).then_inc(b_step, 1)
            dve.wait_ge(ends_ps, 1)
            v.tensor_copy(ends_t, ps[0:PP, 6, 0:PT * NB]).then_inc(ends_sb, 1)
            dve.wait_ge(loaded["consts"], 16)
            dve.wait_ge(k_pool, dt_count[0])
            done = 0

            def phase(ins_):
                nonlocal done
                done += 1
                ins_.then_inc(k_phase, 1)
                dve.wait_ge(k_phase, done)

            phase(v.tensor_tensor(
                theta[:, 0:nm].rearrange("p (h l m) -> p h l m", h=HT, l=NLAG),
                const("lags").unsqueeze(1).unsqueeze(3).to_broadcast([P, HT, NLAG, MODES]),
                km[:, 2, :].rearrange("p (h m) -> p h m", h=HT).unsqueeze(2).to_broadcast([P, HT, NLAG, MODES]),
                ALU.mult))
            phase(v.tensor_scalar(theta[:, nm:2 * nm], theta[:, 0:nm], math.pi / 2, None, ALU.add))
            phase(v.tensor_scalar(turns, theta, 1 / (2 * math.pi), MAGIC, ALU.mult, ALU.add))
            phase(v.tensor_scalar(turns, turns, MAGIC, None, ALU.subtract))
            phase(v.scalar_tensor_tensor(theta, turns, -TWO_PI_HI, theta, ALU.mult, ALU.add))
            phase(v.scalar_tensor_tensor(theta, turns, -TWO_PI_LO, theta, ALU.mult, ALU.add))
            v.tensor_scalar(theta, theta, PI_BELOW, -PI_BELOW, ALU.min, ALU.max).then_inc(k_phase, 1)
            assert done + 1 == K_PHASE

            def a_step(c, h):
                unit = HT * c + h
                par = h % 2
                dve.wait_ge(acc_set, unit + 1)
                acc = conv_acc[:, par, :].rearrange("p (b t) -> p b t", b=CB)
                raw = ps[:, h, 0:CW].rearrange("p (b t) -> p b t", b=CB)
                for back in range(1, TAPS):
                    tap = TAPS - 1 - back
                    ins_ = v.scalar_tensor_tensor(acc[:, :, back:L], raw[:, :, 0:L - back],
                                                  conv_w[:, h, tap:tap + 1], acc[:, :, back:L],
                                                  ALU.mult, ALU.add)
                    if back < TAPS - 1:
                        ins_.then_inc(tap_set, 1)
                        dve.wait_ge(tap_set, (TAPS - 2) * unit + back)
                    else:
                        ins_.then_inc(conv_done, 1)

            dve.wait_ge(loaded["conv"], 32)
            dve.wait_ge(k_pool, recip_count[0])
            v.reciprocal(km[:, 5, :], km[:, 5, :]).then_inc(k_recip, 1)
            v.reciprocal(km[:, 6, :], km[:, 6, :]).then_inc(k_recip, 1)
            for h in range(HT):
                a_step(0, h)
            with dve.Fori(1, NC) as c:
                for h in range(HT):
                    a_step(c, h)
            for n, h in enumerate((0, 3, 1, 2)):
                if h < POOL_K:
                    dve.wait_ge(k_prod_set, h + 1)
                else:
                    dve.wait_ge(k_pool, modes_count[0])
                    k_products(v, h, k_prods[h]).then_inc(k_own, 1)
                    dve.wait_ge(k_own, 1)
                v.tensor_reduce(kern[:, h, :], k_prods[h].rearrange("p (l m) -> p l m", m=2 * MODES), AX_X, ALU.add)\
                 .then_inc(k_sum, 1)
                if n == 1:
                    for c in range(NC):
                        dve.wait_ge(count_ps, c + 1)
                        v.tensor_scalar(plug[:, c * CW:(c + 1) * CW], ps[0:L, 4 + c, 0:CW], 1.0, None, ALU.min)\
                         .then_inc(plug_set, 1)
            dve.wait_ge(k_sum, HT)
            v.tensor_tensor(kern[:, :, 0:1], kern[:, :, 0:1], d_skip.unsqueeze(2), ALU.add).then_inc(k_sum, 1)

            dve.wait_ge(plug_set, NC)
            dve.wait_ge(run_set, 2)
            v.tensor_tensor_scan(plug, run, plug, 0.0, ALU.mult, ALU.add).then_inc(plug_scan, 1)
            dve.wait_ge(plug_scan, 1)
            v.tensor_scalar(plug, plug, -1.0, 0.0, ALU.add, ALU.max).then_inc(plug_ready, 1)
            dve.wait_ge(plug_ready, 1)
            v.tensor_scalar(fall, plug, const("part", L), 0.0, ALU.subtract, ALU.max).then_inc(plug_ready, 1)

            dve.wait_ge(loaded["small"], 16 * 9)
            for k in range(DT):
                v.tensor_scalar(w_x[:, k, :], w_x[:, k, :], g_res[:, k:k + 1], None, ALU.mult).then_inc(b_step, 1)
            v.tensor_scalar(g_init[:, :], g_init[:, :], BCOEF, None, ALU.mult).then_inc(b_step, 1)

            def normalize(o, src, m, rs):
                return v.tensor_scalar(o, src, m, rs, ALU.subtract, ALU.mult)

            def step(pair, q):
                b, par, half = seq(pair, q, 3)
                if b is not None:
                    dve.wait_ge(r1_set, b + 1)
                    need(dve, x1t_ps, b - 1)
                    need(dve, sum1_set, b - 1)
                    normalize(x1[:, par, :], x1_pre, mv[0][par][:, 0:1], nr[0][par][:, 1:2]).then_inc(x1_set, 1)
                b, par, half = seq(pair, q, 0)
                if b is not None:
                    dve.wait_ge(dft_ps, b + 1)
                    dve.wait_ge(spec_set, 3)
                    need(dve, y_set, b)
                    for n, (x_part, k_part) in enumerate(((0, 0), (1, 1), (0, 1), (1, 2))):
                        last = v.tensor_tensor(prod[:, n, :], ps[0:L, x_part, :], spec[:, k_part, :], ALU.mult)
                    last.then_inc(prod_set, 1)
                b, par, half = seq(pair, q, 4)
                if b is not None:
                    dve.wait_ge(r2_set, b + 1)
                    need(dve, x2t_ps, b - 1)
                    need(dve, x2_stored[par], 16 * half)
                    normalize(x2[:, par, :], x2_sum[:, par, :], mv[1][par][:, 0:1], nr[1][par][:, 1:2])\
                        .then_inc(x2_set, 1)
                b, par, half = seq(pair, q, 2)
                if b is not None:
                    dve.wait_ge(cs_set, b + 1)
                    dve.wait_ge(b_step, 6 + DT + 1)
                    need(dve, cross_ps, b - 1)
                    v.scalar_tensor_tensor(u[0:L, par, :], ctx_sb[:, par, 0:D], rr[par][:, 0:1], g_init[:, :],
                                           ALU.mult, ALU.mult).then_inc(u_set, 1)
                b, par, half = seq(pair, q, 1)
                if b is not None:
                    dve.wait_ge(idft_ps, b + 1)
                    dve.wait_ge(z_set, b + 1)
                    need(dve, out_ps, b - 1)
                    v.tensor_tensor(gated[:, par, :], ps[:, 3, 0:HT * L], z_act[:, par, :], ALU.mult)\
                     .then_inc(gate_set, 1)
                b, par, half = seq(pair, q, 2)
                if b is not None:
                    dve.wait_ge(out_ps, b + 1)
                    dve.wait_ge(x_loaded[par], 16 * (half + 1))
                    need(dve, x1_set, b)
                    v.tensor_tensor(x1_pre, ps[0:L, 4, 0:D], x_res[:, par, :], ALU.add).then_inc(pre_set, 1)
                    dve.wait_ge(pre_set, b + 1)
                    v.bn_stats(bn[0], x1_pre).then_inc(bn1_set, 1)
                    apart(dve, (bn1_set, b + 1), (r1_set, b - 1))
                    v.bn_aggr(mv[0][par], bn[0]).then_inc(mv1_set, 1)
                b, par, half = seq(pair, q, 3)
                if b is not None:
                    dve.wait_ge(cross_ps, b + 1)
                    dve.wait_ge(x1_set, b + 1)
                    need(dve, x2_set, b - 1)
                    s2 = x2_sum[:, par, :]
                    v.scalar_tensor_tensor(s2, ps[0:L, 6, 0:D], nr[0][par][:, 3:4], x1[:, par, :],
                                           ALU.mult, ALU.add).then_inc(sum1_set, 1)
                    dve.wait_ge(sum1_set, b + 1)
                    v.tensor_tensor(s2, s2, ps[0:L, 6, D:2 * D], ALU.add).then_inc(sum2_set, 1)
                    dve.wait_ge(sum2_set, b + 1)
                    v.bn_stats(bn[1], s2).then_inc(bn2_set, 1)
                    apart(dve, (bn2_set, b + 1), (r2_set, b - 1))
                    v.bn_aggr(mv[1][par], bn[1]).then_inc(mv2_set, 1)
                b, par, half = seq(pair, q, 4)
                if b is not None:
                    dve.wait_ge(logit_ps, b + 1)
                    v.tensor_tensor(logits[:, bass.ds(b * NE, NE)], ps[0:L, 7, 256:256 + NE], b_r[:, :],
                                    ALU.add).then_inc(logit_set, 1)
                if isinstance(pair, int) and (pair, q) == (0, 1):
                    dve.wait_ge(fall_step, 1)
                    v.scalar_tensor_tensor(plug, plug, const("part", L), fall, ALU.is_ge, ALU.mult)\
                     .then_inc(decay_set, 1)

            b_steps(dve, step)

            done = 0

            def link(ins_):
                nonlocal done
                done += 1
                ins_.then_inc(r_step, 1)
                dve.wait_ge(r_step, done)

            dve.wait_ge(logit_set, NB)
            dve.wait_ge(x2t_set, NB)
            for q in range(2):
                dve.wait_ge(x2_stored[q], 16 * NB // 2)
            be = lambda x, n=L: x[0:n].rearrange("p (b e) -> p b e", b=NB)
            lg = logits[:, :].rearrange("p (b e) -> p b e", b=NB)
            best, key, first = rt[0:L, 0, 0:NB], rt[0:L, 1, :], rt[0:L, 2, 0:NB]
            m8 = const("expert_m8", L)
            link(v.tensor_reduce(best, lg, AX_X, ALU.max))
            link(v.tensor_tensor(be(key), lg, best.unsqueeze(2).to_broadcast([L, NB, NE]), ALU.is_equal))
            link(v.tensor_tensor(key, key, m8, ALU.mult))
            link(v.tensor_reduce(first, be(key), AX_X, ALU.min))
            link(v.tensor_tensor(be(rt[0:L, 3, :]), be(m8), first.unsqueeze(2).to_broadcast([L, NB, NE]),
                                 ALU.is_equal))
            chosen = rt[0:L, 3, :]
            v.tensor_copy(one_hot, chosen).then_inc(one_hot_set, 1)
            dve.wait_ge(rank_ps, 1)
            tot, run_, excl = rt[:, 4, :], rt[:, 5, :], rt[:, 6, :]
            link(v.tensor_copy(tot.rearrange("p (e b) -> p b e", b=NB),
                               ps[:, 1, 0:NB * NE].rearrange("p (b e) -> p b e", b=NB)))
            link(v.tensor_tensor_scan(run_, const("seq_reset"), tot, 0.0, ALU.mult, ALU.add))
            link(v.tensor_tensor(excl, run_, tot, ALU.subtract))
            count = run_.rearrange("p (e b) -> p e b", b=NB)[:, :, NB - 1:NB]
            tn = tile_n.rearrange("p (e j) -> p e j", e=NE)
            link(v.tensor_tensor(tn, count.to_broadcast([P, NE, TPE]),
                                 const("tile_from").rearrange("p (e j) -> p e j", e=NE), ALU.is_gt))
            link(v.tensor_reduce(per_e[:, 0, :], tn, AX_X, ALU.add))
            link(v.memset(per_e[:, 1, :], 1.0))
            link(v.tensor_tensor_scan(per_e[:, 2, :], per_e[:, 1, :], per_e[:, 0, :], 0.0, ALU.mult, ALU.add))
            link(v.tensor_tensor(per_e[:, 3, :], per_e[:, 2, :], per_e[:, 0, :], ALU.subtract))
            link(v.scalar_tensor_tensor(
                rt[0:L, 7, :].rearrange("p (b e) -> p e b", b=NB),
                per_e[0:L, 3, :].unsqueeze(2).to_broadcast([L, NE, NB]), float(P),
                excl[0:L].rearrange("p (e b) -> p e b", b=NB), ALU.mult, ALU.add))
            link(v.tensor_tensor(rt[0:L, 7, :], rt[0:L, 7, :], ps[0:L, 0, 0:NB * NE], ALU.add))
            link(v.tensor_tensor(rt[0:L, 7, :], rt[0:L, 7, :], chosen, ALU.mult))
            link(v.tensor_reduce(slot_f, be(rt[:, 7, :]), AX_X, ALU.add))
            link(v.tensor_scalar(slot_tile, slot_f, 1 / P, 0.5 / P - 0.5, ALU.mult, ALU.add))
            link(v.tensor_scalar(slot_tile, slot_tile, MAGIC, MAGIC, ALU.add, ALU.subtract))
            v.tensor_tensor(in_tile, slot_tile.unsqueeze(2).to_broadcast([L, NB, TILES]),
                            const("iota", L)[:, 0:TILES].unsqueeze(1).to_broadcast([L, NB, TILES]), ALU.is_equal)\
             .then_inc(in_tile_set, 1)
            link(v.scalar_tensor_tensor(slot_part, slot_tile, -float(P), slot_f, ALU.mult, ALU.add))
            for b in range(NB):
                v.tensor_scalar(in_place[:, b, :], const("iota", L), slot_part[:, b:b + 1], None, ALU.is_equal)\
                 .then_inc(place_set, 1)
            link(v.tensor_tensor(tile_hits.rearrange("p (i e) -> p i e", e=NE),
                                 const("tile_no").rearrange("p (i e) -> p i e", e=NE),
                                 per_e[:, 2, :].unsqueeze(1).to_broadcast([P, TILES, NE]), ALU.is_ge))
            link(v.tensor_reduce(tile_e[:, 0, 0:TILES], tile_hits.rearrange("p (i e) -> p i e", e=NE), AX_X, ALU.add))
            v.tensor_copy(tile_e[:, 1, TILES:TILES + 1], per_e[:, 2, NE - 1:NE])
            link(v.tensor_scalar(tile_e[:, 1, 0:TILES], tile_e[:, 0, 0:TILES], float(NE - 1), None, ALU.min))
            v.tensor_copy(tile_expert, tile_e[:, 1, :]).then_inc(experts_set, 1)
            dve.wait_ge(token_ps, 1)
            v.tensor_scalar(token_f, ps[:, 2, 0:TILES], float(L), float(T), ALU.mult, ALU.add).then_inc(token_step, 1)
            dve.wait_ge(token_step, 1)
            v.tensor_tensor(token_of, token_f, ps[:, 2, TILES:2 * TILES], ALU.add).then_inc(token_set, 1)
            dve.wait_ge(experts_set, 1)
            dve.wait_ge(loaded["b2"], 16)

            def f_step(group, q, tiles=TILES):
                i, place, gr = tile_of(group, q, 2, tiles)
                par = place % 2
                if i is not None:
                    dve.wait_ge(fr_set, i + 1)
                    before, b_place, b_gr = tile_of(group, q, 4, tiles)
                    need(dve, rows_out[b_place], 16 * (b_gr + 1) if before is not None else 0)
                    normalize(y_row[:, par, :], y_sum[:, par, :], f_mv[:, par, 0:1], f_nr[:, par, 1:2])\
                        .then_inc(y_done, 1)
                i, place, gr = tile_of(group, q, 0, tiles)
                if i is not None:
                    dve.wait_ge(h_ps, i + 1)
                    need(dve, ht_ps, i)
                    v.tensor_copy(h_sb.rearrange("p (n f) -> p n f", n=2), ps[:, 0:2, :]).then_inc(h_set, 1)
                i, place, gr = tile_of(group, q, 1, tiles)
                par = place % 2
                if i is not None:
                    e = dve.value_load(tile_expert[0:1, bass.ds(i, 1)], min_val=0, max_val=NE - 1)
                    dve.wait_ge(f_ps, i + 1)
                    need(dve, y_done, i - 1)
                    v.tensor_tensor(y_sum[:, par, :], ps[:, 4 + par, 0:D], b2[:, e, :], ALU.add).then_inc(fb_set, 1)
                    dve.wait_ge(fb_set, i + 1)
                    dve.wait_ge(rows_loaded[place], 16 * (gr + 1))
                    v.tensor_tensor(y_sum[:, par, :], y_sum[:, par, :], rows[:, place, 0:D], ALU.add)\
                     .then_inc(fs_set, 1)
                    dve.wait_ge(fs_set, i + 1)
                    v.bn_stats(f_bn, y_sum[:, par, :]).then_inc(fbn_set, 1)
                    apart(dve, (fbn_set, i + 1), (fr_set, i - 1))
                    v.bn_aggr(f_mv[:, par, :], f_bn).then_inc(fmv_set, 1)

            f_steps(dve, f_step)

        @block.tensor
        def _(pe):
            m = nc.tensor
            pe.wait_ge(loaded["consts"], 16)
            pe.wait_ge(b_step, 6)
            for k in range(PT):
                last = m.transpose(ps[0:PP, 6, k * NB:(k + 1) * NB], ends[:, 2, k * PP:(k + 1) * PP],
                                   ident[0:NB, 0:NB])
            last.then_inc(ends_ps, 1)

            def a_in(c, h):
                unit = HT * c + h
                need(pe, conv_done, unit - HT + 1)
                for k in range(DT):
                    last_ = m.matmul(ps[:, h, 0:CW], w_in[:, k, h * P:(h + 1) * P],
                                     hid_t[:, k, bass.ds(c * CW, CW)], start=(k == 0), stop=(k == DT - 1))
                last_.then_inc(in_ps, 1)

            def a_turn(unit, h):
                pe.wait_ge(act_x, unit + 1)
                need(pe, xt_set, unit - 1)
                for b in range(CB):
                    last_ = m.transpose(ps[0:L, 4 + h % 2, b * P:(b + 1) * P],
                                        conv_x[:, h % 2, b * L:(b + 1) * L], ident)
                last_.then_inc(xt_ps, 1)

            def a_unit(c, h):
                a_in(c, h)
                if not (isinstance(c, int) and c == 0 and h < 2):
                    a_turn(HT * c + h - 2, (h - 2) % HT)

            pe.wait_ge(loaded["w_in_x"], 16)
            pe.wait_ge(hid_loaded[0], 16)
            for h in range(HT):
                a_unit(0, h)
            for c in range(1, NC):
                pe.wait_ge(hid_loaded[c], 16)
            with pe.Fori(1, NC) as c:
                for h in range(HT):
                    a_unit(c, h)
            a_turn(HT * NC - 2, HT - 2)
            a_turn(HT * NC - 1, HT - 1)
            pe.wait_ge(xt_set, HT * NC)
            pe.wait_ge(hits_set, PT)
            pe.wait_ge(ones_set, 1)
            for c in range(NC):
                for k in range(PT):
                    last = m.matmul(ps[0:L, 4 + c, 0:CW], ones16[0:PP, 0:L], hits[:, k, c * CW:(c + 1) * CW],
                                    start=(k == 0), stop=(k == PT - 1))
                last.then_inc(count_ps, 1)
            def spectrum_and_z(pair, q):
                b, par, half = seq(pair, q, 0)
                if b is not None:
                    need(pe, prod_set, b)
                    m.matmul(ps[0:L, 0, :], const("f_re", L), x_time[:, b, :], start=True, stop=True)
                    m.matmul(ps[0:L, 1, :], const("f_im", L), x_time[:, b, :], start=True, stop=True)\
                     .then_inc(dft_ps, 1)
                b, par, half = seq(pair, q, 0)
                if b is not None:
                    need(pe, z_set, b)
                    for h in range(HT):
                        for k in range(DT):
                            last_ = m.matmul(ps[:, 2, h * L:(h + 1) * L], w_in[:, k, H + h * P:H + (h + 1) * P],
                                             hid_t[:, k, bass.ds(b * L, L)], start=(k == 0), stop=(k == DT - 1))
                    last_.then_inc(z_ps, 1)

            pe.wait_ge(loaded["w_in_z"], 16)
            spectrum_and_z(0, 0)
            pe.wait_ge(k_sum, HT + 1)
            pe.wait_ge(plug_set, NC)
            for h in range(HT):
                last = m.transpose(ps[0:L, 4, h * P:(h + 1) * P], kern[:, h, :], ident)
            last.then_inc(kern_ps, 1)
            pe.wait_ge(kern_sb, 1)
            for s, name in enumerate(("f_re", "f_im0", "f_d")):
                m.matmul(ps[0:L, 5 + s, :], const(name, L), kern_t, start=True, stop=True).then_inc(spec_ps, 1)
            pe.wait_ge(loaded["w_out"], 16)
            pe.wait_ge(loaded["small"], 16 * 9)
            pe.wait_ge(spec_set, 3)

            def step(pair, q):
                if not (isinstance(pair, int) and (pair, q) == (0, 0)):
                    spectrum_and_z(pair, q)
                b, par, half = seq(pair, q, 1)
                if b is not None:
                    pe.wait_ge(y_set, b + 1)
                    need(pe, gate_set, b)
                    for h in range(HT):
                        for s, name in enumerate(("g_re", "g_im")):
                            last_ = m.matmul(ps[:, 3, h * L:(h + 1) * L], y_spec[:, s, h * P:(h + 1) * P],
                                             const(name, L), start=(s == 0), stop=(s == 1))
                    last_.then_inc(idft_ps, 1)
                b, par, half = seq(pair, q, 3)
                if b is not None:
                    pe.wait_ge(x1_set, b + 1)
                    need(pe, x1t_set, b)
                    for k in range(DT):
                        last_ = m.transpose(ps[:, 5, k * L:(k + 1) * L], x1[:, par, k * P:(k + 1) * P],
                                            ident[0:L, 0:L])
                    last_.then_inc(x1t_ps, 1)
                b, par, half = seq(pair, q, 2)
                if b is not None:
                    pe.wait_ge(gate_set, b + 1)
                    need(pe, pre_set, b)
                    for h in range(HT):
                        last_ = m.matmul(ps[0:L, 4, 0:D], gated[:, par, h * L:(h + 1) * L], w_out[:, h, :],
                                         start=(h == 0), stop=(h == HT - 1))
                    last_.then_inc(out_ps, 1)
                b, par, half = seq(pair, q, 4)
                if b is not None:
                    pe.wait_ge(x2_set, b + 1)
                    need(pe, x2t_set, b)
                    need(pe, logit_set, b)
                    for k in range(DT):
                        last_ = m.transpose(ps[:, 7, k * L:(k + 1) * L], x2[:, par, k * P:(k + 1) * P],
                                            ident[0:L, 0:L])
                    last_.then_inc(x2t_ps, 1)
                b, par, half = seq(pair, q, 3)
                if b is not None:
                    pe.wait_ge(x1t_set, b + 1)
                    pe.wait_ge(b_step, 6 + DT + 1)
                    need(pe, sum2_set, b)
                    for k in range(DT):
                        m.matmul(ps[0:L, 6, 0:D], x1_t[:, par, k * L:(k + 1) * L], w_x[:, k, :],
                                 start=(k == 0), stop=(k == DT - 1))
                    pe.wait_ge(u_set, b + 1)
                    pe.wait_ge(decay_kept, b + 1)
                    m.matmul(ps[0:L, 6, D:2 * D], decay_b[:, par, :], u[:, par, :], start=True, stop=True)\
                     .then_inc(cross_ps, 1)
                b, par, half = seq(pair, q, 4)
                if b is not None:
                    pe.wait_ge(x2t_set, b + 1)
                    for k in range(DT):
                        last_ = m.matmul(ps[0:L, 7, 256:256 + NE], x2_t[:, par, k * L:(k + 1) * L], w_r[:, k, :],
                                         start=(k == 0), stop=(k == DT - 1))
                    last_.then_inc(logit_ps, 1)

            b_steps(pe, step)

            pe.wait_ge(one_hot_set, 1)
            pe.wait_ge(tri_set, 1)
            m.matmul(ps[0:L, 0, 0:NB * NE], tri16[:, :], one_hot, start=True, stop=True)
            m.matmul(ps[:, 1, 0:NB * NE], ones16[0:L, :], one_hot, start=True, stop=True).then_inc(rank_ps, 1)
            pe.wait_ge(parts_set, 1)
            for b in range(NB):
                pe.wait_ge(place_set, b + 1)
                last = m.matmul(ps[:, 2, 0:2 * TILES], in_place[:, b, :],
                                token_parts[:, b, :, :].rearrange("p s i -> p (s i)"), start=(b == 0),
                                stop=(b == NB - 1))
            last.then_inc(token_ps, 1)

            def turn_rows(i, place, gr):
                pe.wait_ge(rows_loaded[place], 16 * (gr + 1))
                need(pe, rt_set, i)
                for k in range(DT):
                    last_ = m.transpose(ps[:, 6, k * P:(k + 1) * P], rows[:, place, k * P:(k + 1) * P], ident)
                last_.then_inc(rt_ps, 1)

            def f_step(group, q, tiles=TILES):
                i, place, gr = tile_of(group, q, 0, tiles)
                if i is not None:
                    par = place % 2
                    e = pe.value_load(tile_expert[0:1, bass.ds(i, 1)], min_val=0, max_val=NE - 1)
                    pe.wait_ge(rt_set, i + 1)
                    need(pe, h_set, i)
                    for n in range(2):
                        for k in range(DT):
                            last_ = m.matmul(ps[:, n, :], rows_t[:, par, k * P:(k + 1) * P],
                                             w1[:, e, k, n * 512:(n + 1) * 512], start=(k == 0), stop=(k == DT - 1))
                    last_.then_inc(h_ps, 1)
                i, place, gr = tile_of(group, q, -1, tiles)
                if i is not None:
                    turn_rows(i, place, gr)
                i, place, gr = tile_of(group, q, 1, tiles)
                if i is not None:
                    par = place % 2
                    e = pe.value_load(tile_expert[0:1, bass.ds(i, 1)], min_val=0, max_val=NE - 1)
                    pe.wait_ge(ht_set, i + 1)
                    need(pe, fb_set, i - 1)
                    for f in range(FT):
                        last_ = m.matmul(ps[:, 4 + par, 0:D], h_t[:, par, f * P:(f + 1) * P], w2[:, e, f, :],
                                         start=(f == 0), stop=(f == FT - 1))
                    last_.then_inc(f_ps, 1)
                i, place, gr = tile_of(group, q, 0, tiles)
                if i is not None:
                    pe.wait_ge(h_set, i + 1)
                    need(pe, ht_set, i)
                    for f in range(FT):
                        last_ = m.transpose(ps[:, 2 + f // 4, (f % 4) * P:(f % 4 + 1) * P],
                                            h_sb[:, f * P:(f + 1) * P], ident)
                    last_.then_inc(ht_ps, 1)

            pe.wait_ge(experts_set, 1)
            turn_rows(0, 0, 0)
            pe.wait_ge(loaded["w1"], 16 * NB)
            pe.wait_ge(loaded["w2"], 16 * (NB + NE // 2))
            f_steps(pe, f_step)


def kernel(**inputs):
    import numpy as _np
    import concourse.bacc as _bacc
    from concourse import mybir as _mybir
    from concourse.bass_utils import run_bass_kernel_spmd as _run

    a = {k.removeprefix("L0_"): _np.asarray(v) for k, v in inputs.items()}

    def rows(x, tiles):
        return x.reshape(tiles, P, *x.shape[1:]).swapaxes(0, 1)

    _, table = constant_columns()
    laid = {
        "consts": table,
        "lens": a["mask_BxS2_if0"],
        "x": a["x"],
        "x_t": rows(a["x"].reshape(T, D).T, DT),
        "ctx": a["ctx_2048"][:, :L, :],
        "w_in": rows(a["attn_W_in"].T, DT),
        "conv_w": rows(a["attn_conv_w"], HT),
        "conv_b": rows(a["attn_conv_b"], HT),
        "log_dt": rows(a["attn_log_dt"], HT),
        "d_skip": rows(a["attn_D"], HT),
        "ssm": _np.stack([rows(a["attn_" + n], HT).reshape(P, HT * MODES)
                          for n in ("log_A_real", "A_imag", "C_re", "C_im")], axis=1),
        "w_out": rows(a["attn_W_out"].T, HT),
        "w_x": rows(a["xattn_W_in"].T, DT),
        "b_x": a["xattn_b_in"].reshape(1, D),
        "one_row": _np.ones((1, T), _np.float32),
        "g_res": rows(a["xattn_g_res"], DT),
        "g_init": a["xattn_g_init"][:D].reshape(1, D),
        "w_r": rows(a["ffn_Wr"].T, DT),
        "b_r": a["ffn_br"].reshape(1, NE),
        "w1": a["ffn_W1"].transpose(0, 2, 1).reshape(NE, DT, P, FF).transpose(2, 0, 1, 3),
        "b1": a["ffn_b1"].reshape(NE, FT, P).transpose(2, 0, 1).reshape(P, NE * FT),
        "w2": a["ffn_W2"].transpose(0, 2, 1).reshape(NE, FT, P, D).transpose(2, 0, 1, 3),
        "b2": a["ffn_b2"].reshape(1, NE * D),
    }
    nc = _bacc.Bacc("TRN2", target_bir_lowering=False, num_devices=1)
    arrays, ins = {}, {}
    for name, x in laid.items():
        x = _np.ascontiguousarray(x)
        arrays[f"in_{name}"] = x
        ins[name] = nc.dram_tensor(f"in_{name}", x.shape, _mybir.dt.from_np(x.dtype), kind="ExternalInput").ap()
    out = nc.dram_tensor("out_0", (T, D), F32, kind="ExternalOutput").ap()
    decoder_layer(nc, ins, out)
    r = _run(nc, [arrays], core_ids=[0])
    return r.results[0]["out_0"].reshape(NB, L, D)
```

```python
from contextlib import ExitStack
import math

import numpy as np
import concourse.bass as bass
from concourse import mybir

F32 = mybir.dt.float32
BF16 = mybir.dt.bfloat16
I32 = mybir.dt.int32
ALU = mybir.AluOpType
ACT = mybir.ActivationFunctionType
AX_X = mybir.AxisListType.X

NB, L, D = 16, 112, 256
H, MODES, TAPS = 512, 8, 4
C, PATCHES = 512, 375
NE, FF = 8, 1024
T = NB * L
P = 128
HT = H // P
DT = D // P
FT = FF // P
NC = 4
CB = NB // NC
CW = CB * L
NFFT = 2 * L
PT, PP = 3, 125
LO, LA = 16, L // 16
TILES = (T - NE) // P + NE
TPE = -(-T // P)

EPS = 1e-5
LOGP = -0.001
DECAY = -math.log(-math.expm1(LOGP))
BCOEF = math.exp(LOGP)
MAGIC = 1.5 * 2.0 ** 23
TWO_PI_HI = 6.28125
TWO_PI_LO = 2 * math.pi - TWO_PI_HI
PI_BELOW = 3.1415925
PAST = 1.0e4


def constant_columns():
    t = np.arange(L)
    parts = {}

    def put(name, a):
        full = np.zeros((P, a.shape[1]), np.float32)
        full[:a.shape[0]] = a
        parts[name] = full

    put("ident", np.eye(P))
    put("iota", np.tile(np.arange(P), (P, 1)))
    put("part", np.arange(P)[:, None])
    lags = list(LO * np.arange(LA)) + list(range(LO)) + [0.5]
    put("lags", np.tile(np.array(lags), (P, 1)))
    put("m_half", np.full((P, 1), -0.5))
    put("eps", np.full((P, 1), EPS))
    angle = 2 * np.pi * np.outer(t, t) / NFFT
    cos, sin = np.cos(angle), np.sin(angle)
    nyquist = (-1.0) ** t
    zero0 = (t > 0).astype(float)
    put("f_re", cos)
    f_im = -sin
    f_im[:, 0] = nyquist
    put("f_im", f_im)
    put("f_im0", -sin * zero0)
    f_d = cos.copy()
    f_d[:, 0] = nyquist
    put("f_d", f_d)
    g_re = 2 * cos / NFFT
    g_re[0] = 1.0 / NFFT
    put("g_re", g_re)
    g_im = -2 * sin / NFFT
    g_im[0] = nyquist / NFFT
    put("g_im", g_im)
    put("earlier", (t[:, None] < t[None, :]).astype(float))
    put("seq_first_mT", np.tile(np.arange(NB) * L - T, (P, 1)))
    put("expert_m8", np.tile(np.arange(NE) - NE, (P, NB)))
    not_first = np.ones((NE, NB))
    not_first[:, 0] = 0
    put("seq_reset", np.tile(not_first.ravel(), (P, 1)))
    put("tile_from", np.tile(P * np.arange(TPE), (P, NE)))
    put("tile_no", np.tile(np.arange(TILES).repeat(NE), (P, 1)))
    at, n = {}, 0
    for name, a in parts.items():
        at[name] = (n, n + a.shape[1])
        n += a.shape[1]
    return at, np.concatenate(list(parts.values()), axis=1)


def need(engine, semaphore, value):
    if not (isinstance(value, int) and value <= 0):
        engine.wait_ge(semaphore, value)


def decoder_layer(nc, ins, out):
    at, _ = constant_columns()
    n_const = max(b for _, b in at.values())
    NLAG = LA + LO + 1

    with ExitStack() as ctx:
        def sb(name, shape, dt=F32):
            return ctx.enter_context(nc.sbuf_tensor(name, shape, dt))

        def sem(name):
            return ctx.enter_context(nc.semaphore(name))

        x2_rows = nc.dram_tensor("x2_rows", (T + 1, D), F32, kind="Internal").ap()
        ps = ctx.enter_context(nc.psum_tensor("ps", [P, 8, 512], F32))

        class Region:

            def __init__(self, tensor, words):
                self.tensor, self.words, self.used = tensor, words, 0

            def cut(self, words, rows=P):
                self.used += words
                assert self.used <= self.words, (self.used, self.words)
                return self.tensor[0:rows, self.used - words:self.used]

        consts = sb("consts", [P, n_const])
        n_early = at["eps"][1]

        def const(name, rows=P):
            a, b = at[name]
            return consts[0:rows, a:b]

        ident = const("ident")
        ones16 = sb("ones16", [P, P], BF16)
        tri16 = sb("tri16", [L, L], BF16)
        iota16 = sb("iota16", [L, P], BF16)
        w_x = sb("w_x", [P, DT, D])
        g_res = sb("g_res", [P, DT])
        w_r = sb("w_r", [P, DT, NE])
        b_r = sb("b_r", [L, NE])
        g_init = sb("g_init", [L, D])
        b1 = sb("b1", [P, NE * FT])
        logits = sb("logits", [L, NB * NE])

        w1_flat = sb("w1", [P, NE * DT * FF])
        w1 = w1_flat[:, :].rearrange("p (e k f) -> p e k f", e=NE, k=DT)
        r = Region(w1_flat, NE * DT * FF)
        nm = HT * NLAG * MODES
        theta = r.cut(2 * nm)
        turns = r.cut(2 * nm)
        mag = r.cut(nm)
        n_prod = LA * LO * 2 * MODES
        k_prods = [w1_flat[:, 0:n_prod], w1_flat[:, n_prod:2 * n_prod], r.cut(n_prod)]
        assert 2 * n_prod <= 5 * nm
        k_tmp = r.cut(HT * LA * MODES).rearrange("p (h a m) -> p h a m", h=HT, a=LA)
        modes_a = r.cut(HT * LA * 2 * MODES).rearrange("p (h a m) -> p h a m", h=HT, a=LA)
        modes_c = r.cut(HT * LO * 2 * MODES).rearrange("p (h c m) -> p h c m", h=HT, c=LO)
        cplx = r.cut(HT * LA * MODES * 2).rearrange("p (s h a m) -> p s h a m", s=2, h=HT, a=LA)
        kern = r.cut(HT * L).rearrange("p (h l) -> p h l", h=HT)
        kern_t = r.cut(H, L)
        log_dt, dt, d_skip = r.cut(HT), r.cut(HT), r.cut(HT)
        ssm = r.cut(4 * HT * MODES).rearrange("p (s m) -> p s m", s=4)
        km = r.cut(24 * HT * MODES).rearrange("p (s m) -> p s m", s=24)
        conv_w = r.cut(HT * TAPS).rearrange("p (h w) -> p h w", h=HT)
        conv_b = r.cut(HT)
        conv_acc = r.cut(2 * CW).rearrange("p (r n) -> p r n", r=2)
        conv_x = r.cut(2 * CW).rearrange("p (r n) -> p r n", r=2)
        n_hits = PT * T // 2
        hits_at = r.used
        hits = r.cut(n_hits, PP).bitcast(BF16).rearrange("p (k n) -> p k n", k=PT)
        lens = w1_flat[0:NB, hits_at:hits_at + PATCHES].bitcast(I32)
        ends = w1_flat[0:NB, hits_at + PATCHES:hits_at + 5 * PATCHES].rearrange("b (s n) -> b s n", s=4)
        assert 5 * PATCHES <= n_hits and hits_at >= 3 * DT * FF
        ends_t = r.cut(PT * NB, PP)
        far = k_prods[2][0:PP, 0:T]
        pad_row = r.cut(D, 1)
        assert r.used >= 3 * DT * FF
        k_prods.append(r.cut(n_prod))
        fall = k_prods[3][0:L, 0:T]
        dt_count, recip_count, mag_count = [], [], []

        w2_flat = sb("w2", [P, NE * FT * D])
        w2 = w2_flat[:, :].rearrange("p (e m d) -> p e m d", e=NE, m=FT)
        r = Region(w2_flat, NE * FT * D)
        x_time = r.cut(NB * H, L).rearrange("p (b h) -> p b h", b=NB)
        hid_t = r.cut(DT * T).rearrange("p (k t) -> p k t", k=DT)
        w_in = r.cut(DT * 2 * H).rearrange("p (k h) -> p k h", k=DT)
        w_out = r.cut(HT * D).rearrange("p (k d) -> p k d", k=HT)
        spec = r.cut(3 * H, L).rearrange("p (s h) -> p s h", s=3)

        shared = sb("shared", [P, 2048])
        plug = shared[0:L, 0:T]
        decay = shared[0:L + 1, 0:T]
        b2 = shared[:, :].rearrange("p (e d) -> p e d", e=NE)

        N_B = 10176
        stage_b = sb("stage_b", [P, N_B])
        r = Region(stage_b, N_B)

        def two(words, rows=P):
            return r.cut(2 * words, rows).rearrange("p (r n) -> p r n", r=2)

        prod = r.cut(4 * H, L).rearrange("p (s h) -> p s h", s=4)
        y_spec = r.cut(2 * H, L).rearrange("p (s h) -> p s h", s=2)
        z_act, gated = two(HT * L), two(HT * L)
        x_res, x1, x2_sum, x2, ctx_sb = two(D, L), two(D, L), two(D, L), two(D, L), two(C, L)
        late = r.used
        x1_pre = r.cut(D, L)
        x1_t, x2_t = two(DT * L), two(DT * L)
        u = two(D, L + 1)
        decay_b = two(L, L + 1)
        ctx_sq = r.cut(C // 2, L).bitcast(BF16)
        small_b = r.cut(80, L)
        bn = [small_b[:, 0:6], small_b[:, 6:12]]
        mv = [[small_b[:, 12 + 4 * n + 2 * q:14 + 4 * n + 2 * q] for q in range(2)] for n in range(2)]
        nr = [[small_b[:, 20 + 8 * n + 4 * q:24 + 8 * n + 4 * q] for q in range(2)] for n in range(2)]
        cs = [small_b[:, 36 + 4 * q:40 + 4 * q] for q in range(2)]
        rr = [small_b[:, 44 + 4 * q:48 + 4 * q] for q in range(2)]
        r = Region(stage_b, N_B)
        run = stage_b[0:L, late:late + T]
        r = Region(stage_b, N_B)
        h_t = two(FF)
        rows_t = two(D)
        y_sum, y_row = two(D), two(D)
        rows = r.cut(4 * D).rearrange("p (r n) -> p r n", r=4)
        w1_now_at = [r.used]
        r.cut(DT * FF)
        w1_now_at.append(r.used)
        rt = r.cut(9 * NB * NE).rearrange("p (s n) -> p s n", s=9)
        one_hot = r.cut(NB * NE // 2, L).bitcast(BF16)
        in_place = r.cut(NB * P // 2, L).bitcast(BF16).rearrange("p (b n) -> p b n", b=NB)
        assert r.used - w1_now_at[1] >= DT * FF
        w1_now = [stage_b[:, at:at + DT * FF].rearrange("p (k f) -> p k f", k=DT) for at in w1_now_at]
        tile_n = r.cut(NE * TPE)
        per_e = r.cut(4 * NE).rearrange("p (s e) -> p s e", s=4)
        tile_hits = r.cut(TILES * NE)
        tile_e = r.cut(2 * (TILES + 1)).rearrange("p (s n) -> p s n", s=2)
        tile_expert = r.cut(TILES + 1).bitcast(I32)
        slot_f = r.cut(NB, L)
        slot_part, slot_tile = r.cut(NB, L), r.cut(NB, L)
        in_tile = r.cut(NB * TILES, L).rearrange("p (b i) -> p b i", b=NB)
        token_parts = r.cut(NB * TILES, L).bitcast(BF16).rearrange("p (b s i) -> p b s i", b=NB, s=2)
        token_of = r.cut(TILES).bitcast(I32)
        f_bn, f_mv, f_nr = r.cut(6), two(2), two(2)
        f_index = two(1).bitcast(I32)
        g_index = r.cut(4).bitcast(I32).rearrange("p (r n) -> p r n", r=4)

        loaded = {k: sem("loaded_" + k) for k in (
            "consts_early", "consts", "ssm", "w_in_x", "w_in_z", "conv", "w_out", "lens", "small", "b2", "w1", "w2", "pad")}
        hid_loaded = [sem(f"hid_loaded{c}") for c in range(NC)]
        far_set = sem("far_set")
        ones_set, tri_set = sem("ones_set"), sem("tri_set")
        b_step, ends_ps, ends_sb, hits_set, count_ps = (
            sem(s) for s in ("b_step", "ends_ps", "ends_sb", "hits_set", "count_ps"))
        run_set, plug_set, plug_scan, plug_ready, fall_step, decay_set, decay_kept = (
            sem(s) for s in ("run_set", "plug_set", "plug_scan", "plug_ready", "fall_step", "decay_set",
                             "decay_kept"))
        k_exp, k_pool, k_phase, k_recip, k_sin, k_prod_set, k_sum = (
            sem(s) for s in ("k_exp", "k_pool", "k_phase", "k_recip", "k_sin", "k_prod_set", "k_sum"))
        kern_ps, kern_sb, spec_ps, spec_set = (sem(s) for s in ("kern_ps", "kern_sb", "spec_ps", "spec_set"))
        in_ps, acc_set, tap_set, conv_done, act_x, xt_ps, xt_set = (
            sem(s) for s in ("in_ps", "acc_set", "tap_set", "conv_done", "act_x", "xt_ps", "xt_set"))
        dft_ps, prod_set, y_set, z_ps, z_set, idft_ps, gate_set, out_ps = (
            sem(s) for s in ("dft_ps", "prod_set", "y_set", "z_ps", "z_set", "idft_ps", "gate_set", "out_ps"))
        x_loaded = [sem(f"x_loaded{q}") for q in range(2)]
        c_loaded = [sem(f"c_loaded{q}") for q in range(2)]
        pre_set, bn1_set, mv1_set, nr1_step, r1_set, x1_set = (
            sem(s) for s in ("pre_set", "bn1_set", "mv1_set", "nr1_step", "r1_set", "x1_set"))
        sq_set, cs_step, cs_set, u_set = (sem(s) for s in ("sq_set", "cs_step", "cs_set", "u_set"))
        x1t_ps, x1t_set, cross_ps, sum1_set, sum2_set = (
            sem(s) for s in ("x1t_ps", "x1t_set", "cross_ps", "sum1_set", "sum2_set"))
        bn2_set, mv2_set, nr2_step, r2_set, x2_set = (
            sem(s) for s in ("bn2_set", "mv2_set", "nr2_step", "r2_set", "x2_set"))
        x2_stored = [sem(f"x2_stored{q}") for q in range(2)]
        x2t_ps, x2t_set, logit_ps, logit_set = (
            sem(s) for s in ("x2t_ps", "x2t_set", "logit_ps", "logit_set"))
        r_step, one_hot_set, rank_ps, experts_set, pad_set = (
            sem(s) for s in ("r_step", "one_hot_set", "rank_ps", "experts_set", "pad_set"))
        place_set, in_tile_set, parts_set, token_ps, token_set = (
            sem(s) for s in ("place_set", "in_tile_set", "parts_set", "token_ps", "token_set"))
        rows_loaded = [sem(f"rows_loaded{q}") for q in range(4)]
        rows_out = [sem(f"rows_out{q}") for q in range(4)]
        rt_ps, rt_set, w1_now_set, ht_ps, ht_set, f_ps = (
            sem(s) for s in ("rt_ps", "rt_set", "w1_now_set", "ht_ps", "ht_set", "f_ps"))
        fb_set, fs_set, fbn_set, fmv_set, fn_step, fr_set, y_done = (
            sem(s) for s in ("fb_set", "fs_set", "fbn_set", "fmv_set", "fn_step", "fr_set", "y_done"))
        index_set, g_index_set = sem("index_set"), sem("g_index_set")

        PRO, EPI = 6, 4
        F_PRO, F_UNROLL = 4, 4
        F_AHEAD = 3

        def b_steps(engine, step):
            for s in range(PRO):
                step(s // 2, s % 2)
            with engine.Fori(PRO // 2, NB // 2) as pair:
                for q in range(2):
                    step(pair, q)
            for s in range(NB, NB + EPI):
                step(s // 2, s % 2)

        def seq(pair, q, lag):
            par, half = (q - lag) % 2, pair + (q - lag) // 2
            b = 2 * half + par
            if isinstance(b, int) and not 0 <= b < NB:
                return None, par, half
            return b, par, half

        def f_steps(engine, step, finish=None):
            groups = (TPE + 2 - F_PRO) // F_UNROLL
            for s in range(F_PRO):
                step(s // F_UNROLL, s % F_UNROLL)
            with engine.Fori(1, 1 + groups) as group:
                for q in range(F_UNROLL):
                    step(group, q)
            used = engine.value_load(tile_expert[0:1, TILES:TILES + 1], min_val=TPE, max_val=TILES)

            def last_steps(s):
                def end(tiles):
                    for n in range(s, tiles + 2):
                        step(n // F_UNROLL, n % F_UNROLL, tiles)
                    if finish:
                        finish(tiles)

                if s == TILES:
                    end(TILES)
                    return
                with engine.If(used > s):
                    step(s // F_UNROLL, s % F_UNROLL)
                    last_steps(s + 1)
                with engine.Else():
                    end(s)

            last_steps(F_UNROLL * (1 + groups))

        def tile_of(group, q, lag, tiles):
            place, g = (q - lag) % F_UNROLL, group + (q - lag) // F_UNROLL
            i = F_UNROLL * g + place
            if isinstance(i, int) and not 0 <= i < tiles:
                return None, place, g
            return i, place, g

        def apart(engine, *waits):
            waits = [(s, v if isinstance(v, int) else engine.snap(v)) for s, v in waits]
            if not all(isinstance(v, int) for _, v in waits):
                engine.wait_ge(loaded["consts"], 16)
            for s, v in waits:
                need(engine, s, v)

        K_PHASE = 7

        block = ctx.enter_context(nc.Block())

        @block.sync
        def _(sp):
            sp.dma_start(lens, ins["lens"]).then_inc(loaded["lens"], 16)
            sp.dma_start(consts[:, 0:n_early], ins["consts"][:, 0:n_early]).then_inc(loaded["consts_early"], 16)
            sp.dma_start(w_in[:, :, 0:H], ins["w_in"][:, :, 0:H]).then_inc(loaded["w_in_x"], 16)

            def load_hid(c):
                sp.dma_start(hid_t[:, :, c * CW:(c + 1) * CW], ins["x_t"][:, :, c * CW:(c + 1) * CW])\
                  .then_inc(hid_loaded[c], 16)

            load_hid(0)
            for dst, name in ((conv_w, "conv_w"), (conv_b, "conv_b"), (d_skip, "d_skip")):
                sp.dma_start(dst, ins[name]).then_inc(loaded["conv"], 16)
            for c in range(1, NC):
                load_hid(c)
            sp.dma_start(consts[:, n_early:], ins["consts"][:, n_early:]).then_inc(loaded["consts"], 16)
            sp.dma_start(w_in[:, :, H:2 * H], ins["w_in"][:, :, H:2 * H]).then_inc(loaded["w_in_z"], 16)
            sp.dma_start(w_out, ins["w_out"]).then_inc(loaded["w_out"], 16)
            for dst, name in ((w_x[:, :, :], "w_x"), (g_res[:, :], "g_res"), (w_r[:, :, :], "w_r"),
                              (b1[:, :], "b1"),
                              (u[L:L + 1, 0, :], "b_x"), (u[L:L + 1, 1, :], "b_x"),
                              (decay[L:L + 1, :], "one_row")):
                sp.dma_start(dst, ins[name]).then_inc(loaded["small"], 16)
            sp.dma_start(b_r[:, :], ins["b_r"].to_broadcast([L, NE])).then_inc(loaded["small"], 16)
            sp.dma_start(g_init[:, :], ins["g_init"].to_broadcast([L, D])).then_inc(loaded["small"], 16)
            sp.wait_ge(pad_set, 1)
            sp.dma_start(x2_rows[T:T + 1, :], pad_row).then_inc(loaded["pad"], 16)
            w2_pieces = ins["w2"].rearrange("p e m d -> p (e m d)")

            def step(pair, q):
                b, par, half = seq(pair, q, 4)
                if b is not None:
                    sp.wait_ge(x2_set, b + 1)
                    sp.dma_start(x2_rows[bass.ds(b * L, L), :], x2[:, par, :]).then_inc(x2_stored[par], 16)
                b, par, half = seq(pair, q, 1)
                if b is not None:
                    sp.wait_ge(dft_ps, b + 1)
                    sp.dma_start(w2_flat[:, bass.ds(b * H, H)], w2_pieces[:, bass.ds(b * H, H)])\
                      .then_inc(loaded["w2"], 16)
                b, par, half = seq(pair, q, 0)
                if b is None:
                    return
                need(sp, u_set, b - 1)
                sp.dma_start(ctx_sb[:, par, :], ins["ctx"][b, :, :]).then_inc(c_loaded[par], 16)
                need(sp, pre_set, b - 1)
                sp.dma_start(x_res[:, par, :], ins["x"][b, :, :]).then_inc(x_loaded[par], 16)
                if isinstance(b, int) and b == 0:
                    sp.wait_ge(spec_set, HT)
                    sp.wait_ge(xt_ps, HT * NC)
                    sp.wait_ge(loaded["pad"], 16)
                if not isinstance(b, int):
                    sp.wait_ge(decay_set, 1)
                sp.dma_start(w1[:, half, par, :], ins["w1"][:, half, par, :]).then_inc(loaded["w1"], 16)

            b_steps(sp, step)
            sp.wait_ge(out_ps, NB)
            sp.wait_ge(gate_set, NB)
            sp.wait_ge(cross_ps, NB)
            sp.dma_start(shared[:, :], ins["b2"].to_broadcast([P, NE * D])).then_inc(loaded["b2"], 16)
            for e in range(NE // 2, NE):
                if e == NE - 1:
                    sp.wait_ge(rows_loaded[0], 16)
                sp.dma_start(w2[:, e, :, :], ins["w2"][:, e, :, :]).then_inc(loaded["w2"], 16)


        @block.gpsimd
        def _(pool):
            g = nc.gpsimd
            g.memset(ones16[:, :], 1.0).then_inc(ones_set, 1)
            g.memset(pad_row, 0.0).then_inc(pad_set, 1)
            pool.wait_ge(loaded["consts_early"], 16)

            done = 0

            def link(ins_):
                nonlocal done
                done += 1
                ins_.then_inc(k_pool, 1)
                pool.wait_ge(k_pool, done)

            def mul(o, a, b):
                link(g.tensor_tensor(o, a, b, ALU.mult))

            def add(o, a, b):
                link(g.tensor_tensor(o, a, b, ALU.add))

            def sub(o, a, b):
                link(g.tensor_tensor(o, a, b, ALU.subtract))

            def scale(o, a, m, c=0.0):
                link(g.tensor_scalar(o, a, m, c, ALU.mult, ALU.add))

            a_re, a_im, c_re, c_im = (ssm[:, n, :] for n in range(4))
            K = [km[:, n, :] for n in range(24)]
            a_abs, dta, dtb, th, em1, den, sq1, sq2, q_inv, sn, cs_, e_re, e_im, n_re, n_im, ct_re, ct_im, \
                tmp, tmp2 = K[0:19]
            pool.wait_ge(k_exp, 2)
            dt_b = dt.unsqueeze(2).to_broadcast([P, HT, MODES])
            as_hm = lambda v: v.rearrange("p (h m) -> p h m", h=HT)
            mul(as_hm(dta), as_hm(a_abs), dt_b)
            scale(dta, dta, -1.0)
            mul(as_hm(dtb), as_hm(a_im), dt_b)
            dt_count.append(done)
            th4 = theta.rearrange("p (s h l m) -> p s h l m", s=2, h=HT, l=NLAG)
            mg4 = mag.rearrange("p (h l m) -> p h l m", h=HT, l=NLAG)
            mul(mg4, const("lags").unsqueeze(1).unsqueeze(3).to_broadcast([P, HT, NLAG, MODES]),
                as_hm(dta).unsqueeze(2).to_broadcast([P, HT, NLAG, MODES]))
            mag_count.append(done)
            mul(sq1, a_abs, a_abs)
            mul(sq2, a_im, a_im)
            add(sq1, sq1, sq2)
            pool.wait_ge(k_exp, 3)
            scale(den, th, -1.0, 1.0)
            recip_count.append(done)
            g.memset(run, 1.0).then_inc(run_set, 1)
            pool.wait_ge(run_set, 1)
            g.memset(run.rearrange("p (b t) -> p b t", b=NB)[:, :, 0:1], 0.0).then_inc(run_set, 1)
            pool.wait_ge(ends_sb, 1)
            iota_b = const("iota", PP)[:, 0:L].unsqueeze(1).to_broadcast([PP, NB, L])
            g.tensor_tensor(far.rearrange("p (b t) -> p b t", b=NB), iota_b,
                            ends_t[:, 0:NB].unsqueeze(2).to_broadcast([PP, NB, L]), ALU.subtract)\
             .then_inc(far_set, 1)
            pool.wait_ge(far_set, 1)
            g.tensor_scalar(hits[:, 0, :], far, 0.0, None, ALU.is_equal).then_inc(hits_set, 1)
            pool.wait_ge(k_recip, 2)
            mul(em1, th, den)
            scale(em1, em1, 2.0)
            pool.wait_ge(k_exp, 4)
            pool.wait_ge(k_sin, 1)
            s_half = th4[:, 0, :, NLAG - 1, :]
            c_half = th4[:, 1, :, NLAG - 1, :]
            mul(as_hm(sn), s_half, c_half)
            scale(sn, sn, 2.0)
            mul(as_hm(tmp), s_half, s_half)
            scale(tmp, tmp, 2.0)
            scale(cs_, tmp, -1.0, 1.0)
            mul(e_re, em1, cs_)
            sub(e_re, e_re, tmp)
            scale(tmp, em1, 1.0, 1.0)
            mul(e_im, tmp, sn)
            mul(n_re, c_re, e_re)
            mul(tmp, c_im, e_im)
            sub(n_re, n_re, tmp)
            mul(n_im, c_re, e_im)
            mul(tmp, c_im, e_re)
            add(n_im, n_im, tmp)
            mul(tmp, n_im, a_im)
            mul(tmp2, n_re, a_abs)
            sub(tmp, tmp, tmp2)
            mul(ct_re, tmp, sq1)
            mul(tmp, n_re, a_im)
            mul(tmp2, n_im, a_abs)
            add(tmp, tmp, tmp2)
            mul(ct_im, tmp, sq1)
            scale(ct_re, ct_re, 2.0)
            scale(ct_im, ct_im, -2.0)
            for s, dst in ((1, 0), (0, MODES)):
                mul(modes_c[:, :, :, dst:dst + MODES], th4[:, s, :, LA:LA + LO, :], mg4[:, :, LA:LA + LO, :])
                mul(cplx[:, 1 - s], th4[:, s, :, 0:LA, :], mg4[:, :, 0:LA, :])
            cr = as_hm(ct_re).unsqueeze(2).to_broadcast([P, HT, LA, MODES])
            ci = as_hm(ct_im).unsqueeze(2).to_broadcast([P, HT, LA, MODES])
            a_r, a_i = modes_a[:, :, :, 0:MODES], modes_a[:, :, :, MODES:2 * MODES]
            mul(a_r, cplx[:, 0], cr)
            mul(k_tmp, cplx[:, 1], ci)
            sub(a_r, a_r, k_tmp)
            mul(a_i, cplx[:, 0], ci)
            mul(k_tmp, cplx[:, 1], cr)
            add(a_i, a_i, k_tmp)
            scale(a_i, a_i, -1.0)
            for h in range(HT):
                for a in range(LA):
                    last = g.tensor_tensor(
                        k_prods[h][:, a * LO * 2 * MODES:(a + 1) * LO * 2 * MODES].rearrange("p (c m) -> p c m", c=LO),
                        modes_c[:, h], modes_a[:, h, a].unsqueeze(1).to_broadcast([P, LO, 2 * MODES]), ALU.mult)
                last.then_inc(k_prod_set, 1)

            m_half = const("m_half", L)

            def rsqrt(o, a, tmp_, chain, count):
                g.tensor_tensor(tmp_, a, const("eps", a.shape[0]), ALU.add).then_inc(chain, 1)
                pool.wait_ge(chain, count + 1)
                return g.tensor_tensor(o, tmp_, m_half[0:o.shape[0]], ALU.pow)

            pool.wait_ge(loaded["consts"], 16)
            g.tensor_copy(tri16[:, :], const("earlier", L)).then_inc(tri_set, 1)
            g.tensor_copy(iota16[:, :], const("iota", L)).then_inc(tri_set, 1)

            def step(pair, q):
                b, par, half = seq(pair, q, 1)
                if b is not None:
                    pool.wait_ge(sq_set, b + 1)
                    need(pool, u_set, b - 1)
                    g.tensor_tensor(cs[par][:, 1:2], cs[par][:, 0:1], const("eps", L), ALU.add).then_inc(cs_step, 1)
                    pool.wait_ge(cs_step, b + 1)
                    g.tensor_tensor(rr[par][:, 0:1], cs[par][:, 1:2], m_half, ALU.pow).then_inc(cs_set, 1)
                b, par, half = seq(pair, q, 0)
                if b is not None:
                    pool.wait_ge(prod_set, b + 1)
                    need(pool, idft_ps, b)
                    g.tensor_tensor(y_spec[:, 0, :], prod[:, 0, :], prod[:, 1, :], ALU.subtract)
                    g.tensor_tensor(y_spec[:, 1, :], prod[:, 2, :], prod[:, 3, :], ALU.add).then_inc(y_set, 1)
                b, par, half = seq(pair, q, 2)
                if b is not None:
                    pool.wait_ge(mv1_set, b + 1)
                    need(pool, x1_set, b - 1)
                    need(pool, sum1_set, b - 1)
                    n_ = nr[0][par]
                    rsqrt(n_[:, 1:2], mv[0][par][:, 1:2], n_[:, 0:1], nr1_step, 5 * b).then_inc(nr1_step, 1)
                    pool.wait_ge(nr1_step, 5 * b + 2)
                    g.tensor_tensor(n_[:, 2:3], mv[0][par][:, 1:2], n_[:, 1:2], ALU.mult).then_inc(nr1_step, 1)
                    pool.wait_ge(nr1_step, 5 * b + 3)
                    g.tensor_tensor(n_[:, 2:3], n_[:, 2:3], n_[:, 1:2], ALU.mult).then_inc(nr1_step, 1)
                    pool.wait_ge(nr1_step, 5 * b + 4)
                    rsqrt(n_[:, 3:4], n_[:, 2:3], n_[:, 0:1], nr1_step, 5 * b + 4).then_inc(r1_set, 1)
                b, par, half = seq(pair, q, 3)
                if b is not None:
                    pool.wait_ge(mv2_set, b + 1)
                    need(pool, x2_set, b - 1)
                    rsqrt(nr[1][par][:, 1:2], mv[1][par][:, 1:2], nr[1][par][:, 0:1], nr2_step, b)\
                        .then_inc(r2_set, 1)

            b_steps(pool, step)

            pool.wait_ge(in_tile_set, 1)
            g.tensor_tensor(token_parts[:, :, 0, :], in_tile,
                            const("seq_first_mT", L).unsqueeze(2).to_broadcast([L, NB, TILES]), ALU.mult)\
             .then_inc(parts_set, 1)

            m_half_f = const("m_half")
            last_token = pool.to_reg(T - 1)

            def take_index(i, place):
                g.tensor_copy(g_index[:, place, :], token_of[:, bass.ds(i, 1)]).then_inc(g_index_set, 1)

            def gather(place, index):
                g.indirect_dma_start(rows[:, place, :], None, x2_rows, bass.IndirectOffsetOnAxis(
                    ap=index, axis=0)).then_inc(rows_loaded[place], 16)

            pool.wait_ge(token_set, 1)
            pool.wait_ge(loaded["pad"], 16)
            for i in range(F_AHEAD):
                gather(i, token_of[:, i:i + 1])

            def f_step(group, q, tiles=TILES):
                ahead, a_place, a_gr = tile_of(group, q, -F_AHEAD, tiles)
                if ahead is not None:
                    apart(pool, (fs_set, ahead - 3))
                    take_index(ahead, a_place)
                i, place, gr = tile_of(group, q, 1, tiles)
                par = place % 2
                if i is not None:
                    pool.wait_ge(fmv_set, i + 1)
                    need(pool, y_done, i - 1)
                if ahead is not None:
                    pool.wait_ge(g_index_set, ahead - F_AHEAD + 1)
                if i is not None:
                    g.tensor_tensor(f_nr[:, par, 0:1], f_mv[:, par, 1:2], const("eps"), ALU.add).then_inc(fn_step, 1)
                if ahead is not None:
                    gather(a_place, g_index[:, a_place, :])
                if i is not None:
                    pool.wait_ge(fn_step, i + 1)
                    g.tensor_tensor(f_nr[:, par, 1:2], f_nr[:, par, 0:1], m_half_f, ALU.pow).then_inc(fr_set, 1)
                    apart(pool, (y_done, i + 1))
                    g.tensor_copy(f_index[:, par, :], token_of[:, bass.ds(i, 1)]).then_inc(index_set, 1)
                    apart(pool, (index_set, i + 1))
                    g.indirect_dma_start(out, bass.IndirectOffsetOnAxis(
                        ap=f_index[:, par, :], axis=0), y_row[:, par, :], None,
                        bounds_check=last_token, oob_is_err=False).then_inc(rows_out[place], 16)
            def finish(tiles):
                for i in range(tiles + 1, min(tiles + F_AHEAD, TILES)):
                    pool.wait_ge(rows_loaded[i % 4], 16 * (i // 4 + 1))
                for place in range(4):
                    pool.wait_ge(rows_out[place], 16 * len(range(place, tiles, 4)))

            f_steps(pool, f_step, finish)

        @block.scalar
        def _(act):
            a = nc.scalar
            act.dma_start(log_dt, ins["log_dt"]).then_inc(loaded["ssm"], 16)
            act.dma_start(ssm, ins["ssm"]).then_inc(loaded["ssm"], 16)
            act.wait_ge(loaded["ssm"], 32)
            a.activation(dt, log_dt, ACT.Exp).then_inc(k_exp, 1)
            a.activation(km[:, 0, :], ssm[:, 0, :], ACT.Exp).then_inc(k_exp, 1)
            act.wait_ge(k_pool, 2)
            a.activation(km[:, 3, :], km[:, 1, :], ACT.Tanh, scale=0.5).then_inc(k_exp, 1)
            act.wait_ge(k_pool, mag_count[0])
            a.activation(mag, mag, ACT.Exp).then_inc(k_exp, 1)

            def a_step(c, h):
                unit = HT * c + h
                par = h % 2
                act.wait_ge(in_ps, unit + 1)
                need(act, act_x, unit - 1)
                a.activation(conv_acc[:, par, :], ps[:, h, 0:CW], ACT.Copy, scale=conv_w[:, h, TAPS - 1:TAPS])\
                 .then_inc(acc_set, 1)

            def a_silu(unit, h):
                par = h % 2
                act.wait_ge(conv_done, unit + 1)
                need(act, xt_ps, unit - 1)
                a.activation(conv_x[:, par, :], conv_acc[:, par, :], ACT.Silu, bias=conv_b[:, h:h + 1])\
                 .then_inc(act_x, 1)

            def a_move(c, h):
                unit = HT * c + h
                act.wait_ge(xt_ps, unit + 1)
                a.activation(x_time[:, bass.ds(CB * c, CB), h * P:(h + 1) * P],
                             ps[0:L, 4 + h % 2, :].rearrange("p (b h) -> p b h", b=CB), ACT.Copy)\
                 .then_inc(xt_set, 1)

            def a_unit(c, h):
                before = (c, h - 1) if h else (c - 1, HT - 1)
                if not (isinstance(c, int) and before[0] < 0):
                    a_silu(HT * c + h - 1, (h - 1) % HT)
                if not (isinstance(c, int) and (c, h) == (NC - 1, HT - 1)):
                    a_step(*((c, h + 1) if h < HT - 1 else (c + 1, 0)))
                before2 = (c, h - 2) if h >= 2 else (c - 1, h + HT - 2)
                if not (isinstance(c, int) and before2[0] < 0):
                    a_move(*before2)

            act.wait_ge(loaded["conv"], 48)
            a_step(0, 0)
            for h in range(HT):
                a_unit(0, h)
                if h == 0:
                    act.wait_ge(k_phase, K_PHASE)
                    a.activation(theta, theta, ACT.Sin).then_inc(k_sin, 1)
                if h == 1:
                    for n in range(NC):
                        act.wait_ge(count_ps, n + 1)
                        a.activation(plug[:, n * CW:(n + 1) * CW], ps[0:L, 4 + n, 0:CW], ACT.Sign)\
                         .then_inc(plug_set, 1)
            with act.Fori(1, NC - 1) as c:
                for h in range(HT):
                    a_unit(c, h)
            for h in range(HT):
                a_unit(NC - 1, h)
            a_silu(HT * NC - 1, HT - 1)
            a_move(NC - 1, HT - 2)
            a_move(NC - 1, HT - 1)
            for h in range(HT):
                tile = slice(h * P, (h + 1) * P)
                act.wait_ge(kern_ps, h + 1)
                a.activation(kern_t[:, tile], ps[0:L, 4, tile], ACT.Copy).then_inc(kern_sb, 1)
                act.wait_ge(spec_ps, h + 1)
                a.activation(spec[:, :, tile], ps[0:L, 5:8, tile], ACT.Copy).then_inc(spec_set, 1)

            def step(pair, q):
                b, par, half = seq(pair, q, 1)
                if b is not None:
                    act.wait_ge(c_loaded[par], 16 * (half + 1))
                    need(act, cs_set, b - 1)
                    need(act, sq_set, b)
                    a.activation(ctx_sq, ctx_sb[:, par, :], ACT.Square, scale=C ** -0.5, accum_out=cs[par][:, 0:1])\
                     .then_inc(sq_set, 1)
                b, par, half = seq(pair, q, 2)
                if b is not None:
                    act.wait_ge(decay_set, 1)
                    need(act, cross_ps, b - 1)
                    a.activation(decay_b[:, par, :], decay[:, bass.ds(b * L, L)], ACT.Copy).then_inc(decay_kept, 1)
                b, par, half = seq(pair, q, 0)
                if b is not None:
                    act.wait_ge(z_ps, b + 1)
                    need(act, gate_set, b - 1)
                    a.activation(z_act[:, par, :], ps[:, 2, 0:HT * L], ACT.Silu).then_inc(z_set, 1)
                b, par, half = seq(pair, q, 3)
                if b is not None:
                    act.wait_ge(x1t_ps, b + 1)
                    need(act, cross_ps, b - 1)
                    a.activation(x1_t[:, par, :], ps[:, 5, 0:DT * L], ACT.Copy).then_inc(x1t_set, 1)
                b, par, half = seq(pair, q, 4)
                if b is not None:
                    act.wait_ge(x2t_ps, b + 1)
                    need(act, logit_ps, b - 1)
                    a.activation(x2_t[:, par, :], ps[:, 7, 0:DT * L], ACT.Copy).then_inc(x2t_set, 1)
                if isinstance(pair, int) and (pair, q) == (0, 0):
                    act.wait_ge(plug_ready, 2)
                    a.activation(fall, fall, ACT.Exp, scale=-DECAY).then_inc(fall_step, 1)

            b_steps(act, step)

            def f_step(group, q, tiles=TILES):
                i, place, gr = tile_of(group, q, -1, tiles)
                if i is not None:
                    move_rows(i, place)
                i, place, gr = tile_of(group, q, 0, tiles)
                par = place % 2
                if i is not None:
                    e = act.value_load(tile_expert[0:1, bass.ds(i, 1)], min_val=0, max_val=NE - 1)
                    act.wait_ge(ht_ps, i + 1)
                    need(act, f_ps, i - 1)
                    for m in range(FT):
                        last = a.activation(h_t[:, par, m * P:(m + 1) * P],
                                            ps[:, 2 * par + m // 4, (m % 4) * P:(m % 4 + 1) * P], ACT.Relu,
                                            bias=b1[:, bass.ds(e * FT + m, 1)])
                    last.then_inc(ht_set, 1)

            def move_rows(i, place):
                par = place % 2
                act.wait_ge(rt_ps, i + 1)
                need(act, ht_ps, i - 1)
                a.activation(rows_t[:, par, :], ps[:, 6, 0:D], ACT.Copy).then_inc(rt_set, 1)

            act.wait_ge(in_tile_set, 1)
            a.activation(token_parts[:, :, 1, :], in_tile, ACT.Copy, scale=const("part", L)).then_inc(parts_set, 1)
            act.wait_ge(experts_set, 1)
            move_rows(0, 0)
            f_steps(act, f_step)

        @block.vector
        def _(dve):
            v = nc.vector
            dve.wait_ge(loaded["lens"], 16)
            v.tensor_copy(ends[:, 0, :], lens).then_inc(b_step, 1)
            v.memset(ends[:, 1, :], 1.0).then_inc(b_step, 1)
            dve.wait_ge(b_step, 2)
            v.tensor_tensor_scan(ends[:, 2, :], ends[:, 1, :], ends[:, 0, :], 0.0, ALU.mult, ALU.add)\
             .then_inc(b_step, 1)
            dve.wait_ge(b_step, 3)
            v.tensor_scalar(ends[:, 2, :], ends[:, 2, :], 1.0, None, ALU.subtract).then_inc(b_step, 1)
            dve.wait_ge(b_step, 4)
            v.tensor_scalar(ends[:, 3, :], ends[:, 2, :], 0.0, float(L), ALU.is_lt, ALU.mult).then_inc(b_step, 1)
            dve.wait_ge(b_step, 5)
            v.tensor_tensor(ends[:, 2, :], ends[:, 2, :], ends[:, 3, :], ALU.add).then_inc(b_step, 1)
            dve.wait_ge(ends_ps, 1)
            v.tensor_copy(ends_t, ps[0:PP, 6, 0:PT * NB]).then_inc(ends_sb, 1)
            dve.wait_ge(loaded["consts_early"], 16)
            dve.wait_ge(k_pool, dt_count[0])
            done = 0

            def phase(ins_):
                nonlocal done
                done += 1
                ins_.then_inc(k_phase, 1)
                dve.wait_ge(k_phase, done)

            phase(v.tensor_tensor(
                theta[:, 0:nm].rearrange("p (h l m) -> p h l m", h=HT, l=NLAG),
                const("lags").unsqueeze(1).unsqueeze(3).to_broadcast([P, HT, NLAG, MODES]),
                km[:, 2, :].rearrange("p (h m) -> p h m", h=HT).unsqueeze(2).to_broadcast([P, HT, NLAG, MODES]),
                ALU.mult))
            phase(v.tensor_scalar(theta[:, nm:2 * nm], theta[:, 0:nm], math.pi / 2, None, ALU.add))
            phase(v.tensor_scalar(turns, theta, 1 / (2 * math.pi), MAGIC, ALU.mult, ALU.add))
            phase(v.tensor_scalar(turns, turns, MAGIC, None, ALU.subtract))
            phase(v.scalar_tensor_tensor(theta, turns, -TWO_PI_HI, theta, ALU.mult, ALU.add))
            phase(v.scalar_tensor_tensor(theta, turns, -TWO_PI_LO, theta, ALU.mult, ALU.add))
            v.tensor_scalar(theta, theta, PI_BELOW, -PI_BELOW, ALU.min, ALU.max).then_inc(k_phase, 1)
            assert done + 1 == K_PHASE
            dve.wait_ge(ends_sb, 1)
            for k in range(1, PT):
                v.tensor_tensor(
                    hits[:, k, :].rearrange("p (b t) -> p b t", b=NB),
                    const("iota", PP)[:, 0:L].unsqueeze(1).to_broadcast([PP, NB, L]),
                    ends_t[:, k * NB:(k + 1) * NB].unsqueeze(2).to_broadcast([PP, NB, L]), ALU.is_equal)\
                 .then_inc(hits_set, 1)

            def a_step(c, h):
                unit = HT * c + h
                par = h % 2
                dve.wait_ge(acc_set, unit + 1)
                acc = conv_acc[:, par, :].rearrange("p (b t) -> p b t", b=CB)
                raw = ps[:, h, 0:CW].rearrange("p (b t) -> p b t", b=CB)
                for back in range(1, TAPS):
                    tap = TAPS - 1 - back
                    ins_ = v.scalar_tensor_tensor(acc[:, :, back:L], raw[:, :, 0:L - back],
                                                  conv_w[:, h, tap:tap + 1], acc[:, :, back:L],
                                                  ALU.mult, ALU.add)
                    if back < TAPS - 1:
                        ins_.then_inc(tap_set, 1)
                        dve.wait_ge(tap_set, (TAPS - 2) * unit + back)
                    else:
                        ins_.then_inc(conv_done, 1)

            dve.wait_ge(loaded["conv"], 48)
            dve.wait_ge(k_pool, recip_count[0])
            v.reciprocal(km[:, 5, :], km[:, 5, :]).then_inc(k_recip, 1)
            v.reciprocal(km[:, 6, :], km[:, 6, :]).then_inc(k_recip, 1)
            for h in range(HT):
                a_step(0, h)
            with dve.Fori(1, NC) as c:
                for h in range(HT):
                    a_step(c, h)
            for h in range(HT):
                dve.wait_ge(k_prod_set, h + 1)
                v.tensor_reduce(kern[:, h, :], k_prods[h].rearrange("p (l m) -> p l m", m=2 * MODES), AX_X, ALU.add)\
                 .then_inc(k_sum, 1)
                dve.wait_ge(k_sum, 2 * h + 1)
                v.tensor_tensor(kern[:, h, 0:1], kern[:, h, 0:1], d_skip[:, h:h + 1], ALU.add).then_inc(k_sum, 1)

            dve.wait_ge(plug_set, NC)
            dve.wait_ge(run_set, 2)
            v.tensor_tensor_scan(plug, run, plug, 0.0, ALU.mult, ALU.add).then_inc(plug_scan, 1)
            dve.wait_ge(plug_scan, 1)
            v.tensor_scalar(plug, plug, -1.0, 0.0, ALU.add, ALU.max).then_inc(plug_ready, 1)
            dve.wait_ge(plug_ready, 1)
            v.tensor_scalar(fall, plug, const("part", L), 0.0, ALU.subtract, ALU.max).then_inc(plug_ready, 1)
            dve.wait_ge(loaded["consts"], 16)

            def normalize(o, src, m, rs):
                return v.tensor_scalar(o, src, m, rs, ALU.subtract, ALU.mult)

            def step(pair, q):
                b, par, half = seq(pair, q, 3)
                if b is not None:
                    dve.wait_ge(r1_set, b + 1)
                    need(dve, x1t_ps, b - 1)
                    need(dve, sum1_set, b - 1)
                    normalize(x1[:, par, :], x1_pre, mv[0][par][:, 0:1], nr[0][par][:, 1:2]).then_inc(x1_set, 1)
                b, par, half = seq(pair, q, 0)
                if b is not None:
                    dve.wait_ge(dft_ps, b + 1)
                    dve.wait_ge(spec_set, HT)
                    need(dve, y_set, b)
                    for n, (x_part, k_part) in enumerate(((0, 0), (1, 1), (0, 1), (1, 2))):
                        last = v.tensor_tensor(prod[:, n, :], ps[0:L, x_part, :], spec[:, k_part, :], ALU.mult)
                    last.then_inc(prod_set, 1)
                b, par, half = seq(pair, q, 4)
                if b is not None:
                    dve.wait_ge(r2_set, b + 1)
                    need(dve, x2t_ps, b - 1)
                    need(dve, x2_stored[par], 16 * half)
                    normalize(x2[:, par, :], x2_sum[:, par, :], mv[1][par][:, 0:1], nr[1][par][:, 1:2])\
                        .then_inc(x2_set, 1)
                b, par, half = seq(pair, q, 2)
                if b is not None:
                    dve.wait_ge(cs_set, b + 1)
                    dve.wait_ge(b_step, 6 + DT + 1)
                    need(dve, cross_ps, b - 1)
                    v.scalar_tensor_tensor(u[0:L, par, :], ctx_sb[:, par, 0:D], rr[par][:, 0:1], g_init[:, :],
                                           ALU.mult, ALU.mult).then_inc(u_set, 1)
                b, par, half = seq(pair, q, 1)
                if b is not None:
                    dve.wait_ge(idft_ps, b + 1)
                    dve.wait_ge(z_set, b + 1)
                    need(dve, out_ps, b - 1)
                    v.tensor_tensor(gated[:, par, :], ps[:, 3, 0:HT * L], z_act[:, par, :], ALU.mult)\
                     .then_inc(gate_set, 1)
                b, par, half = seq(pair, q, 2)
                if b is not None:
                    dve.wait_ge(out_ps, b + 1)
                    dve.wait_ge(x_loaded[par], 16 * (half + 1))
                    need(dve, x1_set, b)
                    v.tensor_tensor(x1_pre, ps[0:L, 4, 0:D], x_res[:, par, :], ALU.add).then_inc(pre_set, 1)
                    dve.wait_ge(pre_set, b + 1)
                    v.bn_stats(bn[0], x1_pre).then_inc(bn1_set, 1)
                    apart(dve, (bn1_set, b + 1), (r1_set, b - 1))
                    v.bn_aggr(mv[0][par], bn[0]).then_inc(mv1_set, 1)
                b, par, half = seq(pair, q, 3)
                if b is not None:
                    dve.wait_ge(cross_ps, b + 1)
                    dve.wait_ge(x1_set, b + 1)
                    need(dve, x2_set, b - 1)
                    s2 = x2_sum[:, par, :]
                    v.scalar_tensor_tensor(s2, ps[0:L, 6, 0:D], nr[0][par][:, 3:4], x1[:, par, :],
                                           ALU.mult, ALU.add).then_inc(sum1_set, 1)
                    dve.wait_ge(sum1_set, b + 1)
                    v.tensor_tensor(s2, s2, ps[0:L, 6, D:2 * D], ALU.add).then_inc(sum2_set, 1)
                    dve.wait_ge(sum2_set, b + 1)
                    v.bn_stats(bn[1], s2).then_inc(bn2_set, 1)
                    apart(dve, (bn2_set, b + 1), (r2_set, b - 1))
                    v.bn_aggr(mv[1][par], bn[1]).then_inc(mv2_set, 1)
                b, par, half = seq(pair, q, 4)
                if b is not None:
                    dve.wait_ge(logit_ps, b + 1)
                    v.tensor_tensor(logits[:, bass.ds(b * NE, NE)], ps[0:L, 7, 256:256 + NE], b_r[:, :],
                                    ALU.add).then_inc(logit_set, 1)
                if isinstance(pair, int) and (pair, q) == (0, 0):
                    dve.wait_ge(loaded["small"], 16 * 9)
                    for k in range(DT):
                        v.tensor_scalar(w_x[:, k, :], w_x[:, k, :], g_res[:, k:k + 1], None, ALU.mult).then_inc(b_step, 1)
                    v.tensor_scalar(g_init[:, :], g_init[:, :], BCOEF, None, ALU.mult).then_inc(b_step, 1)

                if isinstance(pair, int) and (pair, q) == (0, 1):
                    dve.wait_ge(fall_step, 1)
                    v.scalar_tensor_tensor(plug, plug, const("part", L), fall, ALU.is_ge, ALU.mult)\
                     .then_inc(decay_set, 1)

            b_steps(dve, step)

            done = 0

            def link(ins_):
                nonlocal done
                done += 1
                ins_.then_inc(r_step, 1)
                dve.wait_ge(r_step, done)

            dve.wait_ge(logit_set, NB)
            dve.wait_ge(x2t_set, NB)
            for q in range(2):
                dve.wait_ge(x2_stored[q], 16 * NB // 2)
            be = lambda x, n=L: x[0:n].rearrange("p (b e) -> p b e", b=NB)
            lg = logits[:, :].rearrange("p (b e) -> p b e", b=NB)
            best, key, first = rt[0:L, 0, 0:NB], rt[0:L, 1, :], rt[0:L, 2, 0:NB]
            m8 = const("expert_m8", L)
            link(v.tensor_reduce(best, lg, AX_X, ALU.max))
            link(v.tensor_tensor(be(key), lg, best.unsqueeze(2).to_broadcast([L, NB, NE]), ALU.is_equal))
            link(v.tensor_tensor(key, key, m8, ALU.mult))
            link(v.tensor_reduce(first, be(key), AX_X, ALU.min))
            link(v.tensor_tensor(be(rt[0:L, 3, :]), be(m8), first.unsqueeze(2).to_broadcast([L, NB, NE]),
                                 ALU.is_equal))
            chosen = rt[0:L, 3, :]
            v.tensor_copy(one_hot, chosen).then_inc(one_hot_set, 1)
            dve.wait_ge(rank_ps, 1)
            tot, run_, excl = rt[:, 4, :], rt[:, 5, :], rt[:, 6, :]
            link(v.tensor_copy(tot.rearrange("p (e b) -> p b e", b=NB),
                               ps[:, 1, 0:NB * NE].rearrange("p (b e) -> p b e", b=NB)))
            link(v.tensor_tensor_scan(run_, const("seq_reset"), tot, 0.0, ALU.mult, ALU.add))
            link(v.tensor_tensor(excl, run_, tot, ALU.subtract))
            count = run_.rearrange("p (e b) -> p e b", b=NB)[:, :, NB - 1:NB]
            tn = tile_n.rearrange("p (e j) -> p e j", e=NE)
            link(v.tensor_tensor(tn, count.to_broadcast([P, NE, TPE]),
                                 const("tile_from").rearrange("p (e j) -> p e j", e=NE), ALU.is_gt))
            link(v.tensor_reduce(per_e[:, 0, :], tn, AX_X, ALU.add))
            link(v.memset(per_e[:, 1, :], 1.0))
            link(v.tensor_tensor_scan(per_e[:, 2, :], per_e[:, 1, :], per_e[:, 0, :], 0.0, ALU.mult, ALU.add))
            link(v.tensor_tensor(per_e[:, 3, :], per_e[:, 2, :], per_e[:, 0, :], ALU.subtract))
            link(v.scalar_tensor_tensor(
                rt[0:L, 7, :].rearrange("p (b e) -> p e b", b=NB),
                per_e[0:L, 3, :].unsqueeze(2).to_broadcast([L, NE, NB]), float(P),
                excl[0:L].rearrange("p (e b) -> p e b", b=NB), ALU.mult, ALU.add))
            link(v.tensor_tensor(rt[0:L, 7, :], rt[0:L, 7, :], ps[0:L, 0, 0:NB * NE], ALU.add))
            link(v.tensor_tensor(rt[0:L, 7, :], rt[0:L, 7, :], chosen, ALU.mult))
            link(v.tensor_reduce(slot_f, be(rt[:, 7, :]), AX_X, ALU.add))
            link(v.tensor_scalar(slot_tile, slot_f, 1 / P, 0.5 / P - 0.5, ALU.mult, ALU.add))
            link(v.tensor_scalar(slot_tile, slot_tile, MAGIC, MAGIC, ALU.add, ALU.subtract))
            v.tensor_tensor(in_tile, slot_tile.unsqueeze(2).to_broadcast([L, NB, TILES]),
                            const("iota", L)[:, 0:TILES].unsqueeze(1).to_broadcast([L, NB, TILES]), ALU.is_equal)\
             .then_inc(in_tile_set, 1)
            link(v.scalar_tensor_tensor(slot_part, slot_tile, -float(P), slot_f, ALU.mult, ALU.add))
            dve.wait_ge(tri_set, 2)
            for b in range(NB):
                v.tensor_scalar(in_place[:, b, :], iota16[:, :], slot_part[:, b:b + 1], None, ALU.is_equal)\
                 .then_inc(place_set, 1)
            dve.wait_ge(token_ps, 1)
            v.tensor_scalar(token_of, ps[:, 2, 0:TILES], float(T), None, ALU.add).then_inc(token_set, 1)
            link(v.tensor_tensor(tile_hits.rearrange("p (i e) -> p i e", e=NE),
                                 const("tile_no").rearrange("p (i e) -> p i e", e=NE),
                                 per_e[:, 2, :].unsqueeze(1).to_broadcast([P, TILES, NE]), ALU.is_ge))
            link(v.tensor_reduce(tile_e[:, 0, 0:TILES], tile_hits.rearrange("p (i e) -> p i e", e=NE), AX_X, ALU.add))
            v.tensor_copy(tile_e[:, 1, TILES:TILES + 1], per_e[:, 2, NE - 1:NE])
            link(v.tensor_scalar(tile_e[:, 1, 0:TILES], tile_e[:, 0, 0:TILES], float(NE - 1), None, ALU.min))
            v.tensor_copy(tile_expert, tile_e[:, 1, :]).then_inc(experts_set, 1)
            dve.wait_ge(experts_set, 1)
            dve.wait_ge(loaded["b2"], 16)
            dve.wait_ge(loaded["w1"], 16 * NB)

            def take_w1(i, place):
                e = dve.value_load(tile_expert[0:1, bass.ds(i, 1)], min_val=0, max_val=NE - 1)
                need(dve, ht_ps, i - 1)
                v.tensor_copy(w1_now[place % 2], w1[:, e, :, :]).then_inc(w1_now_set, 1)

            take_w1(0, 0)

            def f_step(group, q, tiles=TILES):
                i, place, gr = tile_of(group, q, -1, tiles)
                if i is not None:
                    take_w1(i, place)
                i, place, gr = tile_of(group, q, 2, tiles)
                par = place % 2
                if i is not None:
                    dve.wait_ge(fr_set, i + 1)
                    before, b_place, b_gr = tile_of(group, q, 4, tiles)
                    need(dve, rows_out[b_place], 16 * (b_gr + 1) if before is not None else 0)
                    normalize(y_row[:, par, :], y_sum[:, par, :], f_mv[:, par, 0:1], f_nr[:, par, 1:2])\
                        .then_inc(y_done, 1)
                i, place, gr = tile_of(group, q, 1, tiles)
                par = place % 2
                if i is not None:
                    e = dve.value_load(tile_expert[0:1, bass.ds(i, 1)], min_val=0, max_val=NE - 1)
                    dve.wait_ge(f_ps, i + 1)
                    need(dve, y_done, i - 1)
                    v.tensor_tensor(y_sum[:, par, :], ps[:, 4 + par, 0:D], b2[:, e, :], ALU.add).then_inc(fb_set, 1)
                    dve.wait_ge(fb_set, i + 1)
                    dve.wait_ge(rows_loaded[place], 16 * (gr + 1))
                    v.tensor_tensor(y_sum[:, par, :], y_sum[:, par, :], rows[:, place, 0:D], ALU.add)\
                     .then_inc(fs_set, 1)
                    dve.wait_ge(fs_set, i + 1)
                    v.bn_stats(f_bn, y_sum[:, par, :]).then_inc(fbn_set, 1)
                    apart(dve, (fbn_set, i + 1), (fr_set, i - 1))
                    v.bn_aggr(f_mv[:, par, :], f_bn).then_inc(fmv_set, 1)

            f_steps(dve, f_step)

        @block.tensor
        def _(pe):
            m = nc.tensor
            pe.wait_ge(loaded["consts_early"], 16)
            pe.wait_ge(b_step, 6)
            for k in range(PT):
                last = m.transpose(ps[0:PP, 6, k * NB:(k + 1) * NB], ends[:, 2, k * PP:(k + 1) * PP],
                                   ident[0:NB, 0:NB])
            last.then_inc(ends_ps, 1)

            def a_in(c, h):
                unit = HT * c + h
                need(pe, conv_done, unit - HT + 1)
                for k in range(DT):
                    last_ = m.matmul(ps[:, h, 0:CW], w_in[:, k, h * P:(h + 1) * P],
                                     hid_t[:, k, bass.ds(c * CW, CW)], start=(k == 0), stop=(k == DT - 1))
                last_.then_inc(in_ps, 1)

            def a_turn(unit, h):
                pe.wait_ge(act_x, unit + 1)
                need(pe, xt_set, unit - 1)
                for b in range(CB):
                    last_ = m.transpose(ps[0:L, 4 + h % 2, b * P:(b + 1) * P],
                                        conv_x[:, h % 2, b * L:(b + 1) * L], ident)
                last_.then_inc(xt_ps, 1)

            def a_unit(c, h):
                a_in(c, h)
                a_turn(HT * c + h - 2, (h - 2) % HT)

            pe.wait_ge(loaded["w_in_x"], 16)
            pe.wait_ge(hid_loaded[0], 16)
            for h in range(HT):
                a_in(0, h)
            pe.wait_ge(hits_set, PT)
            pe.wait_ge(ones_set, 1)
            for c in range(NC):
                for k in range(PT):
                    last = m.matmul(ps[0:L, 4 + c, 0:CW], ones16[0:PP, 0:L], hits[:, k, c * CW:(c + 1) * CW],
                                    start=(k == 0), stop=(k == PT - 1))
                last.then_inc(count_ps, 1)
            pe.wait_ge(plug_set, NC)
            a_turn(0, 0)
            a_turn(1, 1)
            for c in range(1, NC):
                pe.wait_ge(hid_loaded[c], 16)
            with pe.Fori(1, NC) as c:
                for h in range(HT):
                    a_unit(c, h)
            a_turn(HT * NC - 2, HT - 2)
            a_turn(HT * NC - 1, HT - 1)
            pe.wait_ge(xt_set, HT * NC)
            def transform(pair, q):
                b, par, half = seq(pair, q, 0)
                if b is not None:
                    need(pe, prod_set, b)
                    m.matmul(ps[0:L, 0, :], const("f_re", L), x_time[:, b, :], start=True, stop=True)
                    m.matmul(ps[0:L, 1, :], const("f_im", L), x_time[:, b, :], start=True, stop=True)\
                     .then_inc(dft_ps, 1)

            def gate_input(pair, q):
                b, par, half = seq(pair, q, 0)
                if b is not None:
                    need(pe, z_set, b)
                    for h in range(HT):
                        for k in range(DT):
                            last_ = m.matmul(ps[:, 2, h * L:(h + 1) * L], w_in[:, k, H + h * P:H + (h + 1) * P],
                                             hid_t[:, k, bass.ds(b * L, L)], start=(k == 0), stop=(k == DT - 1))
                    last_.then_inc(z_ps, 1)

            def turn_kernel(h):
                pe.wait_ge(k_sum, 2 * (h + 1))
                m.transpose(ps[0:L, 4, h * P:(h + 1) * P], kern[:, h, :], ident).then_inc(kern_ps, 1)

            def kernel_spectrum(h):
                tile = slice(h * P, (h + 1) * P)
                pe.wait_ge(kern_sb, h + 1)
                need(pe, spec_set, h)
                for s, name in enumerate(("f_re", "f_im0", "f_d")):
                    last = m.matmul(ps[0:L, 5 + s, tile], const(name, L), kern_t[:, tile], start=True, stop=True)
                last.then_inc(spec_ps, 1)

            pe.wait_ge(loaded["w_in_z"], 16)
            pe.wait_ge(loaded["consts"], 16)
            turn_kernel(0)
            transform(0, 0)
            kernel_spectrum(0)
            turn_kernel(1)
            gate_input(0, 0)
            for h in range(1, HT):
                kernel_spectrum(h)
                if h < HT - 1:
                    turn_kernel(h + 1)
            pe.wait_ge(spec_set, HT)
            pe.wait_ge(loaded["w_out"], 16)
            pe.wait_ge(loaded["small"], 16 * 9)

            def step(pair, q):
                if not (isinstance(pair, int) and (pair, q) == (0, 0)):
                    for part in ((gate_input, transform) if isinstance(pair, int) and (pair, q) == (0, 1)
                                 else (transform, gate_input)):
                        part(pair, q)
                b, par, half = seq(pair, q, 1)
                if b is not None:
                    pe.wait_ge(y_set, b + 1)
                    need(pe, gate_set, b)
                    for h in range(HT):
                        for s, name in enumerate(("g_re", "g_im")):
                            last_ = m.matmul(ps[:, 3, h * L:(h + 1) * L], y_spec[:, s, h * P:(h + 1) * P],
                                             const(name, L), start=(s == 0), stop=(s == 1))
                    last_.then_inc(idft_ps, 1)
                b, par, half = seq(pair, q, 3)
                if b is not None:
                    pe.wait_ge(x1_set, b + 1)
                    need(pe, x1t_set, b)
                    for k in range(DT):
                        last_ = m.transpose(ps[:, 5, k * L:(k + 1) * L], x1[:, par, k * P:(k + 1) * P],
                                            ident[0:L, 0:L])
                    last_.then_inc(x1t_ps, 1)
                b, par, half = seq(pair, q, 2)
                if b is not None:
                    pe.wait_ge(gate_set, b + 1)
                    need(pe, pre_set, b)
                    for h in range(HT):
                        last_ = m.matmul(ps[0:L, 4, 0:D], gated[:, par, h * L:(h + 1) * L], w_out[:, h, :],
                                         start=(h == 0), stop=(h == HT - 1))
                    last_.then_inc(out_ps, 1)
                b, par, half = seq(pair, q, 4)
                if b is not None:
                    pe.wait_ge(x2_set, b + 1)
                    need(pe, x2t_set, b)
                    need(pe, logit_set, b)
                    for k in range(DT):
                        last_ = m.transpose(ps[:, 7, k * L:(k + 1) * L], x2[:, par, k * P:(k + 1) * P],
                                            ident[0:L, 0:L])
                    last_.then_inc(x2t_ps, 1)
                b, par, half = seq(pair, q, 3)
                if b is not None:
                    pe.wait_ge(x1t_set, b + 1)
                    pe.wait_ge(b_step, 6 + DT + 1)
                    need(pe, sum2_set, b)
                    for k in range(DT):
                        m.matmul(ps[0:L, 6, 0:D], x1_t[:, par, k * L:(k + 1) * L], w_x[:, k, :],
                                 start=(k == 0), stop=(k == DT - 1))
                    pe.wait_ge(u_set, b + 1)
                    pe.wait_ge(decay_kept, b + 1)
                    m.matmul(ps[0:L, 6, D:2 * D], decay_b[:, par, :], u[:, par, :], start=True, stop=True)\
                     .then_inc(cross_ps, 1)
                b, par, half = seq(pair, q, 4)
                if b is not None:
                    pe.wait_ge(x2t_set, b + 1)
                    for k in range(DT):
                        last_ = m.matmul(ps[0:L, 7, 256:256 + NE], x2_t[:, par, k * L:(k + 1) * L], w_r[:, k, :],
                                         start=(k == 0), stop=(k == DT - 1))
                    last_.then_inc(logit_ps, 1)

            b_steps(pe, step)

            pe.wait_ge(one_hot_set, 1)
            pe.wait_ge(tri_set, 2)
            m.matmul(ps[0:L, 0, 0:NB * NE], tri16[:, :], one_hot, start=True, stop=True)
            m.matmul(ps[:, 1, 0:NB * NE], ones16[0:L, :], one_hot, start=True, stop=True).then_inc(rank_ps, 1)
            pe.wait_ge(parts_set, 2)
            for b in range(NB):
                pe.wait_ge(place_set, b + 1)
                for part in range(2):
                    last = m.matmul(ps[:, 2, 0:TILES], in_place[:, b, :], token_parts[:, b, part, :],
                                    start=(b == 0 and part == 0), stop=(b == NB - 1 and part == 1))
            last.then_inc(token_ps, 1)

            def turn_rows(i, place, gr):
                pe.wait_ge(rows_loaded[place], 16 * (gr + 1))
                need(pe, rt_set, i)
                for k in range(DT):
                    last_ = m.transpose(ps[:, 6, k * P:(k + 1) * P], rows[:, place, k * P:(k + 1) * P], ident)
                last_.then_inc(rt_ps, 1)

            def f_step(group, q, tiles=TILES):
                i, place, gr = tile_of(group, q, 0, tiles)
                if i is not None:
                    par = place % 2
                    pe.wait_ge(w1_now_set, i + 1)
                    pe.wait_ge(rt_set, i + 1)
                    need(pe, ht_set, i - 1)
                    for f in range(FT):
                        for k in range(DT):
                            last_ = m.matmul(ps[:, 2 * par + f // 4, (f % 4) * P:(f % 4 + 1) * P],
                                             w1_now[par][:, k, f * P:(f + 1) * P], rows_t[:, par, k * P:(k + 1) * P],
                                             start=(k == 0), stop=(k == DT - 1))
                    last_.then_inc(ht_ps, 1)
                i, place, gr = tile_of(group, q, -1, tiles)
                if i is not None:
                    turn_rows(i, place, gr)
                i, place, gr = tile_of(group, q, 1, tiles)
                if i is not None:
                    par = place % 2
                    e = pe.value_load(tile_expert[0:1, bass.ds(i, 1)], min_val=0, max_val=NE - 1)
                    if isinstance(i, int) and i == 0:
                        pe.wait_ge(loaded["w2"], 16 * (NB + NE // 2))
                    pe.wait_ge(ht_set, i + 1)
                    need(pe, fb_set, i - 1)
                    for f in range(FT):
                        last_ = m.matmul(ps[:, 4 + par, 0:D], h_t[:, par, f * P:(f + 1) * P], w2[:, e, f, :],
                                         start=(f == 0), stop=(f == FT - 1))
                    last_.then_inc(f_ps, 1)

            pe.wait_ge(experts_set, 1)
            turn_rows(0, 0, 0)
            f_steps(pe, f_step)


def kernel(**inputs):
    import numpy as _np
    import concourse.bacc as _bacc
    from concourse import mybir as _mybir
    from concourse.bass_utils import run_bass_kernel_spmd as _run

    a = {k.removeprefix("L0_"): _np.asarray(v) for k, v in inputs.items()}

    def rows(x, tiles):
        return x.reshape(tiles, P, *x.shape[1:]).swapaxes(0, 1)

    _, table = constant_columns()
    laid = {
        "consts": table,
        "lens": a["mask_BxS2_if0"],
        "x": a["x"],
        "x_t": rows(a["x"].reshape(T, D).T, DT),
        "ctx": a["ctx_2048"][:, :L, :],
        "w_in": rows(a["attn_W_in"].T, DT),
        "conv_w": rows(a["attn_conv_w"], HT),
        "conv_b": rows(a["attn_conv_b"], HT),
        "log_dt": rows(a["attn_log_dt"], HT),
        "d_skip": rows(a["attn_D"], HT),
        "ssm": _np.stack([rows(a["attn_" + n], HT).reshape(P, HT * MODES)
                          for n in ("log_A_real", "A_imag", "C_re", "C_im")], axis=1),
        "w_out": rows(a["attn_W_out"].T, HT),
        "w_x": rows(a["xattn_W_in"].T, DT),
        "b_x": a["xattn_b_in"].reshape(1, D),
        "one_row": _np.ones((1, T), _np.float32),
        "g_res": rows(a["xattn_g_res"], DT),
        "g_init": a["xattn_g_init"][:D].reshape(1, D),
        "w_r": rows(a["ffn_Wr"].T, DT),
        "b_r": a["ffn_br"].reshape(1, NE),
        "w1": a["ffn_W1"].transpose(0, 2, 1).reshape(NE, DT, P, FF).transpose(2, 0, 1, 3),
        "b1": a["ffn_b1"].reshape(NE, FT, P).transpose(2, 0, 1).reshape(P, NE * FT),
        "w2": a["ffn_W2"].transpose(0, 2, 1).reshape(NE, FT, P, D).transpose(2, 0, 1, 3),
        "b2": a["ffn_b2"].reshape(1, NE * D),
    }
    nc = _bacc.Bacc("TRN2", target_bir_lowering=False, num_devices=1)
    arrays, ins = {}, {}
    for name, x in laid.items():
        x = _np.ascontiguousarray(x)
        arrays[f"in_{name}"] = x
        ins[name] = nc.dram_tensor(f"in_{name}", x.shape, _mybir.dt.from_np(x.dtype), kind="ExternalInput").ap()
    out = nc.dram_tensor("out_0", (T, D), F32, kind="ExternalOutput").ap()
    decoder_layer(nc, ins, out)
    r = _run(nc, [arrays], core_ids=[0])
    return r.results[0]["out_0"].reshape(NB, L, D)
```
